# Optimizing a Trainium2 kernel written in Bass

```python
import numpy as np
import jax
import jax.numpy as jnp

def _softmax(x, axis=-1):
    return jax.nn.softmax(x, axis=axis)

def _gelu(x):
    return jax.nn.gelu(x, approximate=True)

def _silu(x):
    return jax.nn.silu(x)

def _sigmoid(x):
    return jax.nn.sigmoid(x)

def _layernorm(x, axis=-1, eps=1e-05):
    m = jnp.mean(x, axis=axis, keepdims=True)
    v = jnp.var(x, axis=axis, keepdims=True)
    return (x - m) / jnp.sqrt(v + eps)

def _scatter_add(tgt, idx, src, axis=0):
    return tgt.at[idx].add(src)

def _segment_sum(src, seg, n):
    return jax.ops.segment_sum(src, seg, n)
kernel_name = 'mk_gnn_preln_d4_gnn_r32_bbfb9f'

def setup_inputs(seed: int=0):
    np.random.seed(seed)
    _w = jnp.asarray

    def _rec_inputs():
        import jax
        import jax.numpy as jnp
        _gk = jax.random.key(seed)
        x = -0.0001006 + 1 * jax.random.normal(jax.random.fold_in(_gk, 1), (50000, 96), jnp.float32)
        src = jax.random.randint(jax.random.fold_in(_gk, 2), (25000,), 0, 50000, jnp.int32)
        dst = jnp.minimum((50000 * jax.random.uniform(jax.random.fold_in(_gk, 3), (25000,)) ** 2.0).astype(jnp.int32), 49999)
        _o = jnp.argsort(dst, stable=True)
        src = src[_o]
        dst = dst[_o]
        edge_attr_4 = 0.000714719 + 1.00021 * jax.random.normal(jax.random.fold_in(_gk, 11), (25000, 4), jnp.float32)
        return (x, src, dst, edge_attr_4)
    x, src, dst, edge_attr_4 = _rec_inputs()

    def _L0_gnn_setup():
        import jax, jax.numpy as jnp
        import numpy as np
        N = 50000
        E = 25000
        D = 96
        H = 4
        L = 2
        NEG_SLOPE = 0.2
        EPS_BN = 1e-05

        def _gat_layer(x, src, dst, W, a_src, a_dst, b):
            h = (x @ W).reshape(N, H, D)
            alpha_src = jnp.einsum('nhd,hd->nh', h, a_src)
            alpha_dst = jnp.einsum('nhd,hd->nh', h, a_dst)
            e = jax.nn.leaky_relu(alpha_src[src] + alpha_dst[dst], NEG_SLOPE)
            m = jax.ops.segment_max(e, dst, num_segments=N)
            p = jnp.exp(e - m[dst])
            denom = jax.ops.segment_sum(p, dst, num_segments=N)
            alpha = p / (denom[dst] + 1e-16)
            msg = h[src] * alpha[:, :, None]
            out = jax.ops.segment_sum(msg, dst, num_segments=N)
            return out.mean(axis=1) + b
        key = jax.random.key(seed)
        ks = jax.random.split(key, 8)
        x = jax.random.normal(ks[0], (N, D), dtype=jnp.float32)
        edge_index = jax.random.randint(ks[1], (2, E), 0, N, dtype=jnp.int64)
        W = jax.random.normal(ks[2], (L, D, H * D), dtype=jnp.float32) / np.sqrt(D).astype(np.float32)
        att_src = jax.random.normal(ks[3], (L, H, D), dtype=jnp.float32) * 0.1
        att_dst = jax.random.normal(ks[4], (L, H, D), dtype=jnp.float32) * 0.1
        bias = jnp.zeros((L, D), dtype=jnp.float32)
        gamma = jnp.ones((L, D), dtype=jnp.float32)
        beta = jnp.zeros((L, D), dtype=jnp.float32)
        return dict(x=x, edge_index=edge_index, W=W, att_src=att_src, att_dst=att_dst, bias=bias, gamma=gamma, beta=beta)
    _L0_gnn_all = _L0_gnn_setup()
    _L0_gnn_in = {k: v for k, v in _L0_gnn_all.items() if k in ('W', 'att_src', 'att_dst', 'bias', 'gamma', 'beta')}
    del _L0_gnn_all

    def _L1_gnn_setup():
        import jax, jax.numpy as jnp
        import numpy as np
        N, E = (50000, 25000)
        C_IN = 96
        HEADS, C_HEAD = (4, 24)
        NEG_SLOPE = 0.2
        LN_EPS = 1e-05
        key = jax.random.key(seed)
        ks = jax.random.split(key, 6)
        x = jax.random.normal(ks[0], (N, C_IN), dtype=jnp.float32)
        edge_index = jax.random.randint(ks[1], (2, E), 0, N, dtype=jnp.int32)
        W = jax.random.normal(ks[2], (C_IN, HEADS * C_HEAD), dtype=jnp.float32) / np.sqrt(C_IN)
        att_src = jax.random.normal(ks[3], (HEADS, C_HEAD), dtype=jnp.float32) / np.sqrt(C_HEAD)
        att_dst = jax.random.normal(ks[4], (HEADS, C_HEAD), dtype=jnp.float32) / np.sqrt(C_HEAD)
        bias = jnp.zeros((HEADS * C_HEAD,), dtype=jnp.float32)
        gamma = jnp.ones((HEADS * C_HEAD,), dtype=jnp.float32)
        beta = jnp.zeros((HEADS * C_HEAD,), dtype=jnp.float32)
        return {'x': x, 'edge_index': edge_index, 'W': W, 'att_src': att_src, 'att_dst': att_dst, 'bias': bias, 'gamma': gamma, 'beta': beta}
    _L1_gnn_all = _L1_gnn_setup()
    _L1_gnn_in = {k: v for k, v in _L1_gnn_all.items() if k in ('W', 'att_src', 'att_dst', 'bias', 'gamma', 'beta')}
    del _L1_gnn_all

    def _L2_gnn_setup():
        import jax, jax.numpy as jnp
        import numpy as np
        N = 50000
        E = 25000
        D = 96

        def _gcn_conv(x, src, dst, W, b, n_nodes):
            h = x @ W
            loops = jnp.arange(n_nodes, dtype=src.dtype)
            s = jnp.concatenate([src, loops])
            d = jnp.concatenate([dst, loops])
            deg = jax.ops.segment_sum(jnp.ones_like(d, dtype=h.dtype), d, num_segments=n_nodes)
            dinv = jnp.where(deg > 0, jax.lax.rsqrt(deg), 0.0)
            norm = dinv[s] * dinv[d]
            msg = norm[:, None] * h[s]
            out = jax.ops.segment_sum(msg, d, num_segments=n_nodes)
            return out + b
        key = jax.random.key(seed)
        k1, k2, k3, k4 = jax.random.split(key, 4)
        scale = 1.0 / np.sqrt(D)
        return {'x': jax.random.normal(k1, (N, D), dtype=jnp.float32), 'edge_index': jax.random.randint(k2, (2, E), 0, N, dtype=jnp.int64), 'W1': jax.random.normal(k3, (D, D), dtype=jnp.float32) * scale, 'b1': jnp.zeros((D,), dtype=jnp.float32), 'W2': jax.random.normal(k4, (D, D), dtype=jnp.float32) * scale, 'b2': jnp.zeros((D,), dtype=jnp.float32)}
    _L2_gnn_all = _L2_gnn_setup()
    _L2_gnn_in = {k: v for k, v in _L2_gnn_all.items() if k in ('W1', 'b1', 'W2', 'b2')}
    del _L2_gnn_all

    def _L3_gnn_setup():
        import jax, jax.numpy as jnp
        import numpy as np
        EPS = 1e-05

        def _mlp(h, W, b, gamma, beta):
            h = jax.nn.relu(h @ W + b)
            mu = jnp.mean(h, axis=0)
            var = jnp.mean(jnp.square(h - mu), axis=0)
            return gamma * (h - mu) * jax.lax.rsqrt(var + EPS) + beta
        key = jax.random.key(seed)
        ks = jax.random.split(key, 10)
        N, E, C_in, C_out, E_dim = (50000, 25000, 96, 96, 4)
        x = jax.random.normal(ks[0], (N, C_in), dtype=jnp.float32)
        edge_index = jax.random.randint(ks[1], (2, E), 0, N, dtype=jnp.int64)
        edge_attr = jax.random.normal(ks[2], (E, E_dim), dtype=jnp.float32)
        s = lambda fan_in: 1.0 / np.sqrt(fan_in)
        W_node = jax.random.uniform(ks[3], (C_in, C_out), jnp.float32, -s(C_in), s(C_in))
        b_node = jnp.zeros((C_out,), jnp.float32)
        g_node = jnp.ones((C_out,), jnp.float32)
        beta_node = jnp.zeros((C_out,), jnp.float32)
        W_edge = jax.random.uniform(ks[4], (E_dim, C_out), jnp.float32, -s(E_dim), s(E_dim))
        b_edge = jnp.zeros((C_out,), jnp.float32)
        g_edge = jnp.ones((C_out,), jnp.float32)
        beta_edge = jnp.zeros((C_out,), jnp.float32)
        M_in = 2 * C_in + C_out
        W_msg = jax.random.uniform(ks[5], (M_in, C_out), jnp.float32, -s(M_in), s(M_in))
        b_msg = jnp.zeros((C_out,), jnp.float32)
        g_msg = jnp.ones((C_out,), jnp.float32)
        beta_msg = jnp.zeros((C_out,), jnp.float32)
        return dict(x=x, edge_index=edge_index, edge_attr=edge_attr, W_node=W_node, b_node=b_node, g_node=g_node, beta_node=beta_node, W_edge=W_edge, b_edge=b_edge, g_edge=g_edge, beta_edge=beta_edge, W_msg=W_msg, b_msg=b_msg, g_msg=g_msg, beta_msg=beta_msg)
    _L3_gnn_all = _L3_gnn_setup()
    _L3_gnn_in = {k: v for k, v in _L3_gnn_all.items() if k in ('W_node', 'b_node', 'g_node', 'beta_node', 'W_edge', 'b_edge', 'g_edge', 'beta_edge', 'W_msg', 'b_msg', 'g_msg', 'beta_msg')}
    del _L3_gnn_all
    return {'x': x, 'src': src, 'dst': dst, 'edge_attr_4': edge_attr_4, 'L0_gnn_W': _L0_gnn_in['W'], 'L0_gnn_att_src': _L0_gnn_in['att_src'], 'L0_gnn_att_dst': _L0_gnn_in['att_dst'], 'L0_gnn_bias': _L0_gnn_in['bias'], 'L0_gnn_gamma': _L0_gnn_in['gamma'], 'L0_gnn_beta': _L0_gnn_in['beta'], 'L1_gnn_W': _L1_gnn_in['W'], 'L1_gnn_att_src': _L1_gnn_in['att_src'], 'L1_gnn_att_dst': _L1_gnn_in['att_dst'], 'L1_gnn_bias': _L1_gnn_in['bias'], 'L1_gnn_gamma': _L1_gnn_in['gamma'], 'L1_gnn_beta': _L1_gnn_in['beta'], 'L2_gnn_W1': _L2_gnn_in['W1'], 'L2_gnn_b1': _L2_gnn_in['b1'], 'L2_gnn_W2': _L2_gnn_in['W2'], 'L2_gnn_b2': _L2_gnn_in['b2'], 'L3_gnn_W_node': _L3_gnn_in['W_node'], 'L3_gnn_b_node': _L3_gnn_in['b_node'], 'L3_gnn_g_node': _L3_gnn_in['g_node'], 'L3_gnn_beta_node': _L3_gnn_in['beta_node'], 'L3_gnn_W_edge': _L3_gnn_in['W_edge'], 'L3_gnn_b_edge': _L3_gnn_in['b_edge'], 'L3_gnn_g_edge': _L3_gnn_in['g_edge'], 'L3_gnn_beta_edge': _L3_gnn_in['beta_edge'], 'L3_gnn_W_msg': _L3_gnn_in['W_msg'], 'L3_gnn_b_msg': _L3_gnn_in['b_msg'], 'L3_gnn_g_msg': _L3_gnn_in['g_msg'], 'L3_gnn_beta_msg': _L3_gnn_in['beta_msg']}

def reference(x, src, dst, edge_attr_4, L0_gnn_W, L0_gnn_att_src, L0_gnn_att_dst, L0_gnn_bias, L0_gnn_gamma, L0_gnn_beta, L1_gnn_W, L1_gnn_att_src, L1_gnn_att_dst, L1_gnn_bias, L1_gnn_gamma, L1_gnn_beta, L2_gnn_W1, L2_gnn_b1, L2_gnn_W2, L2_gnn_b2, L3_gnn_W_node, L3_gnn_b_node, L3_gnn_g_node, L3_gnn_beta_node, L3_gnn_W_edge, L3_gnn_b_edge, L3_gnn_g_edge, L3_gnn_beta_edge, L3_gnn_W_msg, L3_gnn_b_msg, L3_gnn_g_msg, L3_gnn_beta_msg):
    import jax
    import jax.numpy as jnp

    def _L0_gnn_ref(x, edge_index, W, att_src, att_dst, bias, gamma, beta):
        import jax, jax.numpy as jnp
        import numpy as np
        N = 50000
        E = 25000
        D = 96
        H = 4
        L = 2
        NEG_SLOPE = 0.2
        EPS_BN = 1e-05

        def _gat_layer(x, src, dst, W, a_src, a_dst, b):
            h = (x @ W).reshape(N, H, D)
            alpha_src = jnp.einsum('nhd,hd->nh', h, a_src)
            alpha_dst = jnp.einsum('nhd,hd->nh', h, a_dst)
            e = jax.nn.leaky_relu(alpha_src[src] + alpha_dst[dst], NEG_SLOPE)
            m = jax.ops.segment_max(e, dst, num_segments=N)
            p = jnp.exp(e - m[dst])
            denom = jax.ops.segment_sum(p, dst, num_segments=N)
            alpha = p / (denom[dst] + 1e-16)
            msg = h[src] * alpha[:, :, None]
            out = jax.ops.segment_sum(msg, dst, num_segments=N)
            return out.mean(axis=1) + b
        loops = jnp.arange(N, dtype=edge_index.dtype)
        ei = jnp.concatenate([edge_index, jnp.stack([loops, loops])], axis=1)
        src, dst = (ei[0], ei[1])
        for l in range(L):
            x_res = x
            out = _gat_layer(x, src, dst, W[l], att_src[l], att_dst[l], bias[l])
            mu = out.mean(axis=0)
            var = out.var(axis=0)
            out = (out - mu) / jnp.sqrt(var + EPS_BN) * gamma[l] + beta[l]
            x = jax.nn.relu(out) + x_res
        return x

    def _L1_gnn_ref(x, edge_index, W, att_src, att_dst, bias, gamma, beta):
        import jax, jax.numpy as jnp
        import numpy as np
        N, E = (50000, 25000)
        C_IN = 96
        HEADS, C_HEAD = (4, 24)
        NEG_SLOPE = 0.2
        LN_EPS = 1e-05
        n = x.shape[0]
        loop = jnp.arange(n, dtype=edge_index.dtype)
        src = jnp.concatenate([edge_index[0], loop])
        dst = jnp.concatenate([edge_index[1], loop])
        h = (x @ W).reshape(n, HEADS, C_HEAD)
        a_src = jnp.einsum('nhc,hc->nh', h, att_src)
        a_dst = jnp.einsum('nhc,hc->nh', h, att_dst)
        e = a_src[src] + a_dst[dst]
        e = jnp.where(e > 0, e, NEG_SLOPE * e)
        m = jax.ops.segment_max(e, dst, num_segments=n)
        ex = jnp.exp(e - m[dst])
        s = jax.ops.segment_sum(ex, dst, num_segments=n)
        alpha = ex / (s[dst] + 1e-16)
        msg = h[src] * alpha[:, :, None]
        out = jax.ops.segment_sum(msg, dst, num_segments=n).reshape(n, HEADS * C_HEAD)
        out = out + bias
        out = out + x
        mu = out.mean(-1, keepdims=True)
        var = ((out - mu) ** 2).mean(-1, keepdims=True)
        out = (out - mu) * jax.lax.rsqrt(var + LN_EPS) * gamma + beta
        return jax.nn.relu(out)

    def _L2_gnn_ref(x, edge_index, W1, b1, W2, b2):
        import jax, jax.numpy as jnp
        import numpy as np
        N = 50000
        E = 25000
        D = 96

        def _gcn_conv(x, src, dst, W, b, n_nodes):
            h = x @ W
            loops = jnp.arange(n_nodes, dtype=src.dtype)
            s = jnp.concatenate([src, loops])
            d = jnp.concatenate([dst, loops])
            deg = jax.ops.segment_sum(jnp.ones_like(d, dtype=h.dtype), d, num_segments=n_nodes)
            dinv = jnp.where(deg > 0, jax.lax.rsqrt(deg), 0.0)
            norm = dinv[s] * dinv[d]
            msg = norm[:, None] * h[s]
            out = jax.ops.segment_sum(msg, d, num_segments=n_nodes)
            return out + b
        src, dst = (edge_index[0], edge_index[1])
        h = _gcn_conv(x, src, dst, W1, b1, N)
        h = jax.nn.relu(h)
        h = _gcn_conv(h, src, dst, W2, b2, N)
        h = jax.nn.relu(h)
        return h

    def _L3_gnn_ref(x, edge_index, edge_attr, W_node, b_node, g_node, beta_node, W_edge, b_edge, g_edge, beta_edge, W_msg, b_msg, g_msg, beta_msg):
        import jax, jax.numpy as jnp
        import numpy as np
        EPS = 1e-05

        def _mlp(h, W, b, gamma, beta):
            h = jax.nn.relu(h @ W + b)
            mu = jnp.mean(h, axis=0)
            var = jnp.mean(jnp.square(h - mu), axis=0)
            return gamma * (h - mu) * jax.lax.rsqrt(var + EPS) + beta
        node_feat = _mlp(x, W_node, b_node, g_node, beta_node)
        edge_feat = _mlp(edge_attr, W_edge, b_edge, g_edge, beta_edge)
        row, col = (edge_index[0], edge_index[1])
        message = jnp.concatenate([x[row], x[col], edge_feat], axis=1)
        message = _mlp(message, W_msg, b_msg, g_msg, beta_msg)
        agg = jax.ops.segment_sum(message, col, num_segments=node_feat.shape[0])
        return agg + node_feat
    edge_index = jnp.stack([src, dst])
    h = jnp.maximum(_layernorm(x, axis=-1), 0.0)
    x = x + _L0_gnn_ref(h, edge_index, L0_gnn_W, L0_gnn_att_src, L0_gnn_att_dst, L0_gnn_bias, L0_gnn_gamma, L0_gnn_beta)
    h = jnp.maximum(_layernorm(x, axis=-1), 0.0)
    x = x + _L1_gnn_ref(h, edge_index, L1_gnn_W, L1_gnn_att_src, L1_gnn_att_dst, L1_gnn_bias, L1_gnn_gamma, L1_gnn_beta)
    h = jnp.maximum(_layernorm(x, axis=-1), 0.0)
    x = x + _L2_gnn_ref(h, edge_index, L2_gnn_W1, L2_gnn_b1, L2_gnn_W2, L2_gnn_b2)
    h = jnp.maximum(_layernorm(x, axis=-1), 0.0)
    x = x + _L3_gnn_ref(h, edge_index, edge_attr_4, L3_gnn_W_node, L3_gnn_b_node, L3_gnn_g_node, L3_gnn_beta_node, L3_gnn_W_edge, L3_gnn_b_edge, L3_gnn_g_edge, L3_gnn_beta_edge, L3_gnn_W_msg, L3_gnn_b_msg, L3_gnn_g_msg, L3_gnn_beta_msg)
    return x

_drawn_inputs = setup_inputs


def setup_inputs(seed=0):
    import zlib

    import numpy as np

    out = dict(_drawn_inputs(seed))
    spreads = {'L0_gnn_bias': (0.0, 2.0),
     'L0_gnn_gamma': (1.0, 0.2),
     'L0_gnn_beta': (0.0, 0.1),
     'L1_gnn_bias': (0.0, 0.289),
     'L1_gnn_gamma': (1.0, 0.2),
     'L1_gnn_beta': (0.0, 0.296),
     'L2_gnn_b1': (0.0, 0.422),
     'L2_gnn_b2': (0.0, 0.358),
     'L3_gnn_b_node': (0.0, 0.1),
     'L3_gnn_g_node': (1.0, 0.2),
     'L3_gnn_beta_node': (0.0, 0.1),
     'L3_gnn_b_edge': (0.0, 0.323),
     'L3_gnn_g_edge': (1.0, 0.2),
     'L3_gnn_beta_edge': (0.0, 0.8),
     'L3_gnn_b_msg': (0.0, 0.274),
     'L3_gnn_g_msg': (1.0, 0.2),
     'L3_gnn_beta_msg': (0.0, 0.1)}
    factors = {'L1_gnn_att_src': 2.934, 'L1_gnn_att_dst': 18.567}
    for name, (base, spread) in spreads.items():
        noise = np.random.default_rng([zlib.crc32(name.encode()), seed]).standard_normal(out[name].shape)
        drawn = base * np.exp(spread * noise) if base else spread * noise
        out[name] = jnp.asarray(drawn.astype(out[name].dtype))
    for name, factor in factors.items():
        out[name] = (out[name] * factor).astype(out[name].dtype)
    return out
```

```python
from contextlib import ExitStack

import concourse.bass as bass
from concourse import mybir

F32 = mybir.dt.float32
I32 = mybir.dt.int32
ALU = mybir.AluOpType
ACT = mybir.ActivationFunctionType
AX = mybir.AxisListType

N = 50000
E = 25000
D = 96
H = 4
DH = D // H
P = 125
NT = N // P
ET = E // P
K = 8
HALF = K // 2
NSTEP = NT // K
ESTEP = ET // K
ROW = D + 2 * H
AGG = D + 1
SPARE = 2 * K * P
BIG = 1.0e30
EPS = 1e-5
SLOPE = 0.2
DEBUG = None


def build(nc, A, out):
    whole = ExitStack()
    signals = {}

    class Signal:

        def __init__(self, name):
            self.sem = whole.enter_context(nc.semaphore(name))
            self.base = 0

        def at(self, count):
            return self.base + count

    def signal(name):
        if name not in signals:
            signals[name] = Signal(name)
        return signals[name]

    class Chain:

        def __init__(self, eng, sig, per, step=0):
            self.eng, self.sig, self.per, self.step, self.k = eng, sig, per, step, 0

        def link(self, ins):
            self.k += 1
            ins.then_inc(self.sig.sem, 1)
            self.eng.wait_ge(self.sig.sem, self.sig.at(self.per * self.step + self.k))

        def done(self):
            assert self.k == self.per, (self.k, self.per)

    def steps(eng, n, body):
        peel = 4 - n % 2
        for s in range(peel):
            body(s, s % 2, s // 2, s if s < 2 else None)
        with eng.Fori(0, (n - peel) // 2) as i:
            body(2 * i + peel, peel % 2, i + peel // 2, None)
            body(2 * i + peel + 1, (peel + 1) % 2, i + (peel + 1) // 2, None)

    def dram(name, shape):
        return nc.dram_tensor(name, shape, F32, kind="Internal").ap()

    t_h0 = dram("t_h0", [N, ROW])
    t_x1 = dram("t_x1", [N, ROW])
    t_g = dram("t_g", [N, ROW])
    d_y = dram("d_y", [N, D])
    d_xa = dram("d_xa", [N, D])
    d_xb = dram("d_xb", [N, D])
    d_xc = dram("d_xc", [N, D])
    d_r = dram("d_r", [N, D])
    t_c1 = dram("t_c1", [N, D])
    t_c2 = dram("t_c2", [N, D])
    t_u = dram("t_u", [N, D])
    t_v = dram("t_v", [N, D])
    d_nf = dram("d_nf", [N, D])
    t_agg = dram("t_agg", [N + SPARE, AGG])

    def rows(table, step, w=None):
        v = table[0:N, :].rearrange("(p t) d -> p t d", t=NT)[:, bass.ds(step * K, K), :]
        return v if w is None else v[:, :, 0:w]

    def rows_all(table):
        return table[0:N, 0:D]

    def row1(v):
        return v.rearrange("(a d) -> a d", a=1)

    def sbw(name, shape, dt=F32):
        return whole.enter_context(nc.sbuf_tensor(name, shape, dt))

    ident = sbw("ident", [128, 128])
    ones = sbw("ones", [128, 128])
    ones_row = sbw("ones_row", [1, P])
    src_idx = sbw("src_idx", [P, ET], I32)
    dst_idx = sbw("dst_idx", [P, ET], I32)
    out_idx = sbw("out_idx", [P, ET], I32)
    fix_idx = sbw("fix_idx", [P, 1], I32)
    same_f = sbw("same_f", [P, ET])
    same_b = sbw("same_b", [P, ET])
    pen_f = sbw("pen_f", [P, ET])
    pen_b = sbw("pen_b", [P, ET])
    mask_f = sbw("mask_f", [P, P])
    mask_b = sbw("mask_b", [P, P])
    far_f = sbw("far_f", [P, P])
    far_b = sbw("far_b", [P, P])
    count = sbw("count", [P, NT])
    dinv = sbw("dinv", [P, NT])
    bn_s = sbw("bn_s", [P, D])
    bn_t = sbw("bn_t", [P, D])
    bm_s = sbw("bm_s", [P, D])
    bm_t = sbw("bm_t", [P, D])
    eps_col = sbw("eps_col", [P, 1])

    def prepare():
        with ExitStack() as ctx:
            def sb(name, shape, dt=F32):
                return ctx.enter_context(nc.sbuf_tensor(name, shape, dt))

            dst_f = sb("dst_f", [P, ET])
            next_i = sb("next_i", [P, 1], I32)
            next_f = sb("next_f", [P, 1])
            last = sb("last", [P, ET])
            spare_i = sb("spare_i", [P, (ET + 15) // 16, 2 * K], I32)
            spare = sb("spare", [P, ET])
            diff = sb("diff", [P, ET])
            fixf = sb("fixf", [P, 2])
            tri_f = sb("tri_f", [P, P])
            tri_b = sb("tri_b", [P, P])
            rep = sb("rep", [P, 2, P])
            zero = sb("zero", [P, 2, 26 * AGG])
            turned = ctx.enter_context(nc.psum_tensor("turned", [P, 2, P], F32))
            s_ld, s_pool, s_nx = signal("load_a"), signal("pool_chain"), signal("load_b")
            s_dve, s_pe, s_zero, s_z = signal("dve_chain"), signal("pe_done"), signal("zeroed"), signal("store_a")
            agg_v = t_agg.rearrange("(p t) d -> p (t d)", t=(N + SPARE) // P)
            block = ctx.enter_context(nc.Block())

            @block.sync
            def _(sp):
                sp.dma_start(src_idx[:, :], A["src"].rearrange("(p t) -> p t", t=ET)).then_inc(s_ld.sem, 16)
                sp.dma_start(dst_idx[:, :], A["dst"].rearrange("(p t) -> p t", t=ET)).then_inc(s_ld.sem, 16)
                sp.wait_ge(s_pool.sem, s_pool.at(1))
                sp.dma_start(next_i[0:P - 1, :],
                             A["dst"].rearrange("(p t) -> p t", t=ET)[1:P, 0:1], allow_slow_non_contiguous=True).then_inc(s_nx.sem, 16)
                sp.wait_ge(s_zero.sem, s_zero.at(1))
                for c in range(8):
                    w = 52 * AGG
                    sp.dma_start(agg_v[:, c * w:(c + 1) * w].rearrange("p (a w) -> p a w", a=2),
                                 zero[:, :, :]).then_inc(s_z.sem, 16)
                sp.wait_ge(s_z.sem, s_z.at(128))

            @block.gpsimd
            def _(pool):
                chain = Chain(pool, s_pool, 7)
                chain.link(pool.memset(next_i[:, :], -1))
                chain.link(pool.memset(ident[:, :], 0.0))
                chain.link(pool.affine_select(out=ident[:, :], in_=ident[:, :], compare_op=ALU.not_equal, fill=1.0,
                                              base=0, pattern=[[-1, 128]], channel_multiplier=1))
                chain.link(pool.memset(ones[:, :], 1.0))
                chain.link(pool.affine_select(out=tri_f[:, :], in_=ones[0:P, 0:P], compare_op=ALU.is_gt, fill=0.0,
                                              base=0, pattern=[[1, P]], channel_multiplier=-1))
                chain.link(pool.affine_select(out=tri_b[:, :], in_=ones[0:P, 0:P], compare_op=ALU.is_gt, fill=0.0,
                                              base=0, pattern=[[-1, P]], channel_multiplier=1))
                chain.link(pool.iota(spare_i[:, :, :], pattern=[[0, (ET + 15) // 16], [P, 2 * K]], base=N,
                                     channel_multiplier=1))
                chain.done()

            @block.vector
            def _(dve):
                chain = Chain(dve, s_dve, 18)
                dve.memset(zero[:, :, :], 0.0).then_inc(s_zero.sem, 1)
                dve.memset(eps_col[:, :], EPS)
                dve.memset(ones_row[:, :], 1.0)
                dve.memset(same_f[:, 0:1], 1.0)
                dve.wait_ge(s_ld.sem, s_ld.at(32))
                chain.link(dve.tensor_copy(dst_f[:, :], dst_idx[:, :]))
                dve.wait_ge(s_nx.sem, s_nx.at(16))
                chain.link(dve.tensor_copy(next_f[:, :], next_i[:, :]))
                chain.link(dve.tensor_tensor(same_f[:, 1:ET], dst_f[:, 1:ET], dst_f[:, 0:ET - 1], ALU.is_equal))
                chain.link(dve.memset(same_b[:, ET - 1:ET], 1.0))
                chain.link(dve.tensor_copy(same_b[:, 0:ET - 1], same_f[:, 1:ET]))
                dve.tensor_scalar(pen_f[:, :], same_f[:, :], BIG, -BIG, ALU.mult, ALU.add)
                dve.tensor_scalar(pen_b[:, :], same_b[:, :], BIG, -BIG, ALU.mult, ALU.add)
                dve.tensor_scalar(last[:, 0:ET - 1], same_b[:, 0:ET - 1], -1.0, 1.0, ALU.mult, ALU.add)
                chain.link(dve.tensor_tensor(last[:, ET - 1:ET], dst_f[:, ET - 1:ET], next_f[:, :], ALU.not_equal))
                dve.wait_ge(s_pool.sem, s_pool.at(7))
                chain.link(dve.tensor_copy(spare[:, :],
                                           spare_i[:, :, :].rearrange("p a b -> p (a b)")[:, 0:ET]))
                chain.link(dve.tensor_tensor(diff[:, :], dst_f[:, :], spare[:, :], ALU.subtract))
                dve.tensor_tensor(fixf[:, 0:1], dst_f[:, 0:1], next_f[:, :], ALU.not_equal)
                chain.link(dve.tensor_tensor(last[:, :], last[:, :], diff[:, :], ALU.mult))
                chain.link(dve.tensor_tensor(out_idx[:, :], last[:, :], spare[:, :], ALU.add))
                chain.link(dve.tensor_tensor(fixf[:, 1:2], fixf[:, 0:1], diff[:, 0:1], ALU.mult))
                chain.link(dve.tensor_tensor(fix_idx[:, :], fixf[:, 1:2], spare[:, 0:1], ALU.add))
                chain.link(dve.tensor_scalar(rep[:, 0, :], ones[0:P, 0:P], dst_f[:, 0:1], None, ALU.mult))
                chain.link(dve.tensor_scalar(rep[:, 1, :], ones[0:P, 0:P], dst_f[:, ET - 1:ET], None, ALU.mult))
                dve.wait_ge(s_pe.sem, s_pe.at(1))
                chain.link(dve.scalar_tensor_tensor(mask_f[:, :], turned[:, 0, :], dst_f[:, ET - 1:ET], tri_f[:, :],
                                                    ALU.is_equal, ALU.mult))
                chain.link(dve.scalar_tensor_tensor(mask_b[:, :], turned[:, 1, :], dst_f[:, 0:1], tri_b[:, :],
                                                    ALU.is_equal, ALU.mult))
                chain.link(dve.tensor_scalar(far_f[:, :], mask_b[:, :], BIG, -BIG, ALU.mult, ALU.add))
                chain.link(dve.tensor_scalar(far_b[:, :], mask_f[:, :], BIG, -BIG, ALU.mult, ALU.add))
                chain.done()

            @block.tensor
            def _(pe):
                pe.wait_ge(s_dve.sem, s_dve.at(14))
                pe.wait_ge(s_pool.sem, s_pool.at(3))
                pe.transpose(turned[:, 0, :], rep[:, 0, :], ident[0:P, 0:P])
                pe.transpose(turned[:, 1, :], rep[:, 1, :], ident[0:P, 0:P]).then_inc(s_pe.sem, 1)

        s_ld.base += 32
        s_pool.base += 7
        s_nx.base += 16
        s_dve.base += 18
        s_pe.base += 1
        s_zero.base += 1
        s_z.base += 128

    def norm_stats(dve, link, x, bn, tmp, s_var):
        for k in range(K):
            ins = dve.bn_stats(bn[:, k, :], x[:, k, :])
        link(ins)
        dve.tensor_tensor(tmp[:, 0, :], bn[:, :, 1], bn[:, :, 4], ALU.add)
        dve.tensor_tensor(tmp[:, 2, :], bn[:, :, 2], bn[:, :, 5], ALU.add)
        link(dve.tensor_tensor(tmp[:, 1, :], bn[:, :, 1], bn[:, :, 4], ALU.subtract))
        link(dve.tensor_tensor(tmp[:, 1, :], tmp[:, 1, :], tmp[:, 1, :], ALU.mult))
        dve.scalar_tensor_tensor(tmp[:, 3, :], tmp[:, 1, :], D / 4.0, tmp[:, 2, :],
                                 ALU.mult, ALU.add).then_inc(s_var.sem, 1)

    def norm_scale(dve, link, tmp):
        link(dve.reciprocal(tmp[:, 5, :], tmp[:, 4, :]))
        return dve.scalar_tensor_tensor(tmp[:, 6, :], tmp[:, 0, :], -0.5, tmp[:, 5, :], ALU.mult, ALU.mult)

    def bn_coefficients(name, sums, squares, groups, n, gamma, beta, scale, shift):
        with ExitStack() as ctx:
            row = ctx.enter_context(nc.sbuf_tensor(f"{name}_row", [1, 8, D], F32))
            coef = ctx.enter_context(nc.sbuf_tensor(f"{name}_coef", [1, 2, D], F32))
            wide = ctx.enter_context(nc.psum_tensor(f"{name}_wide", [P, 2, D], F32))
            s_ld, s_dve = signal("load_a0"), signal("dve_chain")
            s_var, s_dev, s_pe = signal("var_ready"), signal("dev_ready"), signal("pe_done")
            block = ctx.enter_context(nc.Block())

            @block.sync
            def _(sp):
                sp.dma_start(row[:, 0, :], row1(gamma)).then_inc(s_ld.sem, 16)
                sp.dma_start(row[:, 1, :], row1(beta)).then_inc(s_ld.sem, 16)

            @block.vector
            def _(dve):
                chain = Chain(dve, s_dve, 9)
                dve.tensor_reduce(row[:, 2, :], sums.rearrange("p (g c) -> p c g", g=groups), AX.X, ALU.add)
                chain.link(dve.tensor_reduce(row[:, 3, :], squares.rearrange("p (g c) -> p c g", g=groups), AX.X,
                                             ALU.add))
                chain.link(dve.tensor_scalar(row[:, 2:4, :], row[:, 2:4, :], 1.0 / n, None, ALU.mult))
                chain.link(dve.tensor_tensor(row[:, 4, :], row[:, 2, :], row[:, 2, :], ALU.mult))
                dve.tensor_tensor(row[:, 5, :], row[:, 3, :], row[:, 4, :], ALU.subtract).then_inc(s_var.sem, 1)
                dve.wait_ge(s_dev.sem, s_dev.at(1))
                chain.link(dve.reciprocal(row[:, 6, :], row[:, 5, :]))
                dve.wait_ge(s_ld.sem, s_ld.at(32))
                chain.link(dve.tensor_tensor(coef[:, 0, :], row[:, 6, :], row[:, 0, :], ALU.mult))
                chain.link(dve.tensor_tensor(row[:, 7, :], row[:, 2, :], coef[:, 0, :], ALU.mult))
                chain.link(dve.tensor_tensor(coef[:, 1, :], row[:, 1, :], row[:, 7, :], ALU.subtract))
                dve.wait_ge(s_pe.sem, s_pe.at(1))
                chain.link(dve.tensor_copy(scale[:, :], wide[:, 0, :]))
                chain.link(dve.tensor_copy(shift[:, :], wide[:, 1, :]))
                chain.done()

            @block.scalar
            def _(act):
                act.wait_ge(s_var.sem, s_var.at(1))
                nc.scalar.activation(row[:, 5, :], row[:, 5, :], ACT.Sqrt, bias=eps_col[0:1, :]).then_inc(s_dev.sem, 1)

            @block.tensor
            def _(pe):
                pe.wait_ge(s_dve.sem, s_dve.at(7))
                pe.matmul(wide[:, :, :], ones_row[:, :], coef[:, :, :], start=True, stop=True).then_inc(s_pe.sem, 1)

        s_ld.base += 32
        s_dve.base += 9
        s_var.base += 1
        s_dev.base += 1
        s_pe.base += 1

    def gat_weights(name, wide, W, a_src, a_dst, heads, at_a, at_mean):
        width = W.shape[1]
        dh = width // heads
        with ExitStack() as ctx:
            w = ctx.enter_context(nc.sbuf_tensor(f"{name}_w", [D, heads, dh], F32))
            a = ctx.enter_context(nc.sbuf_tensor(f"{name}_a", [D, 2, heads, dh], F32))
            part = ctx.enter_context(nc.sbuf_tensor(f"{name}_part", [D, heads, dh], F32))
            s_ld, s_dve = signal("load_a0"), signal("dve_chain")
            block = ctx.enter_context(nc.Block())
            n_link = 4 + (2 if at_mean is not None else 0)

            @block.sync
            def _(sp):
                sp.dma_start(w[:, :, :], W.rearrange("c (h d) -> c h d", h=heads)).then_inc(s_ld.sem, 16)
                sp.dma_start(a[:, 0, :, :], a_src.partition_broadcast(D)).then_inc(s_ld.sem, 16)
                sp.dma_start(a[:, 1, :, :], a_dst.partition_broadcast(D)).then_inc(s_ld.sem, 16)

            @block.vector
            def _(dve):
                chain = Chain(dve, s_dve, n_link)
                dve.wait_ge(s_ld.sem, s_ld.at(48))
                for j in range(2):
                    chain.link(dve.tensor_tensor(part[:, :, :], w[:, :, :], a[:, j, :, :], ALU.mult))
                    chain.link(dve.tensor_reduce(wide[0:D, at_a + j * H:at_a + j * H + H], part[:, :, :], AX.X,
                                                 ALU.add))
                if at_mean is not None:
                    chain.link(dve.tensor_reduce(part[:, 0, :], w[:, :, :].rearrange("c h d -> c d h"), AX.X,
                                                 ALU.add))
                    chain.link(dve.tensor_scalar(wide[0:D, at_mean:at_mean + D], part[:, 0, :], 1.0 / heads, None,
                                                 ALU.mult))
                chain.done()

        s_ld.base += 48
        s_dve.base += n_link

    def node_phase(name, kind, loads, stores, width, weights, gat=None, held=None, bias=None, gamma=None,
                   beta=None, sums=None):
        norms = {"first": 1, "gat": 0, "join": 1, "layer": 2, "gcn": 0, "last": 1}[kind]
        links = {"first": 4, "gat": 2, "join": 7, "layer": 11, "gcn": 2, "last": 7}[kind]
        act_reads = kind in ("first", "gat", "join", "last")
        rounds = 2 if width > 256 else 1
        own_rows = kind in ("first", "gat")
        row_w = ROW if own_rows else D
        with ExitStack() as ctx:
            def sb(nm, shape, dt=F32):
                return ctx.enter_context(nc.sbuf_tensor(f"{name}_{nm}", shape, dt))

            ins = [sb(f"in{j}", [P, 2, K, w]) for j, (_, w) in enumerate(loads)]
            h = sb("h", [P, 2, K, row_w])
            outs = [h if own_rows and j == 0 else sb(f"out{j}", [P, 2, K, w]) for j, (_, w) in enumerate(stores)]
            hT = sb("hT", [D + 1, 2, HALF * P])
            wide = sb("wide", [D + 1, width])
            bn = sb("bn", [P, 2, K, 6])
            tmp = sb("tmp", [P, 2, 2, 7, K])
            if gamma is not None:
                gam, bet = sb("gam", [P, D]), sb("bet", [P, D])
            if bias is not None:
                bia = sb("bia", [P, D])
            if kind in ("layer", "gcn", "last"):
                mid = sb("mid", [P, K, D])
            if kind == "last":
                squares = sb("squares", [P, K, D])
                zeros = sb("zeros", [P, HALF * D])
            pT = ctx.enter_context(nc.psum_tensor(f"{name}_pT", [D, 2, 512], F32))
            pO = ctx.enter_context(nc.psum_tensor(f"{name}_pO", [P, 4, 512], F32))

            s_in = [[signal(f"load_{c}{b}") for b in range(2)] for c in "abc"[:len(loads)]]
            s_out = [[signal(f"store_{c}{b}") for b in range(2)] for c in "abcd"[:len(stores)]]
            s_w, s_set, s_used = signal("weights"), signal("setup"), signal("inputs_used")
            s_var, s_dev, s_scale = signal("var_ready"), signal("dev_ready"), signal("scale_ready")
            s_norm, s_h, s_tr = signal("normed"), signal("h_ready"), signal("turned")
            s_hT, s_mm, s_ev = signal("hT_ready"), signal("product_ready"), signal("product_used")
            s_ev2, s_dve, s_sq, s_st = signal("product_used2"), signal("dve_chain"), signal("squared"), signal("summed")

            n_w = sum((m is not None) + (v is not None) for _, m, v in weights) \
                + 2 * (gamma is not None) + (bias is not None)
            with nc.Block() as setup:
                @setup.sync
                def _(sp):
                    sp.wait_ge(s_set.sem, s_set.at(1))
                    for at, m, v in weights:
                        if m is not None:
                            sp.dma_start(wide[0:D, at:at + D], m).then_inc(s_w.sem, 16)
                        if v is not None:
                            sp.dma_start(wide[D:D + 1, at:at + D], row1(v)).then_inc(s_w.sem, 16)
                    if gamma is not None:
                        sp.dma_start(gam[:, :], gamma.partition_broadcast(P)).then_inc(s_w.sem, 16)
                        sp.dma_start(bet[:, :], beta.partition_broadcast(P)).then_inc(s_w.sem, 16)
                    if bias is not None:
                        sp.dma_start(bia[:, :], bias.partition_broadcast(P)).then_inc(s_w.sem, 16)
                    sp.wait_ge(s_w.sem, s_w.at(16 * n_w))

                @setup.vector
                def _(dve):
                    dve.memset(hT[:, :, :], 1.0)
                    if kind == "last":
                        dve.memset(zeros[:, :], 0.0)
                    dve.memset(wide[:, :], 0.0).then_inc(s_set.sem, 1)
            s_set.base += 1
            s_w.base += 16 * n_w
            if gat is not None:
                gat_weights(name, wide, *gat)

            used = s_h if own_rows else s_used
            x_in = [t[:, :, :, 0:D] for t in ins]
            block = ctx.enter_context(nc.Block())

            @block.sync
            def _(sp):
                def load(s, b, q, first):
                    if first is None:
                        sp.wait_ge(used.sem, used.at(s - 1))
                        sp.nop(nofuse=True)
                    for (table, w), buf, sg in zip(loads, ins, s_in):
                        sp.dma_start(buf[:, b, :, :], rows(table, s, w)).then_inc(sg[b].sem, 16)

                def store(s, b, q):
                    sp.wait_ge(s_ev.sem, s_ev.at(rounds * (s + 1)))
                    sp.nop(nofuse=True)
                    if act_reads:
                        sp.wait_ge(s_ev2.sem, s_ev2.at(rounds * (s + 1)))
                        sp.nop(nofuse=True)
                    for (table, w), buf, sg in zip(stores, outs, s_out):
                        sp.dma_start(rows(table, s), buf[:, b, :, :]).then_inc(sg[b].sem, 16)

                def body(s, b, q, first):
                    load(s, b, q, first)
                    if first != 0:
                        store(s - 1, 1 - b, None)

                steps(sp, NSTEP, body)
                store(NSTEP - 1, (NSTEP - 1) % 2, None)
                for sg in s_out:
                    for b in range(2):
                        sp.wait_ge(sg[b].sem, sg[b].at(16 * (NSTEP // 2)))

            def chained(dve, s):
                return Chain(dve, s_dve, links, s)

            @block.vector
            def _(dve):
                def arrived(b, q):
                    for sg in s_in:
                        dve.wait_ge(sg[b].sem, sg[b].at(16 * (q + 1)))

                def out_free(j, b, q, first):
                    if first is None or first >= 2:
                        dve.wait_ge(s_out[j][b].sem, s_out[j][b].at(16 * q))

                def stats(link, x, s, b, j):
                    norm_stats(dve, link, x, bn[:, b], tmp[:, b, j], s_var)

                def scale(link, s, b, j):
                    dve.wait_ge(s_dev.sem, s_dev.at(norms * s + j + 1))
                    norm_scale(dve, link, tmp[:, b, j]).then_inc(s_scale.sem, 1)

                def head(s, b, q, first):
                    c = chained(dve, s)
                    arrived(b, q)
                    wide_s = bn_s[:, :].unsqueeze(1).broadcast_to([P, K, D])
                    wide_t = bn_t[:, :].unsqueeze(1).broadcast_to([P, K, D])
                    if kind == "first":
                        stats(c.link, x_in[0][:, b], s, b, 0)
                    if kind in ("gat", "join"):
                        o = held[:, bass.ds(s * K, K), :]
                        c.link(dve.tensor_tensor(o, o, wide_s, ALU.mult))
                        c.link(dve.tensor_tensor(o, o, wide_t, ALU.add))
                        if kind == "gat":
                            out_free(0, b, q, first)
                            dve.scalar_tensor_tensor(h[:, b, :, 0:D], o, 0.0, x_in[0][:, b], ALU.max,
                                                     ALU.add).then_inc(s_h.sem, 1)
                        else:
                            c.link(dve.scalar_tensor_tensor(o, o, 0.0, x_in[0][:, b], ALU.max, ALU.add))
                            out_free(0, b, q, first)
                            dve.tensor_tensor(outs[0][:, b], o, x_in[1][:, b], ALU.add).then_inc(s_used.sem, 1)
                            dve.wait_ge(s_used.sem, s_used.at(s + 1))
                            stats(c.link, outs[0][:, b], s, b, 0)
                    if kind == "layer":
                        c.link(dve.tensor_tensor(mid[:, :, :], x_in[0][:, b], x_in[1][:, b], ALU.add))
                        stats(c.link, mid[:, :, :], s, b, 0)
                        scale(c.link, s, b, 0)
                        dve.wait_ge(s_norm.sem, s_norm.at(s + 1))
                        c.link(dve.tensor_tensor(mid[:, :, :], mid[:, :, :],
                                                 gam[:, :].unsqueeze(1).broadcast_to([P, K, D]), ALU.mult))
                        c.link(dve.tensor_tensor(mid[:, :, :], mid[:, :, :],
                                                 bet[:, :].unsqueeze(1).broadcast_to([P, K, D]), ALU.add))
                        out_free(0, b, q, first)
                        dve.scalar_tensor_tensor(outs[0][:, b], mid[:, :, :], 0.0, x_in[2][:, b], ALU.max,
                                                 ALU.add).then_inc(s_used.sem, 1)
                        dve.wait_ge(s_used.sem, s_used.at(s + 1))
                        stats(c.link, outs[0][:, b], s, b, 1)
                    if kind in ("gcn", "last"):
                        dv = dinv[:, bass.ds(s * K, K)].unsqueeze(2).broadcast_to([P, K, D])
                        if kind == "gcn" and first != 0:
                            dve.wait_ge(s_used.sem, s_used.at(s))
                        c.link(dve.tensor_tensor(mid[:, :, :], x_in[0][:, b], x_in[1][:, b], ALU.add))
                        c.link(dve.tensor_tensor(mid[:, :, :], mid[:, :, :], dv, ALU.mult))
                        if kind == "gcn":
                            dve.tensor_tensor(h[:, b], mid[:, :, :], bia[:, :].unsqueeze(1).broadcast_to([P, K, D]),
                                              ALU.add).then_inc(s_used.sem, 1)
                        else:
                            c.link(dve.tensor_tensor(mid[:, :, :], mid[:, :, :],
                                                     bia[:, :].unsqueeze(1).broadcast_to([P, K, D]), ALU.add))
                            out_free(0, b, q, first)
                            dve.scalar_tensor_tensor(outs[0][:, b], mid[:, :, :], 0.0, x_in[2][:, b], ALU.max,
                                                     ALU.add).then_inc(s_used.sem, 1)
                            dve.wait_ge(s_used.sem, s_used.at(s + 1))
                            stats(c.link, outs[0][:, b], s, b, 0)
                    return c

                def tail(c, s, b):
                    if norms:
                        scale(c.link, s, b, norms - 1)
                    c.done()

                def back(s, b):
                    ps = pO[:, :, :].rearrange("p a (b w) -> p (a b) w", b=2)
                    dve.wait_ge(s_mm.sem, s_mm.at(rounds * s + 1))
                    if own_rows:
                        dve.tensor_copy(h[:, b, :, D:ROW], ps[:, :, 0:2 * H]).then_inc(s_ev.sem, 1)
                    if kind == "join":
                        dve.tensor_tensor(outs[2][:, b], ps[:, :, ROW:ROW + D], h[:, b], ALU.add).then_inc(s_ev.sem, 1)
                    if kind in ("layer", "gcn"):
                        dv = dinv[:, bass.ds(s * K, K)].unsqueeze(2).broadcast_to([P, K, D])
                        j = len(outs) - 1
                        dve.tensor_tensor(outs[j][:, b], ps[:, :, 0:D], dv, ALU.mult).then_inc(s_ev.sem, 1)
                    if kind == "last":
                        for r in range(2):
                            dve.wait_ge(s_mm.sem, s_mm.at(2 * s + r + 1))
                            ks = slice(r * HALF, r * HALF + HALF)
                            dve.tensor_scalar(outs[1][:, b, ks, :], pO[:, :, 0:D], 0.0, None, ALU.max)
                            dve.tensor_copy(outs[2][:, b, ks, :], pO[:, :, D:2 * D]).then_inc(s_ev.sem, 1)

                def free_back(s, b, q, first):
                    js = {"first": [], "gat": [], "join": [2], "layer": [1], "gcn": [0], "last": [1, 2]}[kind]
                    if first is None or first >= 2:
                        for j in js:
                            dve.wait_ge(s_out[j][b].sem, s_out[j][b].at(16 * q))

                def body(s, b, q, first):
                    c = head(s, b, q, first)
                    if first != 0:
                        qq = q - 1 if b == 0 else q
                        free_back(s - 1, 1 - b, qq, None if first is None else first - 1)
                        back(s - 1, 1 - b)
                    tail(c, s, b)

                steps(dve, NSTEP, body)
                free_back(NSTEP - 1, (NSTEP - 1) % 2, (NSTEP - 1) // 2, None)
                back(NSTEP - 1, (NSTEP - 1) % 2)

            @block.scalar
            def _(act):
                def norm(s, b, j):
                    act.wait_ge(s_var.sem, s_var.at(norms * s + j + 1))
                    nc.scalar.activation(tmp[:, b, j, 4, :], tmp[:, b, j, 3, :], ACT.Sqrt, scale=1.0 / D,
                                         bias=eps_col[:, :]).then_inc(s_dev.sem, 1)

                def apply(s, b, j, x, y, func, sig):
                    act.wait_ge(s_scale.sem, s_scale.at(norms * s + j + 1))
                    for k in range(K):
                        last = nc.scalar.activation(y[:, k, 0:D], x[:, k, 0:D], func, scale=tmp[:, b, j, 5, k:k + 1],
                                                    bias=tmp[:, b, j, 6, k:k + 1])
                    last.then_inc(sig.sem, 1)

                def back(s, b, q, full):
                    ps = pO[:, :, :].rearrange("p a (b w) -> p (a b) w", b=2)
                    js = {"first": [1], "gat": [1], "join": [1], "layer": [], "gcn": [], "last": [3]}[kind]
                    if full:
                        for j in js:
                            act.wait_ge(s_out[j][b].sem, s_out[j][b].at(16 * q))
                    if act_reads and kind != "last":
                        act.wait_ge(s_ev.sem, s_ev.at(s + 1))
                    if own_rows:
                        nc.scalar.copy(outs[1][:, b], ps[:, :, 2 * H:ROW]).then_inc(s_ev2.sem, 1)
                    elif kind == "join":
                        nc.scalar.copy(outs[1][:, b], ps[:, :, 0:ROW]).then_inc(s_ev2.sem, 1)
                    elif kind == "last":
                        for r in range(2):
                            act.wait_ge(s_ev.sem, s_ev.at(2 * s + r + 1))
                            ks = slice(r * HALF, r * HALF + HALF)
                            nc.scalar.copy(outs[3][:, b, ks, :], pO[:, :, 2 * D:3 * D]).then_inc(s_ev2.sem, 1)
                        act.wait_ge(s_st.sem, s_st.at(s))
                        nc.scalar.activation(squares[:, :, :], outs[1][:, b], ACT.Square).then_inc(s_sq.sem, 1)

                def body(s, b, q, first):
                    if kind == "layer":
                        norm(s, b, 0)
                        apply(s, b, 0, mid[:, :, :], mid[:, :, :], ACT.Identity, s_norm)
                    if norms:
                        norm(s, b, norms - 1)
                    if first != 0:
                        qq = q - 1 if b == 0 else q
                        back(s - 1, 1 - b, qq, first is None or first >= 3)
                    if norms:
                        if first is None:
                            if own_rows:
                                act.wait_ge(s_out[0][b].sem, s_out[0][b].at(16 * q))
                            if kind == "join":
                                act.wait_ge(s_ev.sem, s_ev.at(s - 1))
                        src = {"first": x_in[0], "join": outs[0], "layer": outs[0], "last": outs[0]}[kind]
                        apply(s, b, norms - 1, src[:, b], h[:, b], ACT.Relu, s_h)
                    elif kind == "gcn":
                        act.wait_ge(s_used.sem, s_used.at(s + 1))
                        nc.scalar.activation(h[:, b], h[:, b], ACT.Relu).then_inc(s_h.sem, 1)
                    for r in range(2):
                        act.wait_ge(s_tr.sem, s_tr.at(2 * s + r + 1))
                        act.wait_ge(s_mm.sem, s_mm.at(rounds * s))
                        nc.scalar.copy(hT[0:D, r, :], pT[:, r, 0:HALF * P]).then_inc(s_hT.sem, 1)

                steps(act, NSTEP, body)
                back(NSTEP - 1, (NSTEP - 1) % 2, (NSTEP - 1) // 2, True)

            @block.tensor
            def _(pe):
                def sums_of(s, b):
                    pe.wait_ge(s_sq.sem, s_sq.at(s + 1))
                    for r in range(2):
                        ks = slice(r * HALF, r * HALF + HALF)
                        pe.matmul(sums[0], ones[0:P, 0:1], outs[1][:, b, ks, :], start=False, stop=False)
                        last = pe.matmul(sums[1], ones[0:P, 0:1], squares[:, ks, :], start=False, stop=False)
                    last.then_inc(s_st.sem, 1)

                def body(s, b, q, first):
                    pe.wait_ge(s_h.sem, s_h.at(s + 1))
                    for r in range(2):
                        pe.wait_ge(s_hT.sem, s_hT.at(2 * s))
                        for k in range(HALF):
                            last = pe.transpose(pT[:, r, k * P:(k + 1) * P], h[:, b, r * HALF + k, 0:D],
                                                ident[0:P, 0:P])
                        last.then_inc(s_tr.sem, 1)
                    if kind == "last" and first != 0:
                        sums_of(s - 1, 1 - b)
                    for r in range(2):
                        pe.wait_ge(s_hT.sem, s_hT.at(2 * s + r + 1))
                        pe.wait_ge(s_ev.sem, s_ev.at(rounds * s + (r if rounds == 2 else 0)))
                        if act_reads:
                            pe.wait_ge(s_ev2.sem, s_ev2.at(rounds * s + (r if rounds == 2 else 0)))
                        for k in range(HALF):
                            kk = r * HALF + k
                            o = pO[:, k, 0:width] if rounds == 2 else pO[:, kk // 2, (kk % 2) * 256:(kk % 2) * 256 + width]
                            last = pe.matmul(o, hT[:, r, k * P:(k + 1) * P], wide[:, :], start=True, stop=True)
                        if rounds == 2 or r == 1:
                            last.then_inc(s_mm.sem, 1)

                if kind == "last":
                    for acc in sums:
                        pe.matmul(acc, zeros[:, 0:1], zeros[:, :], start=True, stop=False)
                steps(pe, NSTEP, body)
                if kind == "last":
                    sums_of(NSTEP - 1, (NSTEP - 1) % 2)
                    for acc in sums:
                        pe.matmul(acc, zeros[:, 0:1], zeros[:, :], start=False, stop=True)

        for sg in s_in + s_out:
            for b in range(2):
                sg[b].base += 16 * (NSTEP // 2)
        s_dve.base += links * NSTEP
        s_tr.base += 2 * NSTEP
        s_hT.base += 2 * NSTEP
        s_mm.base += rounds * NSTEP
        s_ev.base += rounds * NSTEP
        s_h.base += NSTEP
        if act_reads:
            s_ev2.base += rounds * NSTEP
        if not own_rows:
            s_used.base += NSTEP
        s_var.base += norms * NSTEP
        s_dev.base += norms * NSTEP
        s_scale.base += norms * NSTEP
        if kind == "layer":
            s_norm.base += NSTEP
        if kind == "last":
            s_sq.base += NSTEP
            s_st.base += NSTEP

    def aggregate_phase(name, held, with_count, sums):
        with ExitStack() as ctx:
            y = ctx.enter_context(nc.sbuf_tensor(f"{name}_y", [P, 2, K, D], F32))
            c = ctx.enter_context(nc.sbuf_tensor(f"{name}_c", [P, 2, K, AGG], F32))
            squares = ctx.enter_context(nc.sbuf_tensor(f"{name}_sq", [P, 2, K, D], F32))
            zeros = ctx.enter_context(nc.sbuf_tensor(f"{name}_zeros", [P, HALF * D], F32))
            s_y = [signal(f"load_a{b}") for b in range(2)]
            s_c = [signal(f"load_b{b}") for b in range(2)]
            s_h, s_sq, s_st, s_z = signal("h_ready"), signal("squared"), signal("summed"), signal("setup")
            s_dve = signal("dve_chain")
            block = ctx.enter_context(nc.Block())

            @block.sync
            def _(sp):
                def body(s, b, q, first):
                    if first is None:
                        sp.wait_ge(s_h.sem, s_h.at(s - 1))
                        sp.nop(nofuse=True)
                    sp.dma_start(y[:, b], rows(d_y, s)).then_inc(s_y[b].sem, 16)
                    sp.dma_start(c[:, b], rows(t_agg, s)).then_inc(s_c[b].sem, 16)

                steps(sp, NSTEP, body)

            @block.vector
            def _(dve):
                dve.memset(zeros[:, :], 0.0).then_inc(s_z.sem, 1)

                def body(s, b, q, first):
                    dve.wait_ge(s_y[b].sem, s_y[b].at(16 * (q + 1)))
                    dve.wait_ge(s_c[b].sem, s_c[b].at(16 * (q + 1)))
                    if with_count:
                        dve.tensor_copy(count[:, bass.ds(s * K, K)], c[:, b, :, D])
                    dve.tensor_tensor(held[:, bass.ds(s * K, K), :], y[:, b], c[:, b, :, 0:D],
                                      ALU.add).then_inc(s_h.sem, 1)

                steps(dve, NSTEP, body)
                if with_count:
                    dve.wait_ge(s_h.sem, s_h.at(NSTEP))
                    dve.tensor_scalar(dinv[:, :], count[:, :], 1.0, None, ALU.add).then_inc(s_dve.sem, 1)
                    dve.wait_ge(s_sq.sem, s_sq.at(NSTEP + 1))
                    dve.reciprocal(dinv[:, :], dinv[:, :])

            @block.scalar
            def _(act):
                def body(s, b, q, first):
                    act.wait_ge(s_h.sem, s_h.at(s + 1))
                    if first is None:
                        act.wait_ge(s_st.sem, s_st.at(s - 1))
                    nc.scalar.activation(squares[:, b], held[:, bass.ds(s * K, K), :],
                                         ACT.Square).then_inc(s_sq.sem, 1)

                steps(act, NSTEP, body)
                if with_count:
                    act.wait_ge(s_dve.sem, s_dve.at(1))
                    nc.scalar.activation(dinv[:, :], dinv[:, :], ACT.Sqrt).then_inc(s_sq.sem, 1)

            @block.tensor
            def _(pe):
                pe.wait_ge(s_z.sem, s_z.at(1))
                for acc in sums:
                    pe.matmul(acc, zeros[:, 0:1], zeros[:, :], start=True, stop=False)

                def body(s, b, q, first):
                    pe.wait_ge(s_h.sem, s_h.at(s + 1))
                    for r in range(2):
                        pe.matmul(sums[0], ones[0:P, 0:1], held[:, bass.ds(s * K + r * HALF, HALF), :],
                                  start=False, stop=False)
                    pe.wait_ge(s_sq.sem, s_sq.at(s + 1))
                    for r in range(2):
                        last = pe.matmul(sums[1], ones[0:P, 0:1], squares[:, b, r * HALF:r * HALF + HALF, :],
                                         start=False, stop=False)
                    last.then_inc(s_st.sem, 1)

                steps(pe, NSTEP, body)
                for acc in sums:
                    pe.matmul(acc, zeros[:, 0:1], zeros[:, :], start=False, stop=True)

        for sg in s_y + s_c:
            sg.base += 16 * (NSTEP // 2)
        s_z.base += 1
        s_h.base += NSTEP
        s_st.base += NSTEP
        s_sq.base += NSTEP
        if with_count:
            s_sq.base += 1
            s_dve.base += 1

    GATHER = bass.IndirectOffsetOnAxis

    def gather_step(pool, chain, s, parts):
        for idx, ring_idx, _, _, _, _ in parts:
            ins = pool.tensor_copy(ring_idx, idx[:, bass.ds(s * K, K)])
            chain.k += 1
            ins.then_inc(chain.sig.sem, 1)
        pool.wait_ge(chain.sig.sem, chain.sig.at(chain.per * s + chain.k))
        pool.nop(nofuse=True)
        for _, ring_idx, table, ring, w, sig in parts:
            for k in range(K):
                pool.indirect_dma_start(out=ring[:, k, 0:w], out_offset=None, in_=table,
                                        in_offset=GATHER(ap=ring_idx[:, k:k + 1], axis=0)).then_inc(sig.sem, 16)

    def scatter_step(pool, chain, ring_idx, sums, sig, step):
        chain.link(pool.tensor_copy(ring_idx, out_idx[:, bass.ds(step * K, K)]))
        pool.nop(nofuse=True)
        for k in range(K):
            pool.indirect_dma_start(out=t_agg, out_offset=GATHER(ap=ring_idx[:, k:k + 1], axis=0),
                                    in_=sums[:, k, :], in_offset=None).then_inc(sig.sem, 16)

    def run_sums(dve, chain, s, b, ks, sums, same, msg, s_m):
        for k in ks:
            prev = sums[:, b, k - 1, :] if k else sums[:, 1 - b, K - 1, :]
            ins = dve.scalar_tensor_tensor(sums[:, b, k, :], prev, same[:, b, k:k + 1], msg[:, k, :],
                                           ALU.mult, ALU.add)
            if k < K - 1:
                chain.link(ins)
            else:
                ins.then_inc(s_m.sem, 1)
                dve.wait_ge(s_m.sem, s_m.at(s + 1))

    def close_segments(name, tail):
        with ExitStack() as ctx:
            carry = ctx.enter_context(nc.sbuf_tensor(f"{name}_before", [P, AGG], F32))
            row = ctx.enter_context(nc.sbuf_tensor(f"{name}_row", [P, 2, AGG], F32))
            pc = ctx.enter_context(nc.psum_tensor(f"{name}_pc", [P, AGG], F32))
            s_pe, s_dve, s_g, s_s = signal("pe_done"), signal("dve_chain"), signal("gather_a0"), signal("scatter_0")
            block = ctx.enter_context(nc.Block())

            @block.tensor
            def _(pe):
                pe.matmul(pc[:, :], mask_f[:, :], tail, start=True, stop=True).then_inc(s_pe.sem, 1)

            @block.vector
            def _(dve):
                dve.wait_ge(s_pe.sem, s_pe.at(1))
                dve.tensor_copy(carry[:, :], pc[:, :]).then_inc(s_dve.sem, 1)
                dve.wait_ge(s_g.sem, s_g.at(16))
                dve.wait_ge(s_dve.sem, s_dve.at(1))
                dve.tensor_tensor(row[:, 1, :], row[:, 0, :], carry[:, :], ALU.add).then_inc(s_dve.sem, 1)

            @block.gpsimd
            def _(pool):
                pool.indirect_dma_start(out=row[:, 0, :], out_offset=None, in_=t_agg,
                                        in_offset=GATHER(ap=fix_idx[:, :], axis=0)).then_inc(s_g.sem, 16)
                pool.wait_ge(s_dve.sem, s_dve.at(2))
                pool.nop(nofuse=True)
                pool.indirect_dma_start(out=t_agg, out_offset=GATHER(ap=fix_idx[:, :], axis=0), in_=row[:, 1, :],
                                        in_offset=None).then_inc(s_s.sem, 16)
                pool.wait_ge(s_s.sem, s_s.at(16))

        s_pe.base += 1
        s_dve.base += 2
        s_g.base += 16
        s_s.base += 16

    def softmax(name, e, e_self, alpha, factor):
        with ExitStack() as ctx:
            def sb(nm, shape):
                return ctx.enter_context(nc.sbuf_tensor(f"{name}_{nm}", shape, F32))

            fw, bw, den = sb("fw", [P, H, ET]), sb("bw", [P, H, ET]), sb("den", [P, H, ET])
            rep, cand = sb("rep", [P, 2, H, P]), sb("cand", [P, 2, H, P])
            ends, carry = sb("ends", [P, 2, H]), sb("carry", [P, 2, H])
            turned = ctx.enter_context(nc.psum_tensor(f"{name}_turned", [P, 2, 512], F32))
            summed = ctx.enter_context(nc.psum_tensor(f"{name}_summed", [P, 2, H], F32))
            s_dve, s_pe, s_exp = signal("dve_chain"), signal("pe_done"), signal("act_done")
            n_link = 18
            block = ctx.enter_context(nc.Block())

            @block.vector
            def _(dve):
                c = Chain(dve, s_dve, n_link)

                def scans(data, gate_f, gate_b, op0, op1, init):
                    for h in range(H):
                        a, b = (init, init) if isinstance(init, float) else (init[:, 0, h:h + 1], init[:, 1, h:h + 1])
                        dve.tensor_tensor_scan(fw[:, h, :], gate_f[:, :], data[:, h, :], a, op0, op1)
                        last = dve.tensor_tensor_scan(bw[:, h, ::-1], gate_b[:, ::-1], data[:, h, ::-1], b, op0, op1)
                    return last

                dve.scalar_tensor_tensor(e, e, SLOPE, e, ALU.mult, ALU.max)
                c.link(dve.scalar_tensor_tensor(e_self, e_self, SLOPE, e_self, ALU.mult, ALU.max))
                c.link(scans(e, pen_f, pen_b, ALU.add, ALU.max, -BIG))
                for h in range(H):
                    dve.tensor_scalar(rep[:, 0, h, :], ones[0:P, 0:P], fw[:, h, ET - 1:ET], None, ALU.mult)
                    last = dve.tensor_scalar(rep[:, 1, h, :], ones[0:P, 0:P], bw[:, h, 0:1], None, ALU.mult)
                c.link(last)
                dve.wait_ge(s_pe.sem, s_pe.at(1))
                for j, far in enumerate((far_f, far_b)):
                    last = dve.tensor_tensor(cand[:, j, :, :], turned[:, j, 0:H * P].rearrange("p (h q) -> p h q", h=H),
                                             far[:, :].unsqueeze(1).broadcast_to([P, H, P]), ALU.add)
                c.link(last)
                c.link(dve.tensor_reduce(carry[:, :, :], cand[:, :, :, :], AX.X, ALU.max))
                c.link(scans(e, pen_f, pen_b, ALU.add, ALU.max, carry))
                c.link(dve.tensor_tensor(fw[:, :, :], fw[:, :, :], bw[:, :, :], ALU.max))
                c.link(dve.tensor_tensor(fw[:, :, :], fw[:, :, :], e_self, ALU.max))
                dve.tensor_tensor(e, e, fw[:, :, :], ALU.subtract)
                c.link(dve.tensor_tensor(e_self, e_self, fw[:, :, :], ALU.subtract))
                dve.wait_ge(s_exp.sem, s_exp.at(1))
                c.link(scans(e, same_f, same_b, ALU.mult, ALU.add, 0.0))
                dve.tensor_copy(ends[:, 0, :], fw[:, :, ET - 1])
                c.link(dve.tensor_copy(ends[:, 1, :], bw[:, :, 0]))
                dve.wait_ge(s_pe.sem, s_pe.at(2))
                c.link(dve.tensor_copy(carry[:, :, :], summed[:, :, :]))
                c.link(scans(e, same_f, same_b, ALU.mult, ALU.add, carry))
                c.link(dve.tensor_tensor(den[:, :, :], fw[:, :, :], bw[:, :, :], ALU.add))
                c.link(dve.tensor_tensor(den[:, :, :], den[:, :, :], e, ALU.subtract))
                c.link(dve.scalar_tensor_tensor(den[:, :, :], den[:, :, :], 1e-16, e_self, ALU.add, ALU.add))
                c.link(dve.reciprocal(den[:, :, :], den[:, :, :]))
                c.link(dve.scalar_tensor_tensor(alpha, e, factor, den[:, :, :], ALU.mult, ALU.mult))
                c.done()

            @block.scalar
            def _(act):
                act.wait_ge(s_dve.sem, s_dve.at(9))
                nc.scalar.activation(e, e, ACT.Exp)
                nc.scalar.activation(e_self, e_self, ACT.Exp).then_inc(s_exp.sem, 1)

            @block.tensor
            def _(pe):
                pe.wait_ge(s_dve.sem, s_dve.at(3))
                for j in range(2):
                    for h in range(H):
                        last = pe.transpose(turned[:, j, h * P:(h + 1) * P], rep[:, j, h, :], ident[0:P, 0:P])
                last.then_inc(s_pe.sem, 1)
                pe.wait_ge(s_dve.sem, s_dve.at(11))
                pe.matmul(summed[:, 0, :], mask_f[:, :], ends[:, 0, :], start=True, stop=True)
                pe.matmul(summed[:, 1, :], mask_b[:, :], ends[:, 1, :], start=True, stop=True).then_inc(s_pe.sem, 1)

        s_dve.base += n_link
        s_pe.base += 2
        s_exp.base += 1

    def gat_edges(name, table, W):
        with ExitStack() as outer:
            def sbo(nm, shape, dt=F32):
                return outer.enter_context(nc.sbuf_tensor(f"{name}_{nm}", shape, dt))

            z = sbo("z", [P, ET, D])
            e, e_self, alpha = sbo("e", [P, H, ET]), sbo("es", [P, H, ET]), sbo("alpha", [P, H, ET])
            with ExitStack() as ctx:
                xs = ctx.enter_context(nc.sbuf_tensor(f"{name}_xs", [P, 2, K, ROW], F32))
                xd = ctx.enter_context(nc.sbuf_tensor(f"{name}_xd", [P, 2, K, ROW], F32))
                idx = ctx.enter_context(nc.sbuf_tensor(f"{name}_idx", [P, 2, 2, K], I32))
                s_g = [[signal(f"gather_{c}{b}") for b in range(2)] for c in "ab"]
                s_pool, s_used = signal("pool_chain"), signal("inputs_used")
                block = ctx.enter_context(nc.Block())

                @block.gpsimd
                def _(pool):
                    def body(s, b, q, first):
                        if first is None:
                            pool.wait_ge(s_used.sem, s_used.at(s - 1))
                        gather_step(pool, Chain(pool, s_pool, 2, s), s,
                                    [(src_idx, idx[:, b, 0, :], table, xs[:, b], ROW, s_g[0][b]),
                                     (dst_idx, idx[:, b, 1, :], table, xd[:, b], ROW, s_g[1][b])])

                    steps(pool, ESTEP, body)

                @block.vector
                def _(dve):
                    def body(s, b, q, first):
                        for sg in s_g:
                            dve.wait_ge(sg[b].sem, sg[b].at(16 * K * (q + 1)))
                        at = bass.ds(s * K, K)
                        dve.tensor_tensor(z[:, at, :], xs[:, b, :, 0:D], xd[:, b, :, 0:D], ALU.subtract)
                        dve.tensor_tensor(e[:, :, at], xs[:, b, :, D:D + H].rearrange("p k h -> p h k"),
                                          xd[:, b, :, D + H:ROW].rearrange("p k h -> p h k"), ALU.add)
                        dve.tensor_tensor(e_self[:, :, at], xd[:, b, :, D:D + H].rearrange("p k h -> p h k"),
                                          xd[:, b, :, D + H:ROW].rearrange("p k h -> p h k"),
                                          ALU.add).then_inc(s_used.sem, 1)

                    steps(dve, ESTEP, body)

            for sg in s_g:
                sg[0].base += 16 * K * ((ESTEP + 1) // 2)
                sg[1].base += 16 * K * (ESTEP // 2)
            s_pool.base += 2 * ESTEP
            s_used.base += ESTEP

            softmax(name, e[:, :, :], e_self[:, :, :], alpha[:, :, :], 1.0 / H if W is not None else 1.0)

            sums = sbo("sums", [P, 2, K, AGG])
            with ExitStack() as ctx:
                def sb(nm, shape, dt=F32):
                    return ctx.enter_context(nc.sbuf_tensor(f"{name}_{nm}", shape, dt))

                idx = sb("sidx", [P, 2, K], I32)
                al = sb("al", [P, 2, K, H])
                msg = sb("msg", [P, K, AGG])
                same = sb("same", [P, 2, K])
                s_sc = [signal(f"scatter_{b}") for b in range(2)]
                s_pool, s_dve, s_m, s_set = signal("pool_chain"), signal("dve_chain"), signal("sums_ready"), signal("setup")
                s_zc, s_tr, s_hT, s_mm = signal("h_ready"), signal("turned"), signal("hT_ready"), signal("product_ready")
                s_ev, s_w = signal("product_used"), signal("weights")
                if W is not None:
                    zc = sb("zc", [P, 2, K, D])
                    zT = sb("zT", [D, 2, 2, HALF * P])
                    w = sb("w", [D, H * D])
                    pT = ctx.enter_context(nc.psum_tensor(f"{name}_pT", [D, 2, 512], F32))
                    pY = ctx.enter_context(nc.psum_tensor(f"{name}_pY", [P, 4, 512], F32))
                    links = 2 + (K // 2) * (H - 1) + (K - 1)
                else:
                    links = 2 + 1 + (K - 1)
                block = ctx.enter_context(nc.Block())

                @block.gpsimd
                def _(pool):
                    def body(s, b, q, first):
                        pool.wait_ge(s_m.sem, s_m.at(s + 1))
                        scatter_step(pool, Chain(pool, s_pool, 1, s), idx[:, b, :], sums[:, b], s_sc[b], s)

                    steps(pool, ESTEP, body)
                    pool.wait_ge(s_sc[0].sem, s_sc[0].at(16 * K * ((ESTEP + 1) // 2)))
                    pool.wait_ge(s_sc[1].sem, s_sc[1].at(16 * K * (ESTEP // 2)))

                @block.vector
                def _(dve):
                    dve.memset(msg[:, :, :], 1.0)
                    dve.memset(sums[:, :, :, :], 0.0).then_inc(s_set.sem, 1)
                    dve.wait_ge(s_set.sem, s_set.at(1))

                    def body(s, b, q, first):
                        c = Chain(dve, s_dve, links, s)
                        at = bass.ds(s * K, K)
                        c.link(dve.tensor_copy(al[:, b, :, :], alpha[:, :, at].rearrange("p h k -> p k h")))
                        c.link(dve.tensor_copy(same[:, b, :], same_f[:, at]))
                        if first is None:
                            dve.wait_ge(s_sc[b].sem, s_sc[b].at(16 * K * q))
                        if W is None:
                            c.link(dve.tensor_tensor(
                                msg[:, :, 0:D].rearrange("p k (h c) -> p k h c", h=H),
                                z[:, at, :].rearrange("p k (h c) -> p k h c", h=H),
                                al[:, b, :, :].unsqueeze(3).broadcast_to([P, K, H, DH]), ALU.mult))
                            run_sums(dve, c, s, b, range(K), sums, same, msg, s_m)
                        else:
                            for j in range(K // 2):
                                dve.wait_ge(s_mm.sem, s_mm.at((K // 2) * s + j + 1))
                                for h in range(H):
                                    for k in (2 * j, 2 * j + 1):
                                        y, a = pY[:, k % 4, h * D:(h + 1) * D], al[:, b, k, h:h + 1]
                                        if h == 0:
                                            ins = dve.tensor_scalar(msg[:, k, 0:D], y, a, None, ALU.mult)
                                        else:
                                            ins = dve.scalar_tensor_tensor(msg[:, k, 0:D], y, a, msg[:, k, 0:D],
                                                                           ALU.mult, ALU.add)
                                    if h < H - 1:
                                        c.link(ins)
                                ins.then_inc(s_ev.sem, 1)
                                dve.wait_ge(s_ev.sem, s_ev.at((K // 2) * s + j + 1))
                                run_sums(dve, c, s, b, (2 * j, 2 * j + 1), sums, same, msg, s_m)
                        c.done()

                    steps(dve, ESTEP, body)

                if W is not None:
                    @block.sync
                    def _(sp):
                        sp.dma_start(w[:, :], W).then_inc(s_w.sem, 16)

                    @block.scalar
                    def _(act):
                        def body(s, b, q, first):
                            nc.scalar.copy(zc[:, b, :, :], z[:, bass.ds(s * K, K), :]).then_inc(s_zc.sem, 1)
                            for r in range(2):
                                act.wait_ge(s_tr.sem, s_tr.at(2 * s + r + 1))
                                if first is None:
                                    act.wait_ge(s_mm.sem, s_mm.at((K // 2) * (s - 1)))
                                nc.scalar.copy(zT[:, b, r, :], pT[:, r, 0:HALF * P]).then_inc(s_hT.sem, 1)

                        steps(act, ESTEP, body)

                    @block.tensor
                    def _(pe):
                        pe.wait_ge(s_w.sem, s_w.at(16))

                        def body(s, b, q, first):
                            pe.wait_ge(s_zc.sem, s_zc.at(s + 1))
                            for r in range(2):
                                pe.wait_ge(s_hT.sem, s_hT.at(2 * s))
                                for k in range(HALF):
                                    last = pe.transpose(pT[:, r, k * P:(k + 1) * P], zc[:, b, r * HALF + k, :],
                                                        ident[0:P, 0:P])
                                last.then_inc(s_tr.sem, 1)
                            for j in range(K // 2):
                                pe.wait_ge(s_hT.sem, s_hT.at(2 * s + j // 2 + 1))
                                if first != 0 or j > 0:
                                    pe.wait_ge(s_ev.sem, s_ev.at((K // 2) * s + j - 1))
                                for k in (2 * j, 2 * j + 1):
                                    last = pe.matmul(pY[:, k % 4, 0:H * D],
                                                     zT[:, b, k // HALF, (k % HALF) * P:(k % HALF + 1) * P], w[:, :],
                                                     start=True, stop=True)
                                last.then_inc(s_mm.sem, 1)

                        steps(pe, ESTEP, body)

            s_sc[0].base += 16 * K * ((ESTEP + 1) // 2)
            s_sc[1].base += 16 * K * (ESTEP // 2)
            s_pool.base += ESTEP
            s_dve.base += links * ESTEP
            s_m.base += ESTEP
            s_set.base += 1
            if W is not None:
                s_w.base += 16
                s_zc.base += ESTEP
                s_tr.base += 2 * ESTEP
                s_hT.base += 2 * ESTEP
                s_mm.base += (K // 2) * ESTEP
                s_ev.base += (K // 2) * ESTEP
            close_segments(name + "_close", sums[:, (ESTEP - 1) % 2, K - 1, :])

    def gcn_edges(name, table):
        with ExitStack() as ctx:
            def sb(nm, shape, dt=F32):
                return ctx.enter_context(nc.sbuf_tensor(f"{name}_{nm}", shape, dt))

            sums = sb("sums", [P, 2, K, AGG])
            x = sb("x", [P, 2, K, AGG])
            same = sb("same", [P, 2, K])
            idx = sb("idx", [P, 2, 2, K], I32)
            s_g = [signal(f"gather_a{b}") for b in range(2)]
            s_sc = [signal(f"scatter_{b}") for b in range(2)]
            s_pool, s_dve, s_m, s_set = signal("pool_chain"), signal("dve_chain"), signal("sums_ready"), signal("setup")
            links = 1 + (K - 1)
            with nc.Block() as block:
                @block.gpsimd
                def _(pool):
                    pool.wait_ge(s_set.sem, s_set.at(1))
                    pool.nop(nofuse=True)

                    def body(s, b, q, first):
                        c = Chain(pool, s_pool, 2, s)
                        c.k = 0 if first == 0 else -1
                        gather_step(pool, c, s, [(src_idx, idx[:, b, 0, :], table, x[:, b], D, s_g[b])])
                        if first != 0:
                            pool.wait_ge(s_m.sem, s_m.at(s))
                            scatter_step(pool, c, idx[:, 1 - b, 1, :], sums[:, 1 - b], s_sc[1 - b], s - 1)

                    steps(pool, ESTEP, body)
                    pool.wait_ge(s_m.sem, s_m.at(ESTEP))
                    b = (ESTEP - 1) % 2
                    c = Chain(pool, s_pool, 2, ESTEP)
                    c.k = -1
                    scatter_step(pool, c, idx[:, b, 1, :], sums[:, b], s_sc[b], ESTEP - 1)
                    pool.wait_ge(s_sc[0].sem, s_sc[0].at(16 * K * ((ESTEP + 1) // 2)))
                    pool.wait_ge(s_sc[1].sem, s_sc[1].at(16 * K * (ESTEP // 2)))

                @block.vector
                def _(dve):
                    dve.memset(sums[:, :, :, :], 0.0)
                    dve.memset(x[:, :, :, :], 1.0).then_inc(s_set.sem, 1)
                    dve.wait_ge(s_set.sem, s_set.at(1))

                    def body(s, b, q, first):
                        c = Chain(dve, s_dve, links, s)
                        c.link(dve.tensor_copy(same[:, b, :], same_f[:, bass.ds(s * K, K)]))
                        dve.wait_ge(s_g[b].sem, s_g[b].at(16 * K * (q + 1)))
                        if first is None:
                            dve.wait_ge(s_sc[b].sem, s_sc[b].at(16 * K * q))
                        run_sums(dve, c, s, b, range(K), sums, same, x[:, b], s_m)
                        c.done()

                    steps(dve, ESTEP, body)

            for sg in (s_g, s_sc):
                sg[0].base += 16 * K * ((ESTEP + 1) // 2)
                sg[1].base += 16 * K * (ESTEP // 2)
            s_pool.base += 2 * ESTEP
            s_dve.base += links * ESTEP
            s_m.base += ESTEP
            s_set.base += 1
            close_segments(name + "_close", sums[:, (ESTEP - 1) % 2, K - 1, :])

    def edge_mlp(name, wmsg):
        with ExitStack() as ctx:
            def sb(nm, shape, dt=F32):
                return ctx.enter_context(nc.sbuf_tensor(f"{name}_{nm}", shape, dt))

            attr = sb("attr", [P, ET, 4])
            now = sb("now", [P, 2, K, 4])
            aT = sb("aT", [4, 2, 2, HALF * P])
            we = sb("we", [4, D])
            r = sb("r", [D, 2, HALF * P])
            r2 = sb("r2", [D, HALF * P])
            acc = sb("acc", [D, 2, 2 * ESTEP])
            cols = sb("cols", [D, 12])
            shift = sb("shift", [D, AGG])
            wraw = sb("wraw", [D, D])
            bm = sb("bm", [AGG, D])
            pT = ctx.enter_context(nc.psum_tensor(f"{name}_pT", [4, 2, 512], F32))
            pY = ctx.enter_context(nc.psum_tensor(f"{name}_pY", [D, 2, 512], F32))
            pC = ctx.enter_context(nc.psum_tensor(f"{name}_pC", [AGG, D], F32))
            s_ld, s_now, s_tr, s_hT = signal("load_a0"), signal("h_ready"), signal("turned"), signal("hT_ready")
            s_mm, s_ev, s_dve, s_dev = signal("product_ready"), signal("product_used"), signal("dve_chain"), signal("dev_ready")
            s_pe, s_set, s_acc = signal("pe_done"), signal("setup"), signal("squared")
            with nc.Block() as block:
                @block.sync
                def _(sp):
                    column = lambda v: v.rearrange("(d a) -> d a", a=1)
                    sp.dma_start(attr[:, :, :], A["edge_attr_4"].rearrange("(p t) c -> p t c", t=ET)).then_inc(s_ld.sem, 16)
                    sp.dma_start(we[:, :], A["L3_gnn_W_edge"]).then_inc(s_ld.sem, 16)
                    for i, nm in enumerate(("b_edge", "g_edge", "beta_edge")):
                        sp.dma_start(cols[:, i:i + 1], column(A[f"L3_gnn_{nm}"]),
                                     allow_slow_non_contiguous=True).then_inc(s_ld.sem, 16)
                    sp.dma_start(wraw[:, :], A["L3_gnn_W_msg"][2 * D:3 * D, :]).then_inc(s_ld.sem, 16)
                    sp.dma_start(bm[D:AGG, :], row1(A["L3_gnn_b_msg"])).then_inc(s_ld.sem, 16)

                @block.vector
                def _(dve):
                    dve.memset(shift[:, :], 0.0).then_inc(s_set.sem, 1)
                    dve.wait_ge(s_ld.sem, s_ld.at(16 * 7))

                    def body(s, b, q, first):
                        for h in range(2):
                            dve.wait_ge(s_tr.sem, s_tr.at(2 * s + h + 1))
                            if first is None:
                                dve.wait_ge(s_mm.sem, s_mm.at(2 * (s - 1)))
                            dve.tensor_copy(aT[:, b, h, :], pT[:, h, 0:HALF * P]).then_inc(s_hT.sem, 1)

                    steps(dve, ESTEP, body)
                    c = Chain(dve, s_dve, 10)
                    dve.wait_ge(s_acc.sem, s_acc.at(2 * ESTEP))
                    c.link(dve.tensor_reduce(cols[:, 3:5], acc[:, :, :], AX.X, ALU.add))
                    c.link(dve.tensor_scalar(cols[:, 3:5], cols[:, 3:5], 1.0 / E, None, ALU.mult))
                    c.link(dve.tensor_tensor(cols[:, 5:6], cols[:, 3:4], cols[:, 3:4], ALU.mult))
                    c.link(dve.tensor_tensor(cols[:, 6:7], cols[:, 4:5], cols[:, 5:6], ALU.subtract))
                    dve.wait_ge(s_dev.sem, s_dev.at(1))
                    c.link(dve.reciprocal(cols[:, 7:8], cols[:, 6:7]))
                    c.link(dve.tensor_tensor(cols[:, 8:9], cols[:, 7:8], cols[:, 1:2], ALU.mult))
                    c.link(dve.tensor_tensor(cols[:, 9:10], cols[:, 3:4], cols[:, 8:9], ALU.mult))
                    c.link(dve.tensor_tensor(shift[:, D:AGG], cols[:, 2:3], cols[:, 9:10], ALU.subtract))
                    c.link(dve.tensor_scalar(wmsg[0:D, :], wraw[:, :], cols[:, 8:9], None, ALU.mult))
                    dve.wait_ge(s_pe.sem, s_pe.at(1))
                    c.link(dve.tensor_tensor(wmsg[D:AGG, :], pC[D:AGG, :], bm[D:AGG, :], ALU.add))
                    c.done()

                @block.scalar
                def _(act):
                    act.wait_ge(s_ld.sem, s_ld.at(16 * 7))

                    def body(s, b, q, first):
                        nc.scalar.copy(now[:, b], attr[:, bass.ds(s * K, K), :]).then_inc(s_now.sem, 1)
                        for h in range(2):
                            act.wait_ge(s_mm.sem, s_mm.at(2 * s + h + 1))
                            if first is None or first > 0 or h > 0:
                                act.wait_ge(s_acc.sem, s_acc.at(2 * s + h))
                            nc.scalar.activation(r[:, h, :], pY[:, h, 0:HALF * P], ACT.Relu, bias=cols[:, 0:1],
                                                 accum_out=acc[:, 0, bass.ds(2 * s + h, 1)]).then_inc(s_ev.sem, 1)
                            act.wait_ge(s_ev.sem, s_ev.at(2 * s + h + 1))
                            nc.scalar.activation(r2[:, :], r[:, h, :], ACT.Square,
                                                 accum_out=acc[:, 1, bass.ds(2 * s + h, 1)]).then_inc(s_acc.sem, 1)

                    steps(act, ESTEP, body)
                    act.wait_ge(s_dve.sem, s_dve.at(4))
                    nc.scalar.activation(cols[:, 6:7], cols[:, 6:7], ACT.Sqrt,
                                         bias=eps_col[0:D, :]).then_inc(s_dev.sem, 1)

                @block.tensor
                def _(pe):
                    pe.wait_ge(s_ld.sem, s_ld.at(16 * 7))

                    def body(s, b, q, first):
                        pe.wait_ge(s_now.sem, s_now.at(s + 1))
                        for h in range(2):
                            pe.wait_ge(s_hT.sem, s_hT.at(2 * s))
                            for k in range(HALF):
                                last = pe.transpose(pT[:, h, k * P:(k + 1) * P], now[:, b, h * HALF + k, :],
                                                    ident[0:P, 0:P])
                            last.then_inc(s_tr.sem, 1)
                        for h in range(2):
                            pe.wait_ge(s_hT.sem, s_hT.at(2 * s + h + 1))
                            pe.wait_ge(s_ev.sem, s_ev.at(2 * s))
                            pe.matmul(pY[:, h, 0:HALF * P], we[:, :], aT[:, b, h, :], start=True,
                                      stop=True).then_inc(s_mm.sem, 1)

                    steps(pe, ESTEP, body)
                    pe.wait_ge(s_dve.sem, s_dve.at(8))
                    pe.matmul(pC[:, :], shift[:, :], wraw[:, :], start=True, stop=True).then_inc(s_pe.sem, 1)

        s_ld.base += 16 * 7
        s_now.base += ESTEP
        for sg in (s_tr, s_hT, s_mm, s_ev, s_acc):
            sg.base += 2 * ESTEP
        s_dve.base += 10
        s_dev.base += 1
        s_pe.base += 1
        s_set.base += 1

    def message_edges(name, wmsg, totals):
        with ExitStack() as ctx:
            def sb(nm, shape, dt=F32):
                return ctx.enter_context(nc.sbuf_tensor(f"{name}_{nm}", shape, dt))

            attr = sb("attr", [P, ET, 4])
            now = sb("now", [P, 2, K, 4])
            aT = sb("aT", [4, 2, 2, HALF * P])
            we = sb("we", [4, D])
            be = sb("be", [D, 1])
            f = sb("f", [AGG, 2, HALF * P])
            u, v = sb("u", [P, 2, K, D]), sb("v", [P, 2, K, D])
            msg = sb("msg", [P, 2, K, AGG])
            squares = sb("squares", [P, 2, K, D])
            zeros = sb("zeros", [P, HALF * D])
            sums = sb("sums", [P, 2, K, AGG])
            same = sb("same", [P, 2, K])
            idx = sb("idx", [P, 2, 3, K], I32)
            pT = ctx.enter_context(nc.psum_tensor(f"{name}_pT", [4, 2, 512], F32))
            pY = ctx.enter_context(nc.psum_tensor(f"{name}_pY", [D, 512], F32))
            pF = ctx.enter_context(nc.psum_tensor(f"{name}_pF", [P, 2, 512], F32))
            s_g = [[signal(f"gather_{c}{b}") for b in range(2)] for c in "ab"]
            s_sc = [signal(f"scatter_{b}") for b in range(2)]
            s_pool, s_dve, s_m, s_set = signal("pool_chain"), signal("dve_chain"), signal("sums_ready"), signal("setup")
            s_ld, s_now, s_tr, s_hT = signal("load_a0"), signal("h_ready"), signal("turned"), signal("hT_ready")
            s_mm, s_f, s_pf, s_pre = signal("product_ready"), signal("product_used"), signal("features"), signal("var_ready")
            s_relu, s_sq, s_st = signal("normed"), signal("squared"), signal("summed")
            links = 2 + (K - 1)
            with nc.Block() as block:
                @block.sync
                def _(sp):
                    sp.dma_start(attr[:, :, :], A["edge_attr_4"].rearrange("(p t) c -> p t c", t=ET)).then_inc(s_ld.sem, 16)
                    sp.dma_start(we[:, :], A["L3_gnn_W_edge"]).then_inc(s_ld.sem, 16)
                    sp.dma_start(be[:, :], A["L3_gnn_b_edge"].rearrange("(d a) -> d a", a=1),
                                 allow_slow_non_contiguous=True).then_inc(s_ld.sem, 16)

                @block.gpsimd
                def _(pool):
                    def body(s, b, q, first):
                        c = Chain(pool, s_pool, 3, s)
                        c.k = 0 if first == 0 else -1
                        if first is None:
                            pool.wait_ge(s_pre.sem, s_pre.at(s - 1))
                        gather_step(pool, c, s, [(src_idx, idx[:, b, 0, :], t_u, u[:, b], D, s_g[0][b]),
                                                 (dst_idx, idx[:, b, 1, :], t_v, v[:, b], D, s_g[1][b])])
                        if first != 0:
                            pool.wait_ge(s_m.sem, s_m.at(s))
                            scatter_step(pool, c, idx[:, 1 - b, 2, :], sums[:, 1 - b], s_sc[1 - b], s - 1)

                    steps(pool, ESTEP, body)
                    pool.wait_ge(s_m.sem, s_m.at(ESTEP))
                    b = (ESTEP - 1) % 2
                    c = Chain(pool, s_pool, 3, ESTEP)
                    c.k = -1
                    scatter_step(pool, c, idx[:, b, 2, :], sums[:, b], s_sc[b], ESTEP - 1)
                    pool.wait_ge(s_sc[0].sem, s_sc[0].at(16 * K * ((ESTEP + 1) // 2)))
                    pool.wait_ge(s_sc[1].sem, s_sc[1].at(16 * K * (ESTEP // 2)))

                @block.vector
                def _(dve):
                    dve.memset(sums[:, :, :, :], 0.0)
                    dve.memset(f[:, :, :], 1.0)
                    dve.memset(zeros[:, :], 0.0)
                    dve.memset(msg[:, :, :, :], 1.0).then_inc(s_set.sem, 1)
                    dve.wait_ge(s_set.sem, s_set.at(1))

                    def attributes(s, b, first):
                        for h in range(2):
                            dve.wait_ge(s_tr.sem, s_tr.at(2 * s + h + 1))
                            if first is None:
                                dve.wait_ge(s_mm.sem, s_mm.at(2 * (s - 1)))
                            dve.tensor_copy(aT[:, b, h, :], pT[:, h, 0:HALF * P]).then_inc(s_hT.sem, 1)

                    def body(s, b, q, first):
                        c = Chain(dve, s_dve, links, s)
                        attributes(s, b, first)
                        c.link(dve.tensor_copy(same[:, b, :], same_f[:, bass.ds(s * K, K)]))
                        for sg in s_g:
                            dve.wait_ge(sg[b].sem, sg[b].at(16 * K * (q + 1)))
                        if first is None:
                            dve.wait_ge(s_st.sem, s_st.at(s - 1))
                        c.link(dve.tensor_tensor(msg[:, b, :, 0:D], u[:, b], v[:, b], ALU.add))
                        dve.wait_ge(s_pf.sem, s_pf.at(s + 1))
                        m4 = msg[:, b, :, :].rearrange("p (a k) c -> p a k c", a=2)[:, :, :, 0:D]
                        dve.tensor_tensor(m4, m4, pF[:, :, 0:HALF * D].rearrange("p a (k c) -> p a k c", k=HALF),
                                          ALU.add).then_inc(s_pre.sem, 1)
                        dve.wait_ge(s_relu.sem, s_relu.at(s + 1))
                        if first is None:
                            dve.wait_ge(s_sc[b].sem, s_sc[b].at(16 * K * q))
                        run_sums(dve, c, s, b, range(K), sums, same, msg[:, b], s_m)
                        c.done()

                    steps(dve, ESTEP, body)

                @block.scalar
                def _(act):
                    act.wait_ge(s_ld.sem, s_ld.at(48))
                    act.wait_ge(s_set.sem, s_set.at(1))

                    def body(s, b, q, first):
                        nc.scalar.copy(now[:, b], attr[:, bass.ds(s * K, K), :]).then_inc(s_now.sem, 1)
                        for h in range(2):
                            act.wait_ge(s_mm.sem, s_mm.at(2 * s + h + 1))
                            if first != 0:
                                act.wait_ge(s_pf.sem, s_pf.at(s))
                            nc.scalar.activation(f[0:D, h, :], pY[:, 0:HALF * P], ACT.Relu,
                                                 bias=be[:, :]).then_inc(s_f.sem, 1)
                        act.wait_ge(s_pre.sem, s_pre.at(s + 1))
                        nc.scalar.activation(msg[:, b, :, 0:D], msg[:, b, :, 0:D], ACT.Relu).then_inc(s_relu.sem, 1)
                        act.wait_ge(s_relu.sem, s_relu.at(s + 1))
                        if first is None:
                            act.wait_ge(s_st.sem, s_st.at(s - 1))
                        nc.scalar.activation(squares[:, b], msg[:, b, :, 0:D], ACT.Square).then_inc(s_sq.sem, 1)

                    steps(act, ESTEP, body)

                @block.tensor
                def _(pe):
                    pe.wait_ge(s_ld.sem, s_ld.at(48))
                    pe.wait_ge(s_set.sem, s_set.at(1))
                    for acc in totals:
                        pe.matmul(acc, zeros[:, 0:1], zeros[:, :], start=True, stop=False)

                    def total(s, b):
                        pe.wait_ge(s_sq.sem, s_sq.at(s + 1))
                        for r in range(2):
                            ks = slice(r * HALF, r * HALF + HALF)
                            pe.matmul(totals[0], ones[0:P, 0:1], msg[:, b, ks, 0:D], start=False, stop=False)
                            last = pe.matmul(totals[1], ones[0:P, 0:1], squares[:, b, ks, :], start=False, stop=False)
                        last.then_inc(s_st.sem, 1)

                    def body(s, b, q, first):
                        pe.wait_ge(s_now.sem, s_now.at(s + 1))
                        for h in range(2):
                            pe.wait_ge(s_hT.sem, s_hT.at(2 * s))
                            for k in range(HALF):
                                last = pe.transpose(pT[:, h, k * P:(k + 1) * P], now[:, b, h * HALF + k, :],
                                                    ident[0:P, 0:P])
                            last.then_inc(s_tr.sem, 1)
                        for h in range(2):
                            pe.wait_ge(s_hT.sem, s_hT.at(2 * s + h + 1))
                            pe.wait_ge(s_f.sem, s_f.at(2 * s + h))
                            pe.matmul(pY[:, 0:HALF * P], we[:, :], aT[:, b, h, :], start=True,
                                      stop=True).then_inc(s_mm.sem, 1)
                        pe.wait_ge(s_pre.sem, s_pre.at(s))
                        for h in range(2):
                            pe.wait_ge(s_f.sem, s_f.at(2 * s + h + 1))
                            for k in range(HALF):
                                last = pe.matmul(pF[:, h, k * D:(k + 1) * D], f[:, h, k * P:(k + 1) * P], wmsg[:, :],
                                                 start=True, stop=True)
                        last.then_inc(s_pf.sem, 1)
                        if first != 0:
                            total(s - 1, 1 - b)

                    steps(pe, ESTEP, body)
                    total(ESTEP - 1, (ESTEP - 1) % 2)
                    for acc in totals:
                        pe.matmul(acc, zeros[:, 0:1], zeros[:, :], start=False, stop=True)

            for sg in s_g + [s_sc]:
                sg[0].base += 16 * K * ((ESTEP + 1) // 2)
                sg[1].base += 16 * K * (ESTEP // 2)
            s_pool.base += 3 * ESTEP
            s_dve.base += links * ESTEP
            s_ld.base += 48
            s_set.base += 1
            for sg in (s_m, s_now, s_pf, s_pre, s_relu, s_sq, s_st):
                sg.base += ESTEP
            for sg in (s_tr, s_hT, s_mm, s_f):
                sg.base += 2 * ESTEP
            close_segments(name + "_close", sums[:, (ESTEP - 1) % 2, K - 1, :])

    def last_sum(name):
        with ExitStack() as ctx:
            def sb(nm, shape, dt=F32):
                return ctx.enter_context(nc.sbuf_tensor(f"{name}_{nm}", shape, dt))

            x, nf, c = sb("x", [P, 2, K, D]), sb("nf", [P, 2, K, D]), sb("c", [P, 2, K, AGG])
            y = sb("y", [P, 2, K, D])
            part = sb("part", [P, 2, K, D])
            s_in = [[signal(f"load_{j}{b}") for b in range(2)] for j in "abc"]
            s_out = [signal(f"store_a{b}") for b in range(2)]
            s_dve, s_ev, s_pool = signal("dve_chain"), signal("product_used"), signal("pool_chain")
            wide = lambda v: v[:, :].unsqueeze(1).broadcast_to([P, K, D])
            with nc.Block() as block:
                @block.sync
                def _(sp):
                    def body(s, b, q, first):
                        if first is None:
                            sp.wait_ge(s_ev.sem, s_ev.at(s - 1))
                            sp.nop(nofuse=True)
                        for (t, buf), sg in zip(((d_xc, x), (d_nf, nf), (t_agg, c)), s_in):
                            sp.dma_start(buf[:, b], rows(t, s)).then_inc(sg[b].sem, 16)
                        if first != 0:
                            sp.wait_ge(s_ev.sem, s_ev.at(s))
                            sp.nop(nofuse=True)
                            sp.dma_start(rows(out, s - 1), y[:, 1 - b]).then_inc(s_out[1 - b].sem, 16)

                    steps(sp, NSTEP, body)
                    sp.wait_ge(s_ev.sem, s_ev.at(NSTEP))
                    sp.dma_start(rows(out, NSTEP - 1), y[:, (NSTEP - 1) % 2]).then_inc(s_out[1].sem, 16)
                    for b in range(2):
                        sp.wait_ge(s_out[b].sem, s_out[b].at(16 * (NSTEP // 2)))

                @block.gpsimd
                def _(pool):
                    def body(s, b, q, first):
                        if first is None:
                            pool.wait_ge(s_ev.sem, s_ev.at(s - 1))
                        cn = count[:, bass.ds(s * K, K)].unsqueeze(2).broadcast_to([P, K, D])
                        pool.tensor_tensor(part[:, b], cn, wide(bm_t), ALU.mult).then_inc(s_pool.sem, 1)

                    steps(pool, NSTEP, body)

                @block.vector
                def _(dve):
                    def body(s, b, q, first):
                        ch = Chain(dve, s_dve, 3, s)
                        for sg in s_in:
                            dve.wait_ge(sg[b].sem, sg[b].at(16 * (q + 1)))
                        dve.tensor_tensor(nf[:, b], nf[:, b], wide(bn_s), ALU.mult)
                        ch.link(dve.tensor_tensor(c[:, b, :, 0:D], c[:, b, :, 0:D], wide(bm_s), ALU.mult))
                        dve.tensor_tensor(x[:, b], x[:, b], wide(bn_t), ALU.add)
                        ch.link(dve.tensor_tensor(nf[:, b], nf[:, b], c[:, b, :, 0:D], ALU.add))
                        ch.link(dve.tensor_tensor(x[:, b], x[:, b], nf[:, b], ALU.add))
                        dve.wait_ge(s_pool.sem, s_pool.at(s + 1))
                        if first is None:
                            dve.wait_ge(s_out[b].sem, s_out[b].at(16 * q))
                        dve.tensor_tensor(y[:, b], x[:, b], part[:, b], ALU.add).then_inc(s_ev.sem, 1)
                        ch.done()

                    steps(dve, NSTEP, body)

    def finish_debug(src, w=None):
        with nc.Block() as block:
            s = signal("store_a")

            @block.sync
            def _(sp):
                sp.dma_start(out, src).then_inc(s.sem, 16)
                sp.wait_ge(s.sem, s.at(16))
        whole.close()

    prepare()
    node_phase("first", "first", [(A["x"], D)], [(t_h0, ROW), (d_y, D)], ROW,
               [(2 * H, None, A["L0_gnn_bias"][0])],
               gat=(A["L0_gnn_W"][0], A["L0_gnn_att_src"][0], A["L0_gnn_att_dst"][0], H, 0, 2 * H))
    if DEBUG == "first":
        return finish_debug(d_y)
    gat_edges("edges0", t_h0, A["L0_gnn_W"][0])
    if DEBUG == "edges0":
        return finish_debug(rows_all(t_agg))

    def psum_pair(ctx, name):
        return [ctx.enter_context(nc.psum_tensor(f"{name}_{k}", [1, HALF * D], F32))[:, :] for k in "ab"]

    for layer in range(2):
        with ExitStack() as ctx:
            held = ctx.enter_context(nc.sbuf_tensor(f"held{layer}", [P, NT, D], F32))
            with ExitStack() as c2:
                sums = psum_pair(c2, f"bn{layer}")
                aggregate_phase(f"agg{layer}", held, layer == 0, sums)
                bn_coefficients(f"bn{layer}", sums[0], sums[1], HALF, N, A["L0_gnn_gamma"][layer],
                                A["L0_gnn_beta"][layer], bn_s, bn_t)
            if layer == 0:
                node_phase("second", "gat", [(t_h0, D)], [(t_x1, ROW), (d_y, D)], ROW,
                           [(2 * H, None, A["L0_gnn_bias"][1])], held=held,
                           gat=(A["L0_gnn_W"][1], A["L0_gnn_att_src"][1], A["L0_gnn_att_dst"][1], H, 0, 2 * H))
            else:
                node_phase("third", "join", [(t_x1, D), (A["x"], D)], [(d_xa, D), (t_g, ROW), (d_r, D)], ROW + D,
                           [(0, A["L1_gnn_W"], None), (ROW, A["L1_gnn_W"], A["L1_gnn_bias"])], held=held,
                           gat=(A["L1_gnn_W"], A["L1_gnn_att_src"], A["L1_gnn_att_dst"], H, D, None))
        if DEBUG == f"nodes{layer}":
            return finish_debug(d_y if layer == 0 else d_r)
        if layer == 0:
            gat_edges("edges1", t_x1, A["L0_gnn_W"][1])
    gat_edges("edges2", t_g, None)
    if DEBUG == "edges2":
        return finish_debug(rows_all(t_agg))
    node_phase("fourth", "layer", [(d_r, D), (t_agg, AGG), (d_xa, D)], [(d_xb, D), (t_c1, D)], D,
               [(0, A["L2_gnn_W1"], None)], gamma=A["L1_gnn_gamma"], beta=A["L1_gnn_beta"])
    if DEBUG == "fourth":
        return finish_debug(d_xb)
    gcn_edges("edges3", t_c1)
    node_phase("fifth", "gcn", [(t_c1, D), (t_agg, AGG)], [(t_c2, D)], D, [(0, A["L2_gnn_W2"], None)],
               bias=A["L2_gnn_b1"])
    if DEBUG == "fifth":
        return finish_debug(t_c2)
    gcn_edges("edges4", t_c2)
    W_msg = A["L3_gnn_W_msg"]
    with ExitStack() as ctx:
        sums = psum_pair(ctx, "bn_nf")
        node_phase("sixth", "last", [(t_c2, D), (t_agg, AGG), (d_xb, D)],
                   [(d_xc, D), (d_nf, D), (t_u, D), (t_v, D)], 3 * D,
                   [(0, A["L3_gnn_W_node"], A["L3_gnn_b_node"]), (D, W_msg[0:D, :], None),
                    (2 * D, W_msg[D:2 * D, :], None)], bias=A["L2_gnn_b2"], sums=sums)
        bn_coefficients("bn_nf", sums[0], sums[1], HALF, N, A["L3_gnn_g_node"], A["L3_gnn_beta_node"], bn_s, bn_t)
    if DEBUG == "sixth":
        return finish_debug(d_nf)
    with ExitStack() as ctx:
        wmsg = ctx.enter_context(nc.sbuf_tensor("wmsg", [AGG, D], F32))
        sums = psum_pair(ctx, "bn_msg")
        edge_mlp("edge_mlp", wmsg)
        message_edges("edges5", wmsg, sums)
        bn_coefficients("bn_msg", sums[0], sums[1], HALF, E, A["L3_gnn_g_msg"], A["L3_gnn_beta_msg"], bm_s, bm_t)
    if DEBUG == "edges5":
        return finish_debug(rows_all(t_agg))
    last_sum("out")
    whole.close()


_INS = ['x', 'src', 'dst', 'edge_attr_4', 'L0_gnn_W', 'L0_gnn_att_src', 'L0_gnn_att_dst', 'L0_gnn_bias',
        'L0_gnn_gamma', 'L0_gnn_beta', 'L1_gnn_W', 'L1_gnn_att_src', 'L1_gnn_att_dst', 'L1_gnn_bias',
        'L1_gnn_gamma', 'L1_gnn_beta', 'L2_gnn_W1', 'L2_gnn_b1', 'L2_gnn_W2', 'L2_gnn_b2', 'L3_gnn_W_node',
        'L3_gnn_b_node', 'L3_gnn_g_node', 'L3_gnn_beta_node', 'L3_gnn_W_edge', 'L3_gnn_b_edge', 'L3_gnn_g_edge',
        'L3_gnn_beta_edge', 'L3_gnn_W_msg', 'L3_gnn_b_msg', 'L3_gnn_g_msg', 'L3_gnn_beta_msg']


def kernel(**inputs):
    import numpy as _np
    import concourse.bacc as _bacc
    from concourse import mybir as _mybir
    from concourse.bass_utils import run_bass_kernel_spmd as _run

    nc = _bacc.Bacc("TRN2", target_bir_lowering=False, num_devices=1)
    arrays, args = {}, {}
    for name in _INS:
        a = _np.ascontiguousarray(inputs[name])
        arrays[f"in_{name}_dram"] = a
        args[name] = nc.dram_tensor(f"in_{name}_dram", a.shape, _mybir.dt.from_np(a.dtype), kind="ExternalInput").ap()
    out = nc.dram_tensor("out_0_dram", (N, D), F32, kind="ExternalOutput").ap()
    build(nc, args, out)
    r = _run(nc, [arrays], core_ids=[0])
    return r.results[0]["out_0_dram"]
```

```python
from contextlib import ExitStack

import concourse.bass as bass
from concourse import mybir

F32 = mybir.dt.float32
I32 = mybir.dt.int32
ALU = mybir.AluOpType
ACT = mybir.ActivationFunctionType
AX = mybir.AxisListType

N = 50000
E = 25000
D = 96
H = 4
DH = D // H
P = 125
NT = N // P
ET = E // P
K = 8
HALF = K // 2
NSTEP = NT // K
ESTEP = ET // K
ROW = D + 2 * H
AGG = D + 1
SPARE = 2 * K * P
BIG = 1.0e30
EPS = 1e-5
SLOPE = 0.2
DEBUG = None


def build(nc, A, out):
    whole = ExitStack()
    signals = {}

    class Signal:

        def __init__(self, name):
            self.sem = whole.enter_context(nc.semaphore(name))
            self.base = 0

        def at(self, count):
            return self.base + count

    def signal(name):
        if name not in signals:
            signals[name] = Signal(name)
        return signals[name]

    class Chain:

        def __init__(self, eng, sig, per, step=0):
            self.eng, self.sig, self.per, self.step, self.k = eng, sig, per, step, 0

        def link(self, ins):
            self.k += 1
            ins.then_inc(self.sig.sem, 1)
            self.eng.wait_ge(self.sig.sem, self.sig.at(self.per * self.step + self.k))

        def done(self):
            assert self.k == self.per, (self.k, self.per)

    def steps(eng, n, body):
        peel = 4 - n % 2
        for s in range(peel):
            body(s, s % 2, s // 2, s if s < 2 else None)
        with eng.Fori(0, (n - peel) // 2) as i:
            body(2 * i + peel, peel % 2, i + peel // 2, None)
            body(2 * i + peel + 1, (peel + 1) % 2, i + (peel + 1) // 2, None)

    class Step:

        def __init__(self, i, c, U):
            self.i, self.c, self.U = i, c, U
            self.b = c % 2
            self.s = c if i is None else U * i + c
            self.q = self.turn(2)

        def turn(self, R):
            return self.c // R if self.i is None else (self.U // R) * self.i + self.c // R

        def after(self, n):
            return self.c >= n

    def pipeline(eng, n, stages, U=2):
        deep = max(lag for lag, _ in stages)
        peel = 4 + deep
        while (n - peel) % U:
            peel += 1
        for c in range(peel):
            for lag, emit in stages:
                if c >= lag:
                    emit(Step(None, c - lag, U))
        with eng.Fori(0, (n - peel) // U) as i:
            for u in range(U):
                for lag, emit in stages:
                    emit(Step(i, peel + u - lag, U))
        for c in range(n, n + deep):
            for lag, emit in stages:
                if c - lag < n:
                    emit(Step(None, c - lag, U))

    def dram(name, shape):
        return nc.dram_tensor(name, shape, F32, kind="Internal").ap()

    t_h0 = dram("t_h0", [N, ROW])
    t_x1 = dram("t_x1", [N, ROW])
    t_g = dram("t_g", [N, ROW])
    d_y = dram("d_y", [N, D])
    d_xa = dram("d_xa", [N, D])
    d_xb = dram("d_xb", [N, D])
    d_xc = dram("d_xc", [N, D])
    d_r = dram("d_r", [N, D])
    t_c1 = dram("t_c1", [N, D])
    t_c2 = dram("t_c2", [N, D])
    t_h3 = dram("t_h3", [N, D])
    d_nf = dram("d_nf", [N, AGG])
    t_agg = dram("t_agg", [N + SPARE, AGG])

    def rows(table, step, w=None):
        v = table[0:N, :].rearrange("(p t) d -> p t d", t=NT)[:, bass.ds(step * K, K), :]
        return v if w is None else v[:, :, 0:w]

    def rows_all(table):
        return table[0:N, 0:D]

    def row1(v):
        return v.rearrange("(a d) -> a d", a=1)

    def sbw(name, shape, dt=F32):
        return whole.enter_context(nc.sbuf_tensor(name, shape, dt))

    ident = sbw("ident", [128, 128])
    ones = sbw("ones", [128, 128])
    ones_row = sbw("ones_row", [1, P])
    src_idx = sbw("src_idx", [P, ET], I32)
    dst_idx = sbw("dst_idx", [P, ET], I32)
    out_idx = sbw("out_idx", [P, ET], I32)
    fix_idx = sbw("fix_idx", [P, 1], I32)
    same_f = sbw("same_f", [P, ET])
    same_b = sbw("same_b", [P, ET])
    pen_f = sbw("pen_f", [P, ET])
    pen_b = sbw("pen_b", [P, ET])
    mask_f = sbw("mask_f", [P, P])
    mask_b = sbw("mask_b", [P, P])
    far_f = sbw("far_f", [P, P])
    far_b = sbw("far_b", [P, P])
    count = sbw("count", [P, NT])
    dinv = sbw("dinv", [P, NT])
    bn_s = sbw("bn_s", [P, D])
    bn_t = sbw("bn_t", [P, D])
    eps_col = sbw("eps_col", [P, 1])

    def prepare():
        with ExitStack() as ctx:
            def sb(name, shape, dt=F32):
                return ctx.enter_context(nc.sbuf_tensor(name, shape, dt))

            dst_f = sb("dst_f", [P, ET])
            next_i = sb("next_i", [P, 1], I32)
            next_f = sb("next_f", [P, 1])
            last = sb("last", [P, ET])
            spare_i = sb("spare_i", [P, (ET + 15) // 16, 2 * K], I32)
            spare = sb("spare", [P, ET])
            diff = sb("diff", [P, ET])
            fixf = sb("fixf", [P, 2])
            tri_f = sb("tri_f", [P, P])
            tri_b = sb("tri_b", [P, P])
            rep = sb("rep", [P, 2, P])
            zero = sb("zero", [P, 2, 26 * AGG])
            turned = ctx.enter_context(nc.psum_tensor("turned", [P, 2, P], F32))
            s_ld, s_pool, s_nx = signal("load_a"), signal("pool_chain"), signal("load_b")
            s_dve, s_pe, s_zero, s_z = signal("dve_chain"), signal("pe_done"), signal("zeroed"), signal("store_a")
            agg_v = t_agg.rearrange("(p t) d -> p (t d)", t=(N + SPARE) // P)
            block = ctx.enter_context(nc.Block())

            @block.sync
            def _(sp):
                sp.dma_start(src_idx[:, :], A["src"].rearrange("(p t) -> p t", t=ET)).then_inc(s_ld.sem, 16)
                sp.dma_start(dst_idx[:, :], A["dst"].rearrange("(p t) -> p t", t=ET)).then_inc(s_ld.sem, 16)
                sp.wait_ge(s_pool.sem, s_pool.at(1))
                sp.dma_start(next_i[0:P - 1, :],
                             A["dst"].rearrange("(p t) -> p t", t=ET)[1:P, 0:1], allow_slow_non_contiguous=True).then_inc(s_nx.sem, 16)
                sp.wait_ge(s_zero.sem, s_zero.at(1))
                for c in range(8):
                    w = 52 * AGG
                    sp.dma_start(agg_v[:, c * w:(c + 1) * w].rearrange("p (a w) -> p a w", a=2),
                                 zero[:, :, :]).then_inc(s_z.sem, 16)
                sp.wait_ge(s_z.sem, s_z.at(128))

            @block.gpsimd
            def _(pool):
                chain = Chain(pool, s_pool, 7)
                chain.link(pool.memset(next_i[:, :], -1))
                chain.link(pool.memset(ident[:, :], 0.0))
                chain.link(pool.affine_select(out=ident[:, :], in_=ident[:, :], compare_op=ALU.not_equal, fill=1.0,
                                              base=0, pattern=[[-1, 128]], channel_multiplier=1))
                chain.link(pool.memset(ones[:, :], 1.0))
                chain.link(pool.affine_select(out=tri_f[:, :], in_=ones[0:P, 0:P], compare_op=ALU.is_gt, fill=0.0,
                                              base=0, pattern=[[1, P]], channel_multiplier=-1))
                chain.link(pool.affine_select(out=tri_b[:, :], in_=ones[0:P, 0:P], compare_op=ALU.is_gt, fill=0.0,
                                              base=0, pattern=[[-1, P]], channel_multiplier=1))
                chain.link(pool.iota(spare_i[:, :, :], pattern=[[0, (ET + 15) // 16], [P, 2 * K]], base=N,
                                     channel_multiplier=1))
                chain.done()

            @block.vector
            def _(dve):
                chain = Chain(dve, s_dve, 18)
                dve.memset(zero[:, :, :], 0.0).then_inc(s_zero.sem, 1)
                dve.memset(eps_col[:, :], EPS)
                dve.memset(ones_row[:, :], 1.0)
                dve.memset(same_f[:, 0:1], 1.0)
                dve.wait_ge(s_ld.sem, s_ld.at(32))
                chain.link(dve.tensor_copy(dst_f[:, :], dst_idx[:, :]))
                dve.wait_ge(s_nx.sem, s_nx.at(16))
                chain.link(dve.tensor_copy(next_f[:, :], next_i[:, :]))
                chain.link(dve.tensor_tensor(same_f[:, 1:ET], dst_f[:, 1:ET], dst_f[:, 0:ET - 1], ALU.is_equal))
                chain.link(dve.memset(same_b[:, ET - 1:ET], 1.0))
                chain.link(dve.tensor_copy(same_b[:, 0:ET - 1], same_f[:, 1:ET]))
                dve.tensor_scalar(pen_f[:, :], same_f[:, :], BIG, -BIG, ALU.mult, ALU.add)
                dve.tensor_scalar(pen_b[:, :], same_b[:, :], BIG, -BIG, ALU.mult, ALU.add)
                dve.tensor_scalar(last[:, 0:ET - 1], same_b[:, 0:ET - 1], -1.0, 1.0, ALU.mult, ALU.add)
                chain.link(dve.tensor_tensor(last[:, ET - 1:ET], dst_f[:, ET - 1:ET], next_f[:, :], ALU.not_equal))
                dve.wait_ge(s_pool.sem, s_pool.at(7))
                chain.link(dve.tensor_copy(spare[:, :],
                                           spare_i[:, :, :].rearrange("p a b -> p (a b)")[:, 0:ET]))
                chain.link(dve.tensor_tensor(diff[:, :], dst_f[:, :], spare[:, :], ALU.subtract))
                dve.tensor_tensor(fixf[:, 0:1], dst_f[:, 0:1], next_f[:, :], ALU.not_equal)
                chain.link(dve.tensor_tensor(last[:, :], last[:, :], diff[:, :], ALU.mult))
                chain.link(dve.tensor_tensor(out_idx[:, :], last[:, :], spare[:, :], ALU.add))
                chain.link(dve.tensor_tensor(fixf[:, 1:2], fixf[:, 0:1], diff[:, 0:1], ALU.mult))
                chain.link(dve.tensor_tensor(fix_idx[:, :], fixf[:, 1:2], spare[:, 0:1], ALU.add))
                chain.link(dve.tensor_scalar(rep[:, 0, :], ones[0:P, 0:P], dst_f[:, 0:1], None, ALU.mult))
                chain.link(dve.tensor_scalar(rep[:, 1, :], ones[0:P, 0:P], dst_f[:, ET - 1:ET], None, ALU.mult))
                dve.wait_ge(s_pe.sem, s_pe.at(1))
                chain.link(dve.scalar_tensor_tensor(mask_f[:, :], turned[:, 0, :], dst_f[:, ET - 1:ET], tri_f[:, :],
                                                    ALU.is_equal, ALU.mult))
                chain.link(dve.scalar_tensor_tensor(mask_b[:, :], turned[:, 1, :], dst_f[:, 0:1], tri_b[:, :],
                                                    ALU.is_equal, ALU.mult))
                chain.link(dve.tensor_scalar(far_f[:, :], mask_b[:, :], BIG, -BIG, ALU.mult, ALU.add))
                chain.link(dve.tensor_scalar(far_b[:, :], mask_f[:, :], BIG, -BIG, ALU.mult, ALU.add))
                chain.done()

            @block.tensor
            def _(pe):
                pe.wait_ge(s_dve.sem, s_dve.at(14))
                pe.wait_ge(s_pool.sem, s_pool.at(3))
                pe.transpose(turned[:, 0, :], rep[:, 0, :], ident[0:P, 0:P])
                pe.transpose(turned[:, 1, :], rep[:, 1, :], ident[0:P, 0:P]).then_inc(s_pe.sem, 1)

        s_ld.base += 32
        s_pool.base += 7
        s_nx.base += 16
        s_dve.base += 18
        s_pe.base += 1
        s_zero.base += 1
        s_z.base += 128

    def norm_stats(dve, link, x, bn, tmp, s_var):
        for k in range(K):
            ins = dve.bn_stats(bn[:, k, :], x[:, k, :])
        link(ins)
        dve.tensor_tensor(tmp[:, 0, :], bn[:, :, 1], bn[:, :, 4], ALU.add)
        dve.tensor_tensor(tmp[:, 2, :], bn[:, :, 2], bn[:, :, 5], ALU.add)
        link(dve.tensor_tensor(tmp[:, 1, :], bn[:, :, 1], bn[:, :, 4], ALU.subtract))
        link(dve.tensor_tensor(tmp[:, 1, :], tmp[:, 1, :], tmp[:, 1, :], ALU.mult))
        dve.scalar_tensor_tensor(tmp[:, 3, :], tmp[:, 1, :], D / 4.0, tmp[:, 2, :],
                                 ALU.mult, ALU.add).then_inc(s_var.sem, 1)

    def norm_scale(dve, link, tmp):
        link(dve.reciprocal(tmp[:, 5, :], tmp[:, 4, :]))
        return dve.scalar_tensor_tensor(tmp[:, 6, :], tmp[:, 0, :], -0.5, tmp[:, 5, :], ALU.mult, ALU.mult)

    def bn_coefficients(name, gram, n, gamma, beta, scale, shift):
        with ExitStack() as ctx:
            diag = ctx.enter_context(nc.sbuf_tensor(f"{name}_diag", [D, D], F32))
            col = ctx.enter_context(nc.sbuf_tensor(f"{name}_col", [D, 10], F32))
            rep = ctx.enter_context(nc.sbuf_tensor(f"{name}_rep", [D, 2, P], F32))
            wide = ctx.enter_context(nc.psum_tensor(f"{name}_wide", [P, 2, D], F32))
            s_ld, s_dve = signal("load_a0"), signal("dve_chain")
            s_var, s_dev, s_pe = signal("var_ready"), signal("dev_ready"), signal("pe_done")
            block = ctx.enter_context(nc.Block())

            @block.sync
            def _(sp):
                for k, v in enumerate((gamma, beta)):
                    sp.dma_start(col[:, k:k + 1], v.rearrange("(d a) -> d a", a=1),
                                 allow_slow_non_contiguous=True).then_inc(s_ld.sem, 16)

            @block.vector
            def _(dve):
                c = Chain(dve, s_dve, 12)
                c.link(dve.tensor_tensor(diag[:, :], gram[:, 0:D], ident[0:D, 0:D], ALU.mult))
                c.link(dve.tensor_reduce(col[:, 3:4], diag[:, :], AX.X, ALU.add))
                dve.tensor_scalar(col[:, 2:3], gram[:, D:AGG], 1.0 / n, None, ALU.mult)
                c.link(dve.tensor_scalar(col[:, 3:4], col[:, 3:4], 1.0 / n, None, ALU.mult))
                c.link(dve.tensor_tensor(col[:, 4:5], col[:, 2:3], col[:, 2:3], ALU.mult))
                dve.tensor_tensor(col[:, 5:6], col[:, 3:4], col[:, 4:5], ALU.subtract).then_inc(s_var.sem, 1)
                dve.wait_ge(s_dev.sem, s_dev.at(1))
                c.link(dve.reciprocal(col[:, 6:7], col[:, 5:6]))
                dve.wait_ge(s_ld.sem, s_ld.at(32))
                c.link(dve.tensor_tensor(col[:, 7:8], col[:, 6:7], col[:, 0:1], ALU.mult))
                c.link(dve.tensor_tensor(col[:, 8:9], col[:, 2:3], col[:, 7:8], ALU.mult))
                c.link(dve.tensor_tensor(col[:, 9:10], col[:, 1:2], col[:, 8:9], ALU.subtract))
                c.link(dve.tensor_scalar(rep[:, 0, :], ones[0:D, 0:P], col[:, 7:8], None, ALU.mult))
                c.link(dve.tensor_scalar(rep[:, 1, :], ones[0:D, 0:P], col[:, 9:10], None, ALU.mult))
                dve.wait_ge(s_pe.sem, s_pe.at(1))
                c.link(dve.tensor_copy(scale[:, :], wide[:, 0, :]))
                c.link(dve.tensor_copy(shift[:, :], wide[:, 1, :]))
                c.done()

            @block.scalar
            def _(act):
                act.wait_ge(s_var.sem, s_var.at(1))
                nc.scalar.activation(col[:, 5:6], col[:, 5:6], ACT.Sqrt, bias=eps_col[0:D, :]).then_inc(s_dev.sem, 1)

            @block.tensor
            def _(pe):
                pe.wait_ge(s_dve.sem, s_dve.at(10))
                pe.transpose(wide[:, 0, :], rep[:, 0, :], ident[0:D, 0:D])
                pe.transpose(wide[:, 1, :], rep[:, 1, :], ident[0:D, 0:D]).then_inc(s_pe.sem, 1)

        s_ld.base += 32
        s_dve.base += 12
        s_var.base += 1
        s_dev.base += 1
        s_pe.base += 1

    def gat_weights(name, wide, W, a_src, a_dst, heads, at_a, at_mean):
        width = W.shape[1]
        dh = width // heads
        with ExitStack() as ctx:
            w = ctx.enter_context(nc.sbuf_tensor(f"{name}_w", [D, heads, dh], F32))
            a = ctx.enter_context(nc.sbuf_tensor(f"{name}_a", [D, 2, heads, dh], F32))
            part = ctx.enter_context(nc.sbuf_tensor(f"{name}_part", [D, heads, dh], F32))
            s_ld, s_dve = signal("load_a0"), signal("dve_chain")
            block = ctx.enter_context(nc.Block())
            n_link = 4 + (2 if at_mean is not None else 0)

            @block.sync
            def _(sp):
                sp.dma_start(w[:, :, :], W.rearrange("c (h d) -> c h d", h=heads)).then_inc(s_ld.sem, 16)
                sp.dma_start(a[:, 0, :, :], a_src.partition_broadcast(D)).then_inc(s_ld.sem, 16)
                sp.dma_start(a[:, 1, :, :], a_dst.partition_broadcast(D)).then_inc(s_ld.sem, 16)

            @block.vector
            def _(dve):
                chain = Chain(dve, s_dve, n_link)
                dve.wait_ge(s_ld.sem, s_ld.at(48))
                for j in range(2):
                    chain.link(dve.tensor_tensor(part[:, :, :], w[:, :, :], a[:, j, :, :], ALU.mult))
                    chain.link(dve.tensor_reduce(wide[0:D, at_a + j * H:at_a + j * H + H], part[:, :, :], AX.X,
                                                 ALU.add))
                if at_mean is not None:
                    chain.link(dve.tensor_reduce(part[:, 0, :], w[:, :, :].rearrange("c h d -> c d h"), AX.X,
                                                 ALU.add))
                    chain.link(dve.tensor_scalar(wide[0:D, at_mean:at_mean + D], part[:, 0, :], 1.0 / heads, None,
                                                 ALU.mult))
                chain.done()

        s_ld.base += 48
        s_dve.base += n_link

    def node_phase(name, kind, loads, stores, width, weights, gat=None, held=None, bias=None, gamma=None,
                   beta=None, gram=None):
        own_rows = kind in ("first", "gat")
        L = 2 if kind == "layer" else 0
        N1 = L + 1 if kind not in ("gat", "gcn") else L
        U = 4
        deep = 2 if held is not None else 4
        normed = kind != "gat" and kind != "gcn"
        row_w = ROW if own_rows else D
        fronts = {"first": 0, "gat": 0, "join": 1, "layer": 1, "gcn": 0, "last": 2}[kind]
        W3 = [P, K, D]
        with ExitStack() as ctx:
            def sb(nm, shape, dt=F32):
                return ctx.enter_context(nc.sbuf_tensor(f"{name}_{nm}", shape, dt))

            ins = [sb(f"in{j}", [P, deep, K, w]) for j, (_, w) in enumerate(loads)]
            R_h = 2 if kind == "join" else 4
            h = sb("h", [P, R_h, K, row_w])
            h_out = {"first": 0, "gat": 0, "last": 1}.get(kind)
            rings = [R_h if j == h_out else deep if j == 0 and fronts else 2 for j in range(len(stores))]
            outs = [h if j == h_out else sb(f"out{j}", [P, rings[j], K, w]) for j, (_, w) in enumerate(stores)]
            R_hT = 1 if kind == "join" else 2
            hT = sb("hT", [D + 1, R_hT, 2, HALF * P])
            wide = sb("wide", [D + 1, width])
            if normed:
                bn = sb("bn", [P, K, 6])
                tmp = sb("tmp", [P, 4, 2 if kind == "layer" else 1, 7, K])
            if gamma is not None:
                gam, bet = sb("gam", [P, D]), sb("bet", [P, D])
            if bias is not None:
                bia = sb("bia", [P, D])
            if kind in ("layer", "gcn", "last"):
                mid = sb("mid", [P, 4, K, D])
            if kind == "last":
                zeros = sb("zeros", [P, AGG])
            pT = ctx.enter_context(nc.psum_tensor(f"{name}_pT", [D, 2, 512], F32))
            pO = ctx.enter_context(nc.psum_tensor(f"{name}_pO", [P, 2, K, 128], F32))

            s_in = [[signal(f"load_{c}{r}") for r in range(deep)] for c in "abc"[:len(loads)]]
            s_out = [[signal(f"store_{c}{r}") for r in range(rings[j])] for j, c in enumerate("abc"[:len(stores)])]
            s_w, s_set, s_front, s_pool = signal("weights"), signal("setup"), signal("front"), signal("pool_ready")
            s_var, s_dev, s_scale = signal("var_ready"), signal("dev_ready"), signal("scale_ready")
            s_var0, s_dev0, s_scale0 = signal("var0_ready"), signal("dev0_ready"), signal("scale0_ready")
            s_norm, s_h, s_tr, s_hT = signal("normed"), signal("h_ready"), signal("turned"), signal("hT_ready")
            s_mm, s_ev, s_ev2 = signal("product_ready"), signal("product_used"), signal("product_used2")
            s_dve, s_dve0, s_pc = signal("dve_chain"), signal("dve_chain0"), signal("pool_chain")
            s_hb, s_gram = signal("h_bias"), signal("summed")
            s_dves, s_dves0 = signal("scale_chain"), signal("scale_chain0")
            used = {"first": s_h, "gat": s_h, "join": s_front, "layer": s_front, "gcn": s_pool, "last": s_front}[kind]

            n_w = sum((m is not None) + (v is not None) for _, m, v in weights) \
                + 2 * (gamma is not None) + (bias is not None)
            with nc.Block() as setup:
                @setup.sync
                def _(sp):
                    sp.wait_ge(s_set.sem, s_set.at(1))
                    for at, m, v in weights:
                        if m is not None:
                            sp.dma_start(wide[0:D, at:at + D], m).then_inc(s_w.sem, 16)
                        if v is not None:
                            sp.dma_start(wide[D:D + 1, at:at + D], row1(v)).then_inc(s_w.sem, 16)
                    if gamma is not None:
                        sp.dma_start(gam[:, :], gamma.partition_broadcast(P)).then_inc(s_w.sem, 16)
                        sp.dma_start(bet[:, :], beta.partition_broadcast(P)).then_inc(s_w.sem, 16)
                    if bias is not None:
                        sp.dma_start(bia[:, :], bias.partition_broadcast(P)).then_inc(s_w.sem, 16)
                    if n_w:
                        sp.wait_ge(s_w.sem, s_w.at(16 * n_w))

                @setup.vector
                def _(dve):
                    dve.memset(hT[:, :, :, :], 1.0)
                    if kind == "last":
                        dve.memset(outs[2][:, :, :, :], 1.0)
                        dve.memset(zeros[:, :], 0.0)
                    dve.memset(wide[:, :], 0.0).then_inc(s_set.sem, 1)
            s_set.base += 1
            s_w.base += 16 * n_w
            if gat is not None:
                gat_weights(name, wide, *gat)

            x_in = [t[:, :, :, 0:D] for t in ins]
            block = ctx.enter_context(nc.Block())

            def over(v):
                return v[:, :].unsqueeze(1).broadcast_to(W3)

            def dinv_of(t):
                return dinv[:, bass.ds(t.s * K, K)].unsqueeze(2).broadcast_to(W3)

            def buf_in(j, t):
                return x_in[j][:, t.c % deep]

            def buf_out(j, t):
                return outs[j][:, t.c % rings[j]]

            def buf_h(t):
                return h[:, t.c % R_h]

            def arrived(eng, t, which):
                for j in which:
                    sg = s_in[j][t.c % deep]
                    eng.wait_ge(sg.sem, sg.at(16 * (t.turn(deep) + 1)))

            def stored(eng, t, j):
                R = rings[j]
                if t.after(R):
                    eng.wait_ge(s_out[j][t.c % R].sem, s_out[j][t.c % R].at(16 * t.turn(R)))

            @block.sync
            def _(sp):
                def load(t):
                    if t.after(deep):
                        sp.wait_ge(used.sem, used.at(t.s - deep + 1))
                        sp.nop(nofuse=True)
                    for (table, w), buf, sg in zip(loads, ins, s_in):
                        sp.dma_start(buf[:, t.c % deep, :, :],
                                     rows(table, t.s, w)).then_inc(sg[t.c % deep].sem, 16)

                def store_front(t):
                    sp.wait_ge(s_front.sem, s_front.at(t.s + 1))
                    sp.nop(nofuse=True)
                    sp.dma_start(rows(stores[0][0], t.s), buf_out(0, t)).then_inc(s_out[0][t.c % rings[0]].sem, 16)

                def store_h(t):
                    if kind == "last":
                        sp.wait_ge(s_h.sem, s_h.at(t.s + 1))
                        sp.nop(nofuse=True)
                        sp.dma_start(rows(stores[1][0], t.s), buf_h(t)).then_inc(s_out[1][t.c % R_h].sem, 16)

                def store_back(t):
                    if kind != "last":
                        sp.wait_ge(s_ev.sem, s_ev.at(t.s + 1))
                        sp.nop(nofuse=True)
                    if kind in ("join", "last"):
                        sp.wait_ge(s_ev2.sem, s_ev2.at(t.s + 1))
                        sp.nop(nofuse=True)
                    for j in range(fronts, len(stores)):
                        sp.dma_start(rows(stores[j][0], t.s), buf_out(j, t)).then_inc(s_out[j][t.c % rings[j]].sem, 16)

                stages = [(0, load)] + ([(L + 1, store_front)] if fronts else []) \
                    + ([(N1 + 1, store_h)] if kind == "last" else []) + [(N1 + 4, store_back)]
                pipeline(sp, NSTEP, stages, U)
                for sg in s_out:
                    for r, x in enumerate(sg):
                        sp.wait_ge(x.sem, x.at(16 * len(range(r, NSTEP, len(sg)))))

            @block.vector
            def _(dve):
                def stream_free(t):
                    stored(dve, t, 0)
                    if t.after(rings[0]):
                        dve.wait_ge(s_h.sem, s_h.at(t.s - rings[0] + 1))

                def front(t):
                    if kind == "first":
                        arrived(dve, t, (0,))
                        norm_stats(dve, Chain(dve, s_dve, 3, t.s).link, buf_in(0, t), bn, tmp[:, t.c % 4, 0], s_var)
                    if kind == "gat":
                        arrived(dve, t, (0,))
                        dve.wait_ge(s_pool.sem, s_pool.at(t.s + 1))
                        stored(dve, t, 0)
                        dve.scalar_tensor_tensor(buf_h(t)[:, :, 0:D], held[:, bass.ds(t.s * K, K), :], 0.0,
                                                 buf_in(0, t), ALU.max, ALU.add).then_inc(s_h.sem, 1)
                    if kind == "join":
                        c = Chain(dve, s_dve, 4, t.s)
                        arrived(dve, t, (0, 1))
                        dve.wait_ge(s_pool.sem, s_pool.at(t.s + 1))
                        o = held[:, bass.ds(t.s * K, K), :]
                        c.link(dve.scalar_tensor_tensor(o, o, 0.0, buf_in(0, t), ALU.max, ALU.add))
                        stream_free(t)
                        dve.tensor_tensor(buf_out(0, t), o, buf_in(1, t), ALU.add).then_inc(s_front.sem, 1)
                        dve.wait_ge(s_front.sem, s_front.at(t.s + 1))
                        norm_stats(dve, c.link, buf_out(0, t), bn, tmp[:, t.c % 4, 0], s_var)
                    if kind == "gcn":
                        dve.wait_ge(s_pool.sem, s_pool.at(t.s + 1))
                        dve.tensor_tensor(buf_h(t), mid[:, t.c % 4], over(bia), ALU.add).then_inc(s_front.sem, 1)
                    if kind == "last":
                        c = Chain(dve, s_dve, 4, t.s)
                        dve.wait_ge(s_pool.sem, s_pool.at(t.s + 1))
                        c.link(dve.tensor_tensor(mid[:, t.c % 4], mid[:, t.c % 4], over(bia), ALU.add))
                        arrived(dve, t, (2,))
                        stream_free(t)
                        dve.scalar_tensor_tensor(buf_out(0, t), mid[:, t.c % 4], 0.0, buf_in(2, t), ALU.max,
                                                 ALU.add).then_inc(s_front.sem, 1)
                        dve.wait_ge(s_front.sem, s_front.at(t.s + 1))
                        norm_stats(dve, c.link, buf_out(0, t), bn, tmp[:, t.c % 4, 0], s_var)
                    if kind == "layer":
                        c = Chain(dve, s_dve, 5, t.s)
                        dve.wait_ge(s_norm.sem, s_norm.at(t.s + 1))
                        c.link(dve.tensor_tensor(mid[:, t.c % 4], mid[:, t.c % 4], over(gam), ALU.mult))
                        c.link(dve.tensor_tensor(mid[:, t.c % 4], mid[:, t.c % 4], over(bet), ALU.add))
                        arrived(dve, t, (2,))
                        stream_free(t)
                        dve.scalar_tensor_tensor(buf_out(0, t), mid[:, t.c % 4], 0.0, buf_in(2, t), ALU.max,
                                                 ALU.add).then_inc(s_front.sem, 1)
                        dve.wait_ge(s_front.sem, s_front.at(t.s + 1))
                        norm_stats(dve, c.link, buf_out(0, t), bn, tmp[:, t.c % 4, 1], s_var)

                def scale(t):
                    c = Chain(dve, s_dves, 1, t.s)
                    dve.wait_ge(s_dev.sem, s_dev.at(t.s + 1))
                    norm_scale(dve, c.link, tmp[:, t.c % 4, min(L, 1)]).then_inc(s_scale.sem, 1)

                def inner_norm(t):
                    c = Chain(dve, s_dve0, 3, t.s)
                    dve.wait_ge(s_pool.sem, s_pool.at(t.s + 1))
                    norm_stats(dve, c.link, mid[:, t.c % 4], bn, tmp[:, t.c % 4, 0], s_var0)

                def inner_scale(t):
                    c = Chain(dve, s_dves0, 1, t.s)
                    dve.wait_ge(s_dev0.sem, s_dev0.at(t.s + 1))
                    norm_scale(dve, c.link, tmp[:, t.c % 4, 0]).then_inc(s_scale0.sem, 1)

                def back(t):
                    ps = pO[:, t.b, :, :]
                    dve.wait_ge(s_mm.sem, s_mm.at(t.s + 1))
                    if own_rows:
                        dve.tensor_copy(buf_h(t)[:, :, D:ROW], ps[:, :, 0:2 * H])
                        stored(dve, t, 1)
                        dve.tensor_copy(buf_out(1, t), ps[:, :, 2 * H:ROW]).then_inc(s_ev.sem, 1)
                    if kind == "join":
                        dve.wait_ge(s_hb.sem, s_hb.at(t.s + 1))
                        dve.tensor_tensor(buf_out(2, t), ps[:, :, 0:D], buf_out(2, t), ALU.add)\
                            .then_inc(s_ev.sem, 1)
                    if kind in ("layer", "gcn"):
                        stored(dve, t, fronts)
                        dve.tensor_tensor(buf_out(fronts, t), ps[:, :, 0:D], dinv_of(t), ALU.mult)\
                            .then_inc(s_ev.sem, 1)

                stages = ([(0, inner_norm), (1, inner_scale)] if kind == "layer" else []) + [(L, front)] \
                    + ([(N1, scale)] if normed else []) + ([(N1 + 2, back)] if kind != "last" else [])
                pipeline(dve, NSTEP, stages, U)

            @block.scalar
            def _(act):
                def root(t, j, var, dev):
                    act.wait_ge(var.sem, var.at(t.s + 1))
                    nc.scalar.activation(tmp[:, t.c % 4, j, 4, :], tmp[:, t.c % 4, j, 3, :], ACT.Sqrt, scale=1.0 / D,
                                         bias=eps_col[:, :]).then_inc(dev.sem, 1)

                def apply(t, j, x, y, func, ready, done):
                    act.wait_ge(ready.sem, ready.at(t.s + 1))
                    for k in range(K):
                        last = nc.scalar.activation(y[:, k, 0:D], x[:, k, 0:D], func,
                                                    scale=tmp[:, t.c % 4, j, 5, k:k + 1], bias=tmp[:, t.c % 4, j, 6, k:k + 1])
                    last.then_inc(done.sem, 1)

                def root_last(t):
                    root(t, min(L, 1), s_var, s_dev)

                def norm_last(t):
                    if h_out is not None:
                        stored(act, t, h_out)
                    if kind == "join" and t.after(2):
                        act.wait_ge(s_hb.sem, s_hb.at(t.s - 1))
                    apply(t, min(L, 1), (buf_in(0, t) if kind == "first" else buf_out(0, t)), buf_h(t), ACT.Relu, s_scale, s_h)

                def root_inner(t):
                    root(t, 0, s_var0, s_dev0)

                def norm_inner(t):
                    apply(t, 0, mid[:, t.c % 4], mid[:, t.c % 4], ACT.Identity, s_scale0, s_norm)

                def relu(t):
                    act.wait_ge(s_front.sem, s_front.at(t.s + 1))
                    nc.scalar.activation(buf_h(t), buf_h(t), ACT.Relu).then_inc(s_h.sem, 1)

                def evacuate(t):
                    act.wait_ge(s_tr.sem, s_tr.at(t.s + 1))
                    if t.after(R_hT):
                        act.wait_ge(s_mm.sem, s_mm.at(t.s + 1 - R_hT))
                    nc.scalar.copy(hT[0:D, t.c % R_hT, :, :], pT[:, :, 0:HALF * P]).then_inc(s_hT.sem, 1)

                def back(t):
                    if kind == "join":
                        stored(act, t, 1)
                        act.wait_ge(s_ev.sem, s_ev.at(t.s + 1))
                        nc.scalar.copy(buf_out(1, t), pO[:, t.b, :, 0:ROW]).then_inc(s_ev2.sem, 1)
                    else:
                        stored(act, t, 2)
                        if t.after(2):
                            act.wait_ge(s_gram.sem, s_gram.at(t.s - 1))
                        act.wait_ge(s_mm.sem, s_mm.at(t.s + 1))
                        nc.scalar.activation(buf_out(2, t)[:, :, 0:D], pO[:, t.b, :, 0:D], ACT.Relu)\
                            .then_inc(s_ev2.sem, 1)

                stages = {
                    "first": [(1, norm_last), (2, evacuate), (0, root_last)],
                    "gat": [(1, evacuate)],
                    "join": [(1, norm_last), (2, evacuate), (0, root_last), (3, back)],
                    "layer": [(1, norm_inner), (3, norm_last), (4, evacuate), (0, root_inner), (2, root_last)],
                    "gcn": [(0, relu), (1, evacuate)],
                    "last": [(1, norm_last), (2, evacuate), (0, root_last), (3, back)],
                }[kind]
                pipeline(act, NSTEP, stages, U)

            @block.tensor
            def _(pe):
                def turn(t):
                    pe.wait_ge(s_h.sem, s_h.at(t.s + 1))
                    if t.after(1):
                        pe.wait_ge(s_hT.sem, s_hT.at(t.s))
                    for k in range(K):
                        last = pe.transpose(pT[:, k // HALF, (k % HALF) * P:(k % HALF + 1) * P],
                                            buf_h(t)[:, k, 0:D], ident[0:P, 0:P])
                    last.then_inc(s_tr.sem, 1)

                def product(t):
                    pe.wait_ge(s_hT.sem, s_hT.at(t.s + 1))
                    if t.after(2):
                        if kind != "last":
                            pe.wait_ge(s_ev.sem, s_ev.at(t.s - 1))
                        if kind in ("join", "last"):
                            pe.wait_ge(s_ev2.sem, s_ev2.at(t.s - 1))
                    for k in range(K):
                        last = pe.matmul(pO[:, t.b, k, 0:width], hT[:, t.c % R_hT, k // HALF, (k % HALF) * P:(k % HALF + 1) * P],
                                         wide[:, :], start=True, stop=True)
                    last.then_inc(s_mm.sem, 1)

                def sums_of(t):
                    pe.wait_ge(s_ev2.sem, s_ev2.at(t.s + 1))
                    gram_step(pe, gram, buf_out(2, t)).then_inc(s_gram.sem, 1)

                if kind == "last":
                    gram_edge(pe, gram, zeros, True)
                pipeline(pe, NSTEP, [(N1, turn), (N1 + 1, product)] + ([(4, sums_of)] if kind == "last" else []), U)
                if kind == "last":
                    gram_edge(pe, gram, zeros, False)

            if kind in ("join", "gat", "layer", "gcn", "last"):
                @block.gpsimd
                def _(pool):
                    def batch_norm(t):
                        c = Chain(pool, s_pc, 1, t.s)
                        o = held[:, bass.ds(t.s * K, K), :]
                        c.link(pool.tensor_tensor(o, o, over(bn_s), ALU.mult))
                        pool.nop(nofuse=True)
                        pool.tensor_tensor(o, o, over(bn_t), ALU.add).then_inc(s_pool.sem, 1)

                    def add_bias(t):
                        pool.wait_ge(s_h.sem, s_h.at(t.s + 1))
                        stored(pool, t, 2)
                        pool.tensor_tensor(buf_out(2, t), buf_h(t), over(bia), ALU.add).then_inc(s_hb.sem, 1)

                    def add_aggregate(t):
                        arrived(pool, t, (0, 1))
                        if t.after(4):
                            pool.wait_ge(s_front.sem, s_front.at(t.s - 3))
                        ins_ = pool.tensor_tensor(mid[:, t.c % 4], buf_in(0, t), buf_in(1, t), ALU.add)
                        if kind == "layer":
                            ins_.then_inc(s_pool.sem, 1)
                        else:
                            Chain(pool, s_pc, 1, t.s).link(ins_)
                            pool.nop(nofuse=True)
                            pool.tensor_tensor(mid[:, t.c % 4], mid[:, t.c % 4], dinv_of(t), ALU.mult)\
                                .then_inc(s_pool.sem, 1)

                    pipeline(pool, NSTEP, {"gat": [(0, batch_norm)], "join": [(0, batch_norm), (2, add_bias)]}
                             .get(kind, [(0, add_aggregate)]), U)

        for sg in s_in + s_out:
            for r, x in enumerate(sg):
                x.base += 16 * len(range(r, NSTEP, len(sg)))
        once = [s_tr, s_hT, s_mm, s_h]
        if normed:
            once += [s_var, s_dev, s_scale, s_dves]
            s_dve.base += {"first": 3, "join": 4, "layer": 5, "last": 4}[kind] * NSTEP
        if kind != "last":
            once += [s_ev]
        if kind in ("join", "last"):
            once += [s_ev2]
        if kind not in ("first", "gat"):
            once += [s_front]
        if kind != "first":
            once += [s_pool]
        if kind not in ("first", "layer"):
            once += [s_pc]
        if kind == "join":
            once += [s_hb]
        if kind == "last":
            once += [s_gram]
        if kind == "layer":
            once += [s_var0, s_dev0, s_scale0, s_norm, s_dves0]
            s_dve0.base += 3 * NSTEP
        for x in once:
            x.base += NSTEP

    def gram_step(pe, gram, x):
        for k in range(K):
            last = pe.matmul(gram, x[:, k, 0:D], x[:, k, 0:AGG], start=False, stop=False)
        return last

    def gram_edge(pe, gram, zeros, start):
        pe.matmul(gram, zeros[:, 0:D], zeros[:, :], start=start, stop=not start)

    def aggregate_phase(name, held, with_count, gram):
        with ExitStack() as ctx:
            c = ctx.enter_context(nc.sbuf_tensor(f"{name}_c", [P, 4, K, AGG], F32))
            zeros = ctx.enter_context(nc.sbuf_tensor(f"{name}_zeros", [P, AGG], F32))
            s_y = [signal(f"store_a{b}") for b in range(4)]
            s_c = [signal(f"store_b{b}") for b in range(4)]
            s_h, s_st, s_z, s_cp = signal("h_ready"), signal("summed"), signal("setup"), signal("pool_ready")
            s_dve, s_root, s_one = signal("dve_chain"), signal("dev_ready"), signal("front")
            block = ctx.enter_context(nc.Block())

            @block.sync
            def _(sp):
                def load(t):
                    if t.after(4):
                        sp.wait_ge(s_cp.sem, s_cp.at(t.s - 3))
                        sp.nop(nofuse=True)
                        sp.wait_ge(s_st.sem, s_st.at(t.s - 3))
                        sp.nop(nofuse=True)
                    sp.dma_start(held[:, bass.ds(t.s * K, K), :], rows(d_y, t.s)).then_inc(s_y[t.c % 4].sem, 16)
                    sp.dma_start(c[:, t.c % 4], rows(t_agg, t.s)).then_inc(s_c[t.c % 4].sem, 16)

                pipeline(sp, NSTEP, [(0, load)], 4)

            @block.vector
            def _(dve):
                dve.memset(zeros[:, :], 0.0).then_inc(s_z.sem, 1)

                def add(t):
                    dve.wait_ge(s_y[t.c % 4].sem, s_y[t.c % 4].at(16 * (t.turn(4) + 1)))
                    dve.wait_ge(s_c[t.c % 4].sem, s_c[t.c % 4].at(16 * (t.turn(4) + 1)))
                    if with_count:
                        dve.tensor_copy(count[:, bass.ds(t.s * K, K)], c[:, t.c % 4, :, D]).then_inc(s_dve.sem, 1)
                        dve.wait_ge(s_dve.sem, s_dve.at(t.s + 1))
                    dve.memset(c[:, t.c % 4, :, D], 1.0)
                    dve.tensor_tensor(c[:, t.c % 4, :, 0:D], c[:, t.c % 4, :, 0:D], held[:, bass.ds(t.s * K, K), :],
                                      ALU.add).then_inc(s_h.sem, 1)

                pipeline(dve, NSTEP, [(0, add)], 4)
                if with_count:
                    dve.tensor_scalar(dinv[:, :], count[:, :], 1.0, None, ALU.add).then_inc(s_one.sem, 1)
                    dve.wait_ge(s_root.sem, s_root.at(1))
                    dve.reciprocal(dinv[:, :], dinv[:, :])

            @block.scalar
            def _(act):
                def keep(t):
                    act.wait_ge(s_h.sem, s_h.at(t.s + 1))
                    nc.scalar.copy(held[:, bass.ds(t.s * K, K), :], c[:, t.c % 4, :, 0:D]).then_inc(s_cp.sem, 1)

                pipeline(act, NSTEP, [(0, keep)], 4)
                if with_count:
                    act.wait_ge(s_one.sem, s_one.at(1))
                    nc.scalar.activation(dinv[:, :], dinv[:, :], ACT.Sqrt).then_inc(s_root.sem, 1)

            @block.tensor
            def _(pe):
                pe.wait_ge(s_z.sem, s_z.at(1))
                gram_edge(pe, gram, zeros, True)

                def add_up(t):
                    pe.wait_ge(s_h.sem, s_h.at(t.s + 1))
                    gram_step(pe, gram, c[:, t.c % 4]).then_inc(s_st.sem, 1)

                pipeline(pe, NSTEP, [(0, add_up)], 4)
                gram_edge(pe, gram, zeros, False)

        for sg in s_y, s_c:
            for r, x in enumerate(sg):
                x.base += 16 * len(range(r, NSTEP, 4))
        s_z.base += 1
        for x in (s_h, s_st, s_cp):
            x.base += NSTEP
        if with_count:
            s_root.base += 1
            s_one.base += 1
            s_dve.base += NSTEP

    GATHER = bass.IndirectOffsetOnAxis

    def gather_step(pool, chain, s, parts):
        for idx, ring_idx, _, _, _, _ in parts:
            ins = pool.tensor_copy(ring_idx, idx[:, bass.ds(s * K, K)])
            chain.k += 1
            ins.then_inc(chain.sig.sem, 1)
        pool.wait_ge(chain.sig.sem, chain.sig.at(chain.per * s + chain.k))
        pool.nop(nofuse=True)
        for _, ring_idx, table, ring, w, sig in parts:
            for k in range(K):
                pool.indirect_dma_start(out=ring[:, k, 0:w], out_offset=None, in_=table,
                                        in_offset=GATHER(ap=ring_idx[:, k:k + 1], axis=0)).then_inc(sig.sem, 16)

    def scatter_step(pool, chain, ring_idx, sums, sig, step):
        chain.link(pool.tensor_copy(ring_idx, out_idx[:, bass.ds(step * K, K)]))
        pool.nop(nofuse=True)
        for k in range(K):
            pool.indirect_dma_start(out=t_agg, out_offset=GATHER(ap=ring_idx[:, k:k + 1], axis=0),
                                    in_=sums[:, k, :], in_offset=None).then_inc(sig.sem, 16)

    def run_sums(dve, chain, s, b, ks, sums, same, msg, s_m):
        for k in ks:
            prev = sums[:, b, k - 1, :] if k else sums[:, 1 - b, K - 1, :]
            ins = dve.scalar_tensor_tensor(sums[:, b, k, :], prev, same[:, b, k:k + 1], msg[:, k, :],
                                           ALU.mult, ALU.add)
            if k < K - 1:
                chain.link(ins)
            else:
                ins.then_inc(s_m.sem, 1)
                dve.wait_ge(s_m.sem, s_m.at(s + 1))

    def close_segments(name, tail):
        with ExitStack() as ctx:
            carry = ctx.enter_context(nc.sbuf_tensor(f"{name}_before", [P, AGG], F32))
            row = ctx.enter_context(nc.sbuf_tensor(f"{name}_row", [P, 2, AGG], F32))
            pc = ctx.enter_context(nc.psum_tensor(f"{name}_pc", [P, AGG], F32))
            s_pe, s_dve, s_g, s_s = signal("pe_done"), signal("dve_chain"), signal("gather_a0"), signal("scatter_0")
            block = ctx.enter_context(nc.Block())

            @block.tensor
            def _(pe):
                pe.matmul(pc[:, :], mask_f[:, :], tail, start=True, stop=True).then_inc(s_pe.sem, 1)

            @block.vector
            def _(dve):
                dve.wait_ge(s_pe.sem, s_pe.at(1))
                dve.tensor_copy(carry[:, :], pc[:, :]).then_inc(s_dve.sem, 1)
                dve.wait_ge(s_g.sem, s_g.at(16))
                dve.wait_ge(s_dve.sem, s_dve.at(1))
                dve.tensor_tensor(row[:, 1, :], row[:, 0, :], carry[:, :], ALU.add).then_inc(s_dve.sem, 1)

            @block.gpsimd
            def _(pool):
                pool.indirect_dma_start(out=row[:, 0, :], out_offset=None, in_=t_agg,
                                        in_offset=GATHER(ap=fix_idx[:, :], axis=0)).then_inc(s_g.sem, 16)
                pool.wait_ge(s_dve.sem, s_dve.at(2))
                pool.nop(nofuse=True)
                pool.indirect_dma_start(out=t_agg, out_offset=GATHER(ap=fix_idx[:, :], axis=0), in_=row[:, 1, :],
                                        in_offset=None).then_inc(s_s.sem, 16)
                pool.wait_ge(s_s.sem, s_s.at(16))

        s_pe.base += 1
        s_dve.base += 2
        s_g.base += 16
        s_s.base += 16

    def softmax(name, e, e_self, alpha, factor):
        with ExitStack() as ctx:
            def sb(nm, shape):
                return ctx.enter_context(nc.sbuf_tensor(f"{name}_{nm}", shape, F32))

            fw, bw, den = sb("fw", [P, H, ET]), sb("bw", [P, H, ET]), sb("den", [P, H, ET])
            rep, cand = sb("rep", [P, 2, H, P]), sb("cand", [P, 2, H, P])
            ends, carry = sb("ends", [P, 2, H]), sb("carry", [P, 2, H])
            turned = ctx.enter_context(nc.psum_tensor(f"{name}_turned", [P, 2, 512], F32))
            summed = ctx.enter_context(nc.psum_tensor(f"{name}_summed", [P, 2, H], F32))
            s_dve, s_pe, s_exp = signal("dve_chain"), signal("pe_done"), signal("act_done")
            n_link = 18
            block = ctx.enter_context(nc.Block())

            @block.vector
            def _(dve):
                c = Chain(dve, s_dve, n_link)

                def scans(data, gate_f, gate_b, op0, op1, init):
                    for h in range(H):
                        a, b = (init, init) if isinstance(init, float) else (init[:, 0, h:h + 1], init[:, 1, h:h + 1])
                        dve.tensor_tensor_scan(fw[:, h, :], gate_f[:, :], data[:, h, :], a, op0, op1)
                        last = dve.tensor_tensor_scan(bw[:, h, ::-1], gate_b[:, ::-1], data[:, h, ::-1], b, op0, op1)
                    return last

                dve.scalar_tensor_tensor(e, e, SLOPE, e, ALU.mult, ALU.max)
                c.link(dve.scalar_tensor_tensor(e_self, e_self, SLOPE, e_self, ALU.mult, ALU.max))
                c.link(scans(e, pen_f, pen_b, ALU.add, ALU.max, -BIG))
                for h in range(H):
                    dve.tensor_scalar(rep[:, 0, h, :], ones[0:P, 0:P], fw[:, h, ET - 1:ET], None, ALU.mult)
                    last = dve.tensor_scalar(rep[:, 1, h, :], ones[0:P, 0:P], bw[:, h, 0:1], None, ALU.mult)
                c.link(last)
                dve.wait_ge(s_pe.sem, s_pe.at(1))
                for j, far in enumerate((far_f, far_b)):
                    last = dve.tensor_tensor(cand[:, j, :, :], turned[:, j, 0:H * P].rearrange("p (h q) -> p h q", h=H),
                                             far[:, :].unsqueeze(1).broadcast_to([P, H, P]), ALU.add)
                c.link(last)
                c.link(dve.tensor_reduce(carry[:, :, :], cand[:, :, :, :], AX.X, ALU.max))
                c.link(scans(e, pen_f, pen_b, ALU.add, ALU.max, carry))
                c.link(dve.tensor_tensor(fw[:, :, :], fw[:, :, :], bw[:, :, :], ALU.max))
                c.link(dve.tensor_tensor(fw[:, :, :], fw[:, :, :], e_self, ALU.max))
                dve.tensor_tensor(e, e, fw[:, :, :], ALU.subtract)
                c.link(dve.tensor_tensor(e_self, e_self, fw[:, :, :], ALU.subtract))
                dve.wait_ge(s_exp.sem, s_exp.at(1))
                c.link(scans(e, same_f, same_b, ALU.mult, ALU.add, 0.0))
                dve.tensor_copy(ends[:, 0, :], fw[:, :, ET - 1])
                c.link(dve.tensor_copy(ends[:, 1, :], bw[:, :, 0]))
                dve.wait_ge(s_pe.sem, s_pe.at(2))
                c.link(dve.tensor_copy(carry[:, :, :], summed[:, :, :]))
                c.link(scans(e, same_f, same_b, ALU.mult, ALU.add, carry))
                c.link(dve.tensor_tensor(den[:, :, :], fw[:, :, :], bw[:, :, :], ALU.add))
                c.link(dve.tensor_tensor(den[:, :, :], den[:, :, :], e, ALU.subtract))
                c.link(dve.scalar_tensor_tensor(den[:, :, :], den[:, :, :], 1e-16, e_self, ALU.add, ALU.add))
                c.link(dve.reciprocal(den[:, :, :], den[:, :, :]))
                c.link(dve.scalar_tensor_tensor(alpha, e, factor, den[:, :, :], ALU.mult, ALU.mult))
                c.done()

            @block.scalar
            def _(act):
                act.wait_ge(s_dve.sem, s_dve.at(9))
                nc.scalar.activation(e, e, ACT.Exp)
                nc.scalar.activation(e_self, e_self, ACT.Exp).then_inc(s_exp.sem, 1)

            @block.tensor
            def _(pe):
                pe.wait_ge(s_dve.sem, s_dve.at(3))
                for j in range(2):
                    for h in range(H):
                        last = pe.transpose(turned[:, j, h * P:(h + 1) * P], rep[:, j, h, :], ident[0:P, 0:P])
                last.then_inc(s_pe.sem, 1)
                pe.wait_ge(s_dve.sem, s_dve.at(11))
                pe.matmul(summed[:, 0, :], mask_f[:, :], ends[:, 0, :], start=True, stop=True)
                pe.matmul(summed[:, 1, :], mask_b[:, :], ends[:, 1, :], start=True, stop=True).then_inc(s_pe.sem, 1)

        s_dve.base += n_link
        s_pe.base += 2
        s_exp.base += 1

    def gat_edges(name, table, W):
        with ExitStack() as outer:
            def sbo(nm, shape, dt=F32):
                return outer.enter_context(nc.sbuf_tensor(f"{name}_{nm}", shape, dt))

            z = sbo("z", [P, ET, D])
            e, e_self, alpha = sbo("e", [P, H, ET]), sbo("es", [P, H, ET]), sbo("alpha", [P, H, ET])
            with ExitStack() as ctx:
                xs = ctx.enter_context(nc.sbuf_tensor(f"{name}_xs", [P, 2, K, ROW], F32))
                xd = ctx.enter_context(nc.sbuf_tensor(f"{name}_xd", [P, 2, K, ROW], F32))
                idx = ctx.enter_context(nc.sbuf_tensor(f"{name}_idx", [P, 2, 2, K], I32))
                s_g = [[signal(f"gather_{c}{b}") for b in range(2)] for c in "ab"]
                s_pool, s_used = signal("pool_chain"), signal("inputs_used")
                block = ctx.enter_context(nc.Block())

                @block.gpsimd
                def _(pool):
                    def body(s, b, q, first):
                        if first is None:
                            pool.wait_ge(s_used.sem, s_used.at(s - 1))
                        gather_step(pool, Chain(pool, s_pool, 2, s), s,
                                    [(src_idx, idx[:, b, 0, :], table, xs[:, b], ROW, s_g[0][b]),
                                     (dst_idx, idx[:, b, 1, :], table, xd[:, b], ROW, s_g[1][b])])

                    steps(pool, ESTEP, body)

                @block.vector
                def _(dve):
                    def body(s, b, q, first):
                        for sg in s_g:
                            dve.wait_ge(sg[b].sem, sg[b].at(16 * K * (q + 1)))
                        at = bass.ds(s * K, K)
                        dve.tensor_tensor(z[:, at, :], xs[:, b, :, 0:D], xd[:, b, :, 0:D], ALU.subtract)
                        dve.tensor_tensor(e[:, :, at], xs[:, b, :, D:D + H].rearrange("p k h -> p h k"),
                                          xd[:, b, :, D + H:ROW].rearrange("p k h -> p h k"), ALU.add)
                        dve.tensor_tensor(e_self[:, :, at], xd[:, b, :, D:D + H].rearrange("p k h -> p h k"),
                                          xd[:, b, :, D + H:ROW].rearrange("p k h -> p h k"),
                                          ALU.add).then_inc(s_used.sem, 1)

                    steps(dve, ESTEP, body)

            for sg in s_g:
                sg[0].base += 16 * K * ((ESTEP + 1) // 2)
                sg[1].base += 16 * K * (ESTEP // 2)
            s_pool.base += 2 * ESTEP
            s_used.base += ESTEP

            softmax(name, e[:, :, :], e_self[:, :, :], alpha[:, :, :], 1.0 / H if W is not None else 1.0)

            sums = sbo("sums", [P, 2, K, AGG])
            with ExitStack() as ctx:
                def sb(nm, shape, dt=F32):
                    return ctx.enter_context(nc.sbuf_tensor(f"{name}_{nm}", shape, dt))

                idx = sb("sidx", [P, 2, K], I32)
                al = sb("al", [P, 2, K, H])
                msg = sb("msg", [P, K, AGG])
                same = sb("same", [P, 2, K])
                s_sc = [signal(f"scatter_{b}") for b in range(2)]
                s_pool, s_dve, s_m, s_set = signal("pool_chain"), signal("dve_chain"), signal("sums_ready"), signal("setup")
                s_zc, s_tr, s_hT, s_mm = signal("h_ready"), signal("turned"), signal("hT_ready"), signal("product_ready")
                s_ev, s_w = signal("product_used"), signal("weights")
                if W is not None:
                    zc = sb("zc", [P, 2, K, D])
                    zT = sb("zT", [D, 2, 2, HALF * P])
                    w = sb("w", [D, H * D])
                    pT = ctx.enter_context(nc.psum_tensor(f"{name}_pT", [D, 2, 512], F32))
                    pY = ctx.enter_context(nc.psum_tensor(f"{name}_pY", [P, 4, 512], F32))
                    links = 2 + (K // 2) * (H - 1) + (K - 1)
                else:
                    links = 2 + 1 + (K - 1)
                block = ctx.enter_context(nc.Block())

                @block.gpsimd
                def _(pool):
                    def body(s, b, q, first):
                        pool.wait_ge(s_m.sem, s_m.at(s + 1))
                        scatter_step(pool, Chain(pool, s_pool, 1, s), idx[:, b, :], sums[:, b], s_sc[b], s)

                    steps(pool, ESTEP, body)
                    pool.wait_ge(s_sc[0].sem, s_sc[0].at(16 * K * ((ESTEP + 1) // 2)))
                    pool.wait_ge(s_sc[1].sem, s_sc[1].at(16 * K * (ESTEP // 2)))

                @block.vector
                def _(dve):
                    dve.memset(msg[:, :, :], 1.0)
                    dve.memset(sums[:, :, :, :], 0.0).then_inc(s_set.sem, 1)
                    dve.wait_ge(s_set.sem, s_set.at(1))

                    def body(s, b, q, first):
                        c = Chain(dve, s_dve, links, s)
                        at = bass.ds(s * K, K)
                        c.link(dve.tensor_copy(al[:, b, :, :], alpha[:, :, at].rearrange("p h k -> p k h")))
                        c.link(dve.tensor_copy(same[:, b, :], same_f[:, at]))
                        if first is None:
                            dve.wait_ge(s_sc[b].sem, s_sc[b].at(16 * K * q))
                        if W is None:
                            c.link(dve.tensor_tensor(
                                msg[:, :, 0:D].rearrange("p k (h c) -> p k h c", h=H),
                                z[:, at, :].rearrange("p k (h c) -> p k h c", h=H),
                                al[:, b, :, :].unsqueeze(3).broadcast_to([P, K, H, DH]), ALU.mult))
                            run_sums(dve, c, s, b, range(K), sums, same, msg, s_m)
                        else:
                            for j in range(K // 2):
                                dve.wait_ge(s_mm.sem, s_mm.at((K // 2) * s + j + 1))
                                for h in range(H):
                                    for k in (2 * j, 2 * j + 1):
                                        y, a = pY[:, k % 4, h * D:(h + 1) * D], al[:, b, k, h:h + 1]
                                        if h == 0:
                                            ins = dve.tensor_scalar(msg[:, k, 0:D], y, a, None, ALU.mult)
                                        else:
                                            ins = dve.scalar_tensor_tensor(msg[:, k, 0:D], y, a, msg[:, k, 0:D],
                                                                           ALU.mult, ALU.add)
                                    if h < H - 1:
                                        c.link(ins)
                                ins.then_inc(s_ev.sem, 1)
                                dve.wait_ge(s_ev.sem, s_ev.at((K // 2) * s + j + 1))
                                run_sums(dve, c, s, b, (2 * j, 2 * j + 1), sums, same, msg, s_m)
                        c.done()

                    steps(dve, ESTEP, body)

                if W is not None:
                    @block.sync
                    def _(sp):
                        sp.dma_start(w[:, :], W).then_inc(s_w.sem, 16)

                    @block.scalar
                    def _(act):
                        def body(s, b, q, first):
                            nc.scalar.copy(zc[:, b, :, :], z[:, bass.ds(s * K, K), :]).then_inc(s_zc.sem, 1)
                            for r in range(2):
                                act.wait_ge(s_tr.sem, s_tr.at(2 * s + r + 1))
                                if first is None:
                                    act.wait_ge(s_mm.sem, s_mm.at((K // 2) * (s - 1)))
                                nc.scalar.copy(zT[:, b, r, :], pT[:, r, 0:HALF * P]).then_inc(s_hT.sem, 1)

                        steps(act, ESTEP, body)

                    @block.tensor
                    def _(pe):
                        pe.wait_ge(s_w.sem, s_w.at(16))

                        def body(s, b, q, first):
                            pe.wait_ge(s_zc.sem, s_zc.at(s + 1))
                            for r in range(2):
                                pe.wait_ge(s_hT.sem, s_hT.at(2 * s))
                                for k in range(HALF):
                                    last = pe.transpose(pT[:, r, k * P:(k + 1) * P], zc[:, b, r * HALF + k, :],
                                                        ident[0:P, 0:P])
                                last.then_inc(s_tr.sem, 1)
                            for j in range(K // 2):
                                pe.wait_ge(s_hT.sem, s_hT.at(2 * s + j // 2 + 1))
                                if first != 0 or j > 0:
                                    pe.wait_ge(s_ev.sem, s_ev.at((K // 2) * s + j - 1))
                                for k in (2 * j, 2 * j + 1):
                                    last = pe.matmul(pY[:, k % 4, 0:H * D],
                                                     zT[:, b, k // HALF, (k % HALF) * P:(k % HALF + 1) * P], w[:, :],
                                                     start=True, stop=True)
                                last.then_inc(s_mm.sem, 1)

                        steps(pe, ESTEP, body)

            s_sc[0].base += 16 * K * ((ESTEP + 1) // 2)
            s_sc[1].base += 16 * K * (ESTEP // 2)
            s_pool.base += ESTEP
            s_dve.base += links * ESTEP
            s_m.base += ESTEP
            s_set.base += 1
            if W is not None:
                s_w.base += 16
                s_zc.base += ESTEP
                s_tr.base += 2 * ESTEP
                s_hT.base += 2 * ESTEP
                s_mm.base += (K // 2) * ESTEP
                s_ev.base += (K // 2) * ESTEP
            close_segments(name + "_close", sums[:, (ESTEP - 1) % 2, K - 1, :])

    def gcn_edges(name, table):
        with ExitStack() as ctx:
            def sb(nm, shape, dt=F32):
                return ctx.enter_context(nc.sbuf_tensor(f"{name}_{nm}", shape, dt))

            sums = sb("sums", [P, 2, K, AGG])
            x = sb("x", [P, 2, K, AGG])
            same = sb("same", [P, 2, K])
            idx = sb("idx", [P, 2, 2, K], I32)
            s_g = [signal(f"gather_a{b}") for b in range(2)]
            s_sc = [signal(f"scatter_{b}") for b in range(2)]
            s_pool, s_dve, s_m, s_set = signal("pool_chain"), signal("dve_chain"), signal("sums_ready"), signal("setup")
            links = 1 + (K - 1)
            with nc.Block() as block:
                @block.gpsimd
                def _(pool):
                    pool.wait_ge(s_set.sem, s_set.at(1))
                    pool.nop(nofuse=True)

                    def body(s, b, q, first):
                        c = Chain(pool, s_pool, 2, s)
                        c.k = 0 if first == 0 else -1
                        gather_step(pool, c, s, [(src_idx, idx[:, b, 0, :], table, x[:, b], D, s_g[b])])
                        if first != 0:
                            pool.wait_ge(s_m.sem, s_m.at(s))
                            scatter_step(pool, c, idx[:, 1 - b, 1, :], sums[:, 1 - b], s_sc[1 - b], s - 1)

                    steps(pool, ESTEP, body)
                    pool.wait_ge(s_m.sem, s_m.at(ESTEP))
                    b = (ESTEP - 1) % 2
                    c = Chain(pool, s_pool, 2, ESTEP)
                    c.k = -1
                    scatter_step(pool, c, idx[:, b, 1, :], sums[:, b], s_sc[b], ESTEP - 1)
                    pool.wait_ge(s_sc[0].sem, s_sc[0].at(16 * K * ((ESTEP + 1) // 2)))
                    pool.wait_ge(s_sc[1].sem, s_sc[1].at(16 * K * (ESTEP // 2)))

                @block.vector
                def _(dve):
                    dve.memset(sums[:, :, :, :], 0.0)
                    dve.memset(x[:, :, :, :], 1.0).then_inc(s_set.sem, 1)
                    dve.wait_ge(s_set.sem, s_set.at(1))

                    def body(s, b, q, first):
                        c = Chain(dve, s_dve, links, s)
                        c.link(dve.tensor_copy(same[:, b, :], same_f[:, bass.ds(s * K, K)]))
                        dve.wait_ge(s_g[b].sem, s_g[b].at(16 * K * (q + 1)))
                        if first is None:
                            dve.wait_ge(s_sc[b].sem, s_sc[b].at(16 * K * q))
                        run_sums(dve, c, s, b, range(K), sums, same, x[:, b], s_m)
                        c.done()

                    steps(dve, ESTEP, body)

            for sg in (s_g, s_sc):
                sg[0].base += 16 * K * ((ESTEP + 1) // 2)
                sg[1].base += 16 * K * (ESTEP // 2)
            s_pool.base += 2 * ESTEP
            s_dve.base += links * ESTEP
            s_m.base += ESTEP
            s_set.base += 1
            close_segments(name + "_close", sums[:, (ESTEP - 1) % 2, K - 1, :])

    def edge_mlp(name, wmsg):
        with ExitStack() as ctx:
            def sb(nm, shape, dt=F32):
                return ctx.enter_context(nc.sbuf_tensor(f"{name}_{nm}", shape, dt))

            attr = sb("attr", [P, ET, 4])
            now = sb("now", [P, 2, K, 4])
            aT = sb("aT", [4, 2, 2, HALF * P])
            we = sb("we", [4, D])
            r = sb("r", [D, 2, HALF * P])
            r2 = sb("r2", [D, HALF * P])
            acc = sb("acc", [D, 2, 2 * ESTEP])
            cols = sb("cols", [D, 12])
            shift = sb("shift", [D, AGG])
            wraw = sb("wraw", [D, D])
            bm = sb("bm", [AGG, D])
            pT = ctx.enter_context(nc.psum_tensor(f"{name}_pT", [4, 2, 512], F32))
            pY = ctx.enter_context(nc.psum_tensor(f"{name}_pY", [D, 2, 512], F32))
            pC = ctx.enter_context(nc.psum_tensor(f"{name}_pC", [AGG, D], F32))
            s_ld, s_now, s_tr, s_hT = signal("load_a0"), signal("h_ready"), signal("turned"), signal("hT_ready")
            s_mm, s_ev, s_dve, s_dev = signal("product_ready"), signal("product_used"), signal("dve_chain"), signal("dev_ready")
            s_pe, s_set, s_acc = signal("pe_done"), signal("setup"), signal("squared")
            with nc.Block() as block:
                @block.sync
                def _(sp):
                    column = lambda v: v.rearrange("(d a) -> d a", a=1)
                    sp.dma_start(attr[:, :, :], A["edge_attr_4"].rearrange("(p t) c -> p t c", t=ET)).then_inc(s_ld.sem, 16)
                    sp.dma_start(we[:, :], A["L3_gnn_W_edge"]).then_inc(s_ld.sem, 16)
                    for i, nm in enumerate(("b_edge", "g_edge", "beta_edge")):
                        sp.dma_start(cols[:, i:i + 1], column(A[f"L3_gnn_{nm}"]),
                                     allow_slow_non_contiguous=True).then_inc(s_ld.sem, 16)
                    sp.dma_start(wraw[:, :], A["L3_gnn_W_msg"][2 * D:3 * D, :]).then_inc(s_ld.sem, 16)
                    sp.dma_start(bm[D:AGG, :], row1(A["L3_gnn_b_msg"])).then_inc(s_ld.sem, 16)

                @block.vector
                def _(dve):
                    dve.memset(shift[:, :], 0.0).then_inc(s_set.sem, 1)
                    dve.wait_ge(s_ld.sem, s_ld.at(16 * 7))

                    def body(s, b, q, first):
                        for h in range(2):
                            dve.wait_ge(s_tr.sem, s_tr.at(2 * s + h + 1))
                            if first is None:
                                dve.wait_ge(s_mm.sem, s_mm.at(2 * (s - 1)))
                            dve.tensor_copy(aT[:, b, h, :], pT[:, h, 0:HALF * P]).then_inc(s_hT.sem, 1)

                    steps(dve, ESTEP, body)
                    c = Chain(dve, s_dve, 10)
                    dve.wait_ge(s_acc.sem, s_acc.at(2 * ESTEP))
                    c.link(dve.tensor_reduce(cols[:, 3:5], acc[:, :, :], AX.X, ALU.add))
                    c.link(dve.tensor_scalar(cols[:, 3:5], cols[:, 3:5], 1.0 / E, None, ALU.mult))
                    c.link(dve.tensor_tensor(cols[:, 5:6], cols[:, 3:4], cols[:, 3:4], ALU.mult))
                    c.link(dve.tensor_tensor(cols[:, 6:7], cols[:, 4:5], cols[:, 5:6], ALU.subtract))
                    dve.wait_ge(s_dev.sem, s_dev.at(1))
                    c.link(dve.reciprocal(cols[:, 7:8], cols[:, 6:7]))
                    c.link(dve.tensor_tensor(cols[:, 8:9], cols[:, 7:8], cols[:, 1:2], ALU.mult))
                    c.link(dve.tensor_tensor(cols[:, 9:10], cols[:, 3:4], cols[:, 8:9], ALU.mult))
                    c.link(dve.tensor_tensor(shift[:, D:AGG], cols[:, 2:3], cols[:, 9:10], ALU.subtract))
                    c.link(dve.tensor_scalar(wmsg[0:D, :], wraw[:, :], cols[:, 8:9], None, ALU.mult))
                    dve.wait_ge(s_pe.sem, s_pe.at(1))
                    c.link(dve.tensor_tensor(wmsg[D:AGG, :], pC[D:AGG, :], bm[D:AGG, :], ALU.add))
                    c.done()

                @block.scalar
                def _(act):
                    act.wait_ge(s_ld.sem, s_ld.at(16 * 7))

                    def body(s, b, q, first):
                        nc.scalar.copy(now[:, b], attr[:, bass.ds(s * K, K), :]).then_inc(s_now.sem, 1)
                        for h in range(2):
                            act.wait_ge(s_mm.sem, s_mm.at(2 * s + h + 1))
                            if first is None or first > 0 or h > 0:
                                act.wait_ge(s_acc.sem, s_acc.at(2 * s + h))
                            nc.scalar.activation(r[:, h, :], pY[:, h, 0:HALF * P], ACT.Relu, bias=cols[:, 0:1],
                                                 accum_out=acc[:, 0, bass.ds(2 * s + h, 1)]).then_inc(s_ev.sem, 1)
                            act.wait_ge(s_ev.sem, s_ev.at(2 * s + h + 1))
                            nc.scalar.activation(r2[:, :], r[:, h, :], ACT.Square,
                                                 accum_out=acc[:, 1, bass.ds(2 * s + h, 1)]).then_inc(s_acc.sem, 1)

                    steps(act, ESTEP, body)
                    act.wait_ge(s_dve.sem, s_dve.at(4))
                    nc.scalar.activation(cols[:, 6:7], cols[:, 6:7], ACT.Sqrt,
                                         bias=eps_col[0:D, :]).then_inc(s_dev.sem, 1)

                @block.tensor
                def _(pe):
                    pe.wait_ge(s_ld.sem, s_ld.at(16 * 7))

                    def body(s, b, q, first):
                        pe.wait_ge(s_now.sem, s_now.at(s + 1))
                        for h in range(2):
                            pe.wait_ge(s_hT.sem, s_hT.at(2 * s))
                            for k in range(HALF):
                                last = pe.transpose(pT[:, h, k * P:(k + 1) * P], now[:, b, h * HALF + k, :],
                                                    ident[0:P, 0:P])
                            last.then_inc(s_tr.sem, 1)
                        for h in range(2):
                            pe.wait_ge(s_hT.sem, s_hT.at(2 * s + h + 1))
                            pe.wait_ge(s_ev.sem, s_ev.at(2 * s))
                            pe.matmul(pY[:, h, 0:HALF * P], we[:, :], aT[:, b, h, :], start=True,
                                      stop=True).then_inc(s_mm.sem, 1)

                    steps(pe, ESTEP, body)
                    pe.wait_ge(s_dve.sem, s_dve.at(8))
                    pe.matmul(pC[:, :], shift[:, :], wraw[:, :], start=True, stop=True).then_inc(s_pe.sem, 1)

        s_ld.base += 16 * 7
        s_now.base += ESTEP
        for sg in (s_tr, s_hT, s_mm, s_ev, s_acc):
            sg.base += 2 * ESTEP
        s_dve.base += 10
        s_dev.base += 1
        s_pe.base += 1
        s_set.base += 1

    def message_edges(name, wmsg, gram):
        with ExitStack() as ctx:
            def sb(nm, shape, dt=F32):
                return ctx.enter_context(nc.sbuf_tensor(f"{name}_{nm}", shape, dt))

            attr = sb("attr", [P, ET, 4])
            now = sb("now", [P, 2, K, 4])
            aT = sb("aT", [4, 2, HALF * P])
            we = sb("we", [4, D])
            be = sb("be", [D, 1])
            w = sb("w", [D, 2, D])
            f = sb("f", [AGG, 2, HALF * P])
            x = sb("x", [P, 2, 2, K, D])
            xT = sb("xT", [D, 2, 2, HALF * P])
            msg = sb("msg", [P, 2, K, AGG])
            zeros = sb("zeros", [P, AGG])
            sums = sb("sums", [P, 2, K, AGG])
            same = sb("same", [P, 2, K])
            idx = sb("idx", [P, 2, 3, K], I32)
            banks = ctx.enter_context(ExitStack())
            pA = banks.enter_context(nc.psum_tensor(f"{name}_pA", [D, 512], F32))
            pX = banks.enter_context(nc.psum_tensor(f"{name}_pX", [D, 2, 2, 512], F32))
            pM = banks.enter_context(nc.psum_tensor(f"{name}_pM", [P, 2, 512], F32))
            s_g = [[signal(f"gather_{c}{b}") for b in range(2)] for c in "ab"]
            s_sc = [signal(f"scatter_{b}") for b in range(2)]
            s_pool, s_dve, s_m, s_set = signal("pool_chain"), signal("dve_chain"), signal("sums_ready"), signal("setup")
            s_ld, s_now, s_ta, s_aT = signal("load_a0"), signal("h_ready"), signal("turned"), signal("hT_ready")
            s_ea, s_f, s_tx, s_xT = signal("edge_product"), signal("features"), signal("rows_turned"), signal("rows_ready")
            s_mm, s_relu, s_st = signal("product_ready"), signal("normed"), signal("summed")
            links = 1 + (K - 1)
            with nc.Block() as block:
                @block.sync
                def _(sp):
                    sp.dma_start(attr[:, :, :], A["edge_attr_4"].rearrange("(p t) c -> p t c", t=ET))\
                        .then_inc(s_ld.sem, 16)
                    sp.dma_start(we[:, :], A["L3_gnn_W_edge"]).then_inc(s_ld.sem, 16)
                    sp.dma_start(be[:, :], A["L3_gnn_b_edge"].rearrange("(d a) -> d a", a=1),
                                 allow_slow_non_contiguous=True).then_inc(s_ld.sem, 16)
                    for j in range(2):
                        sp.dma_start(w[:, j, :], A["L3_gnn_W_msg"][j * D:(j + 1) * D, :]).then_inc(s_ld.sem, 16)

                @block.gpsimd
                def _(pool):
                    def gather(t):
                        if t.after(2):
                            pool.wait_ge(s_tx.sem, s_tx.at(2 * (t.s - 1)))
                        c = Chain(pool, s_pool, 3, t.s)
                        c.k = -1 if t.c else 0
                        gather_step(pool, c, t.s, [(src_idx, idx[:, t.b, 0, :], t_h3, x[:, t.b, 0], D, s_g[0][t.b]),
                                                   (dst_idx, idx[:, t.b, 1, :], t_h3, x[:, t.b, 1], D, s_g[1][t.b])])

                    def scatter(t):
                        pool.wait_ge(s_m.sem, s_m.at(t.s + 1))
                        c = Chain(pool, s_pool, 3, t.s)
                        c.k = 2 if t.c == ESTEP - 1 else 4
                        scatter_step(pool, c, idx[:, t.b, 2, :], sums[:, t.b], s_sc[t.b], t.s)

                    pipeline(pool, ESTEP, [(0, gather), (1, scatter)])
                    pool.wait_ge(s_sc[0].sem, s_sc[0].at(16 * K * ((ESTEP + 1) // 2)))
                    pool.wait_ge(s_sc[1].sem, s_sc[1].at(16 * K * (ESTEP // 2)))

                @block.vector
                def _(dve):
                    dve.memset(sums[:, :, :, :], 0.0)
                    dve.memset(f[:, :, :], 1.0)
                    dve.memset(zeros[:, :], 0.0)
                    dve.memset(msg[:, :, :, :], 1.0).then_inc(s_set.sem, 1)
                    dve.wait_ge(s_set.sem, s_set.at(1))

                    def rows_back(t):
                        for j in range(2):
                            dve.wait_ge(s_tx.sem, s_tx.at(2 * t.s + j + 1))
                            if t.after(1):
                                dve.wait_ge(s_mm.sem, s_mm.at(t.s))
                            dve.tensor_copy(xT[:, j], pX[:, j, :, 0:HALF * P]).then_inc(s_xT.sem, 1)

                    def run(t):
                        c = Chain(dve, s_dve, links, t.s)
                        c.link(dve.tensor_copy(same[:, t.b, :], same_f[:, bass.ds(t.s * K, K)]))
                        dve.wait_ge(s_relu.sem, s_relu.at(t.s + 1))
                        if t.after(2):
                            dve.wait_ge(s_sc[t.b].sem, s_sc[t.b].at(16 * K * t.q))
                        run_sums(dve, c, t.s, t.b, range(K), sums, same, msg[:, t.b], s_m)
                        c.done()

                    pipeline(dve, ESTEP, [(0, rows_back), (0, run)])

                @block.scalar
                def _(act):
                    act.wait_ge(s_ld.sem, s_ld.at(80))
                    act.wait_ge(s_set.sem, s_set.at(1))

                    def features(t):
                        nc.scalar.copy(now[:, t.b], attr[:, bass.ds(t.s * K, K), :]).then_inc(s_now.sem, 1)
                        for j in range(2):
                            act.wait_ge(s_ta.sem, s_ta.at(2 * t.s + j + 1))
                            nc.scalar.copy(aT[:, j, :], pA[0:4, 0:HALF * P]).then_inc(s_aT.sem, 1)
                            act.wait_ge(s_ea.sem, s_ea.at(2 * t.s + j + 1))
                            if t.after(1):
                                act.wait_ge(s_mm.sem, s_mm.at(t.s))
                            nc.scalar.activation(f[0:D, j, :], pA[:, 0:HALF * P], ACT.Relu,
                                                 bias=be[:, :]).then_inc(s_f.sem, 1)

                    def relu(t):
                        act.wait_ge(s_mm.sem, s_mm.at(t.s + 1))
                        if t.after(2):
                            act.wait_ge(s_st.sem, s_st.at(t.s - 1))
                            act.wait_ge(s_m.sem, s_m.at(t.s - 1))
                        nc.scalar.activation(msg[:, t.b, :, 0:D].rearrange("p (a k) c -> p a k c", a=2),
                                             pM[:, :, 0:HALF * D].rearrange("p a (k c) -> p a k c", k=HALF),
                                             ACT.Relu).then_inc(s_relu.sem, 1)

                    pipeline(act, ESTEP, [(0, features), (0, relu)])

                @block.tensor
                def _(pe):
                    pe.wait_ge(s_ld.sem, s_ld.at(80))
                    pe.wait_ge(s_set.sem, s_set.at(1))
                    gram_edge(pe, gram, zeros, True)

                    def features(t):
                        pe.wait_ge(s_now.sem, s_now.at(t.s + 1))
                        for j in range(2):
                            if t.after(1) or j:
                                pe.wait_ge(s_f.sem, s_f.at(2 * t.s + j))
                            for k in range(HALF):
                                last = pe.transpose(pA[0:4, k * P:(k + 1) * P], now[:, t.b, j * HALF + k, :],
                                                    ident[0:P, 0:P])
                            last.then_inc(s_ta.sem, 1)
                            pe.wait_ge(s_aT.sem, s_aT.at(2 * t.s + j + 1))
                            pe.matmul(pA[:, 0:HALF * P], we[:, :], aT[:, j, :], start=True,
                                      stop=True).then_inc(s_ea.sem, 1)

                    def turn(t):
                        for j in range(2):
                            pe.wait_ge(s_g[j][t.b].sem, s_g[j][t.b].at(16 * K * (t.q + 1)))
                            if t.after(1):
                                pe.wait_ge(s_xT.sem, s_xT.at(2 * (t.s - 1) + j + 1))
                            for k in range(K):
                                last = pe.transpose(pX[:, j, k // HALF, (k % HALF) * P:(k % HALF + 1) * P],
                                                    x[:, t.b, j, k, :], ident[0:P, 0:P])
                            last.then_inc(s_tx.sem, 1)

                    def product(t):
                        pe.wait_ge(s_f.sem, s_f.at(2 * t.s + 2))
                        pe.wait_ge(s_xT.sem, s_xT.at(2 * t.s + 2))
                        if t.after(1):
                            pe.wait_ge(s_relu.sem, s_relu.at(t.s))
                        for k in range(K):
                            a, at = k // HALF, slice((k % HALF) * P, (k % HALF + 1) * P)
                            o = pM[:, a, (k % HALF) * D:(k % HALF + 1) * D]
                            pe.matmul(o, f[:, a, at], wmsg[:, :], start=True, stop=False)
                            pe.matmul(o, xT[:, 0, a, at], w[:, 0, :], start=False, stop=False)
                            last = pe.matmul(o, xT[:, 1, a, at], w[:, 1, :], start=False, stop=True)
                        last.then_inc(s_mm.sem, 1)

                    def total(t):
                        pe.wait_ge(s_relu.sem, s_relu.at(t.s + 1))
                        gram_step(pe, gram, msg[:, t.b]).then_inc(s_st.sem, 1)

                    pipeline(pe, ESTEP, [(0, features), (0, turn), (1, total), (0, product)])
                    gram_edge(pe, gram, zeros, False)

            for sg in s_g + [s_sc]:
                sg[0].base += 16 * K * ((ESTEP + 1) // 2)
                sg[1].base += 16 * K * (ESTEP // 2)
            s_pool.base += 3 * ESTEP
            s_dve.base += links * ESTEP
            s_ld.base += 80
            s_set.base += 1
            for x_ in (s_m, s_now, s_mm, s_relu, s_st):
                x_.base += ESTEP
            for x_ in (s_ta, s_aT, s_ea, s_f, s_tx, s_xT):
                x_.base += 2 * ESTEP
            banks.close()
            close_segments(name + "_close", sums[:, (ESTEP - 1) % 2, K - 1, :])

    def last_sum(name):
        with ExitStack() as ctx:
            def sb(nm, shape, dt=F32):
                return ctx.enter_context(nc.sbuf_tensor(f"{name}_{nm}", shape, dt))

            x, nf, c = sb("x", [P, 2, K, D]), sb("nf", [P, 2, K, AGG]), sb("c", [P, 2, K, AGG])
            y = sb("y", [P, 2, K, D])
            part = sb("part", [P, 2, K, D])
            s_in = [[signal(f"load_{j}{b}") for b in range(2)] for j in "abc"]
            s_out = [signal(f"store_a{b}") for b in range(2)]
            s_dve, s_ev, s_pool = signal("dve_chain"), signal("product_used"), signal("pool_chain")
            wide = lambda v: v[:, :].unsqueeze(1).broadcast_to([P, K, D])
            with nc.Block() as block:
                @block.sync
                def _(sp):
                    def body(s, b, q, first):
                        if first is None:
                            sp.wait_ge(s_ev.sem, s_ev.at(s - 1))
                            sp.nop(nofuse=True)
                        for (t, buf), sg in zip(((d_xc, x), (d_nf, nf), (t_agg, c)), s_in):
                            sp.dma_start(buf[:, b], rows(t, s)).then_inc(sg[b].sem, 16)
                        if first != 0:
                            sp.wait_ge(s_ev.sem, s_ev.at(s))
                            sp.nop(nofuse=True)
                            sp.dma_start(rows(out, s - 1), y[:, 1 - b]).then_inc(s_out[1 - b].sem, 16)

                    steps(sp, NSTEP, body)
                    sp.wait_ge(s_ev.sem, s_ev.at(NSTEP))
                    sp.dma_start(rows(out, NSTEP - 1), y[:, (NSTEP - 1) % 2]).then_inc(s_out[1].sem, 16)
                    for b in range(2):
                        sp.wait_ge(s_out[b].sem, s_out[b].at(16 * (NSTEP // 2)))

                @block.gpsimd
                def _(pool):
                    def body(s, b, q, first):
                        if first is None:
                            pool.wait_ge(s_ev.sem, s_ev.at(s - 1))
                        cn = count[:, bass.ds(s * K, K)].unsqueeze(2).broadcast_to([P, K, D])
                        pool.tensor_tensor(part[:, b], cn, wide(bm_t), ALU.mult).then_inc(s_pool.sem, 1)

                    steps(pool, NSTEP, body)

                @block.vector
                def _(dve):
                    def body(s, b, q, first):
                        ch = Chain(dve, s_dve, 3, s)
                        for sg in s_in:
                            dve.wait_ge(sg[b].sem, sg[b].at(16 * (q + 1)))
                        dve.tensor_tensor(nf[:, b, :, 0:D], nf[:, b, :, 0:D], wide(bn_s), ALU.mult)
                        ch.link(dve.tensor_tensor(c[:, b, :, 0:D], c[:, b, :, 0:D], wide(bm_s), ALU.mult))
                        dve.tensor_tensor(x[:, b], x[:, b], wide(bn_t), ALU.add)
                        ch.link(dve.tensor_tensor(nf[:, b, :, 0:D], nf[:, b, :, 0:D], c[:, b, :, 0:D], ALU.add))
                        ch.link(dve.tensor_tensor(x[:, b], x[:, b], nf[:, b, :, 0:D], ALU.add))
                        dve.wait_ge(s_pool.sem, s_pool.at(s + 1))
                        if first is None:
                            dve.wait_ge(s_out[b].sem, s_out[b].at(16 * q))
                        dve.tensor_tensor(y[:, b], x[:, b], part[:, b], ALU.add).then_inc(s_ev.sem, 1)
                        ch.done()

                    steps(dve, NSTEP, body)

    def finish_debug(src, w=None):
        with nc.Block() as block:
            s = signal("store_a")

            @block.sync
            def _(sp):
                sp.dma_start(out, src).then_inc(s.sem, 16)
                sp.wait_ge(s.sem, s.at(16))
        whole.close()

    prepare()
    node_phase("first", "first", [(A["x"], D)], [(t_h0, ROW), (d_y, D)], ROW,
               [(2 * H, None, A["L0_gnn_bias"][0])],
               gat=(A["L0_gnn_W"][0], A["L0_gnn_att_src"][0], A["L0_gnn_att_dst"][0], H, 0, 2 * H))
    if DEBUG == "first":
        return finish_debug(d_y)
    gat_edges("edges0", t_h0, A["L0_gnn_W"][0])
    if DEBUG == "edges0":
        return finish_debug(rows_all(t_agg))

    def gram_bank(ctx, name):
        return ctx.enter_context(nc.psum_tensor(name, [D, AGG], F32))[:, :]

    for layer in range(2):
        with ExitStack() as ctx:
            held = ctx.enter_context(nc.sbuf_tensor(f"held{layer}", [P, NT, D], F32))
            with ExitStack() as c2:
                gram = gram_bank(c2, f"gram{layer}")
                aggregate_phase(f"agg{layer}", held, layer == 0, gram)
                bn_coefficients(f"bn{layer}", gram, N, A["L0_gnn_gamma"][layer], A["L0_gnn_beta"][layer], bn_s, bn_t)
            if layer == 0:
                node_phase("second", "gat", [(t_h0, D)], [(t_x1, ROW), (d_y, D)], ROW,
                           [(2 * H, None, A["L0_gnn_bias"][1])], held=held,
                           gat=(A["L0_gnn_W"][1], A["L0_gnn_att_src"][1], A["L0_gnn_att_dst"][1], H, 0, 2 * H))
            else:
                node_phase("third", "join", [(t_x1, D), (A["x"], D)], [(d_xa, D), (t_g, ROW), (d_r, D)], ROW,
                           [(0, A["L1_gnn_W"], None)], held=held, bias=A["L1_gnn_bias"],
                           gat=(A["L1_gnn_W"], A["L1_gnn_att_src"], A["L1_gnn_att_dst"], H, D, None))
        if DEBUG == f"nodes{layer}":
            return finish_debug(d_y if layer == 0 else d_r)
        if layer == 0:
            gat_edges("edges1", t_x1, A["L0_gnn_W"][1])
    gat_edges("edges2", t_g, None)
    if DEBUG == "edges2":
        return finish_debug(rows_all(t_agg))
    node_phase("fourth", "layer", [(d_r, D), (t_agg, AGG), (d_xa, D)], [(d_xb, D), (t_c1, D)], D,
               [(0, A["L2_gnn_W1"], None)], gamma=A["L1_gnn_gamma"], beta=A["L1_gnn_beta"])
    if DEBUG == "fourth":
        return finish_debug(d_xb)
    gcn_edges("edges3", t_c1)
    node_phase("fifth", "gcn", [(t_c1, D), (t_agg, AGG)], [(t_c2, D)], D, [(0, A["L2_gnn_W2"], None)],
               bias=A["L2_gnn_b1"])
    if DEBUG == "fifth":
        return finish_debug(t_c2)
    gcn_edges("edges4", t_c2)
    with ExitStack() as ctx:
        gram = gram_bank(ctx, "gram_nf")
        node_phase("sixth", "last", [(t_c2, D), (t_agg, AGG), (d_xb, D)], [(d_xc, D), (t_h3, D), (d_nf, AGG)], D,
                   [(0, A["L3_gnn_W_node"], A["L3_gnn_b_node"])], bias=A["L2_gnn_b2"], gram=gram)
        bn_coefficients("bn_nf", gram, N, A["L3_gnn_g_node"], A["L3_gnn_beta_node"], bn_s, bn_t)
    if DEBUG == "sixth":
        return finish_debug(rows_all(d_nf))
    bm_s = sbw("bm_s", [P, D])
    bm_t = sbw("bm_t", [P, D])
    with ExitStack() as ctx:
        wmsg = ctx.enter_context(nc.sbuf_tensor("wmsg", [AGG, D], F32))
        edge_mlp("edge_mlp", wmsg)
        gram = gram_bank(ctx, "gram_msg")
        message_edges("edges5", wmsg, gram)
        bn_coefficients("bn_msg", gram, E, A["L3_gnn_g_msg"], A["L3_gnn_beta_msg"], bm_s, bm_t)
    if DEBUG == "edges5":
        return finish_debug(rows_all(t_agg))
    last_sum("out")
    whole.close()


_INS = ['x', 'src', 'dst', 'edge_attr_4', 'L0_gnn_W', 'L0_gnn_att_src', 'L0_gnn_att_dst', 'L0_gnn_bias',
        'L0_gnn_gamma', 'L0_gnn_beta', 'L1_gnn_W', 'L1_gnn_att_src', 'L1_gnn_att_dst', 'L1_gnn_bias',
        'L1_gnn_gamma', 'L1_gnn_beta', 'L2_gnn_W1', 'L2_gnn_b1', 'L2_gnn_W2', 'L2_gnn_b2', 'L3_gnn_W_node',
        'L3_gnn_b_node', 'L3_gnn_g_node', 'L3_gnn_beta_node', 'L3_gnn_W_edge', 'L3_gnn_b_edge', 'L3_gnn_g_edge',
        'L3_gnn_beta_edge', 'L3_gnn_W_msg', 'L3_gnn_b_msg', 'L3_gnn_g_msg', 'L3_gnn_beta_msg']


def kernel(**inputs):
    import numpy as _np
    import concourse.bacc as _bacc
    from concourse import mybir as _mybir
    from concourse.bass_utils import run_bass_kernel_spmd as _run

    nc = _bacc.Bacc("TRN2", target_bir_lowering=False, num_devices=1)
    arrays, args = {}, {}
    for name in _INS:
        a = _np.ascontiguousarray(inputs[name])
        arrays[f"in_{name}_dram"] = a
        args[name] = nc.dram_tensor(f"in_{name}_dram", a.shape, _mybir.dt.from_np(a.dtype), kind="ExternalInput").ap()
    out = nc.dram_tensor("out_0_dram", (N, D), F32, kind="ExternalOutput").ap()
    build(nc, args, out)
    r = _run(nc, [arrays], core_ids=[0])
    return r.results[0]["out_0_dram"]
```

```python
from contextlib import ExitStack

import concourse.bass as bass
from concourse import mybir

F32 = mybir.dt.float32
I32 = mybir.dt.int32
ALU = mybir.AluOpType
ACT = mybir.ActivationFunctionType
AX = mybir.AxisListType

N = 50000
E = 25000
D = 96
H = 4
DH = D // H
P = 125
NT = N // P
ET = E // P
K = 8
HALF = K // 2
NSTEP = NT // K
ESTEP = ET // K
ROW = D + 2 * H
AGG = D + 1
SPARE = 2 * K * P
CLEAR = (N + SPARE) // P // 16
BIG = 1.0e30
EPS = 1e-5
SLOPE = 0.2


def build(nc, A, out):
    whole = ExitStack()
    signals = {}

    class Signal:

        def __init__(self, name):
            self.sem = whole.enter_context(nc.semaphore(name))
            self.base = 0

        def at(self, count):
            return self.base + count

    def signal(name):
        if name not in signals:
            signals[name] = Signal(name)
        return signals[name]

    class Chain:

        def __init__(self, eng, sig, per, step=0):
            self.eng, self.sig, self.per, self.step, self.k = eng, sig, per, step, 0

        def link(self, ins):
            self.k += 1
            ins.then_inc(self.sig.sem, 1)
            self.eng.wait_ge(self.sig.sem, self.sig.at(self.per * self.step + self.k))

        def done(self):
            assert self.k == self.per, (self.k, self.per)

    def steps(eng, n, body):
        peel = 4 - n % 2
        for s in range(peel):
            body(s, s % 2, s // 2, s if s < 2 else None)
        with eng.Fori(0, (n - peel) // 2) as i:
            body(2 * i + peel, peel % 2, i + peel // 2, None)
            body(2 * i + peel + 1, (peel + 1) % 2, i + (peel + 1) // 2, None)

    class Step:

        def __init__(self, i, c, U):
            self.i, self.c, self.U = i, c, U
            self.b = c % 2
            self.s = c if i is None else U * i + c
            self.q = self.turn(2)

        @property
        def before(self):
            return Step(self.i, self.c - 1, self.U)

        def turn(self, R):
            return self.c // R if self.i is None else (self.U // R) * self.i + self.c // R

        def after(self, n):
            return self.c >= n

    def pipeline(eng, n, stages, U=2):
        deep = max(lag for lag, _ in stages)
        peel = 4 + deep
        while (n - peel) % U:
            peel += 1
        for c in range(peel):
            for lag, emit in stages:
                if c >= lag:
                    emit(Step(None, c - lag, U))
        with eng.Fori(0, (n - peel) // U) as i:
            for u in range(U):
                for lag, emit in stages:
                    emit(Step(i, peel + u - lag, U))
        for c in range(n, n + deep):
            for lag, emit in stages:
                if c - lag < n:
                    emit(Step(None, c - lag, U))

    def dram(name, shape):
        return nc.dram_tensor(name, shape, F32, kind="Internal").ap()

    t_h0 = dram("t_h0", [N, ROW])
    t_x1 = dram("t_x1", [N, ROW])
    t_g = dram("t_g", [N, ROW])
    d_y = dram("d_y", [N, D])
    d_xa = dram("d_xa", [N, D])
    d_xb = dram("d_xb", [N, D])
    d_xc = dram("d_xc", [N, D])
    d_r = dram("d_r", [N, D])
    d_base = dram("d_base", [N, D])
    t_c1 = dram("t_c1", [N, D])
    t_c2 = dram("t_c2", [N, D])
    t_h3 = dram("t_h3", [N, D])
    d_nf = dram("d_nf", [N, AGG])
    t_agg = dram("t_agg", [N + SPARE, AGG])

    def rows(table, step, w=None, tiles=K):
        v = table[0:N, :].rearrange("(p t) d -> p t d", t=NT)[:, bass.ds(step * tiles, tiles), :]
        return v if w is None else v[:, :, 0:w]

    def row1(v):
        return v.rearrange("(a d) -> a d", a=1)

    def sbw(name, shape, dt=F32):
        return whole.enter_context(nc.sbuf_tensor(name, shape, dt))

    ident = sbw("ident", [128, 128])
    ones = sbw("ones", [128, 128])
    ones_row = sbw("ones_row", [1, P])
    src_idx = sbw("src_idx", [P, ET], I32)
    dst_idx = sbw("dst_idx", [P, ET], I32)
    out_idx = sbw("out_idx", [P, ET], I32)
    fix_idx = sbw("fix_idx", [P, 1], I32)
    same_f = sbw("same_f", [P, ET])
    same_b = sbw("same_b", [P, ET])
    pen_f = sbw("pen_f", [P, ET])
    pen_b = sbw("pen_b", [P, ET])
    mask_f = sbw("mask_f", [P, P])
    mask_b = sbw("mask_b", [P, P])
    far_f = sbw("far_f", [P, P])
    far_b = sbw("far_b", [P, P])
    count = sbw("count", [P, NT])
    dinv = sbw("dinv", [P, NT])
    bn_s = sbw("bn_s", [P, D])
    bn_t = sbw("bn_t", [P, D])
    eps_col = sbw("eps_col", [P, 1])

    def prepare():
        with ExitStack() as ctx:
            def sb(name, shape, dt=F32):
                return ctx.enter_context(nc.sbuf_tensor(name, shape, dt))

            dst_f = sb("dst_f", [P, ET])
            next_i = sb("next_i", [P, 1], I32)
            next_f = sb("next_f", [P, 1])
            last = sb("last", [P, ET])
            spare_i = sb("spare_i", [P, (ET + 15) // 16, 2 * K], I32)
            spare = sb("spare", [P, ET])
            diff = sb("diff", [P, ET])
            fixf = sb("fixf", [P, 2])
            tri_f = sb("tri_f", [P, P])
            tri_b = sb("tri_b", [P, P])
            rep = sb("rep", [P, 2, P])
            turned = ctx.enter_context(nc.psum_tensor("turned", [P, 2, P], F32))
            s_ld, s_pool, s_nx = signal("load_a"), signal("pool_chain"), signal("load_b")
            s_dve, s_pe = signal("dve_chain"), signal("pe_done")
            block = ctx.enter_context(nc.Block())

            @block.sync
            def _(sp):
                sp.dma_start(src_idx[:, :], A["src"].rearrange("(p t) -> p t", t=ET)).then_inc(s_ld.sem, 16)
                sp.dma_start(dst_idx[:, :], A["dst"].rearrange("(p t) -> p t", t=ET)).then_inc(s_ld.sem, 16)
                sp.wait_ge(s_pool.sem, s_pool.at(1))
                sp.dma_start(next_i[0:P - 1, :],
                             A["dst"].rearrange("(p t) -> p t", t=ET)[1:P, 0:1],
                             allow_slow_non_contiguous=True).then_inc(s_nx.sem, 16)

            @block.gpsimd
            def _(pool):
                chain = Chain(pool, s_pool, 7)
                chain.link(pool.memset(next_i[:, :], -1))
                chain.link(pool.memset(ident[:, :], 0.0))
                chain.link(pool.affine_select(out=ident[:, :], in_=ident[:, :], compare_op=ALU.not_equal, fill=1.0,
                                              base=0, pattern=[[-1, 128]], channel_multiplier=1))
                chain.link(pool.memset(ones[:, :], 1.0))
                chain.link(pool.affine_select(out=tri_f[:, :], in_=ones[0:P, 0:P], compare_op=ALU.is_gt, fill=0.0,
                                              base=0, pattern=[[1, P]], channel_multiplier=-1))
                chain.link(pool.affine_select(out=tri_b[:, :], in_=ones[0:P, 0:P], compare_op=ALU.is_gt, fill=0.0,
                                              base=0, pattern=[[-1, P]], channel_multiplier=1))
                chain.link(pool.iota(spare_i[:, :, :], pattern=[[0, (ET + 15) // 16], [P, 2 * K]], base=N,
                                     channel_multiplier=1))
                chain.done()

            @block.vector
            def _(dve):
                chain = Chain(dve, s_dve, 18)
                dve.memset(eps_col[:, :], EPS)
                dve.memset(ones_row[:, :], 1.0)
                dve.memset(same_f[:, 0:1], 1.0)
                dve.wait_ge(s_ld.sem, s_ld.at(32))
                chain.link(dve.tensor_copy(dst_f[:, :], dst_idx[:, :]))
                dve.wait_ge(s_nx.sem, s_nx.at(16))
                chain.link(dve.tensor_copy(next_f[:, :], next_i[:, :]))
                chain.link(dve.tensor_tensor(same_f[:, 1:ET], dst_f[:, 1:ET], dst_f[:, 0:ET - 1], ALU.is_equal))
                chain.link(dve.memset(same_b[:, ET - 1:ET], 1.0))
                chain.link(dve.tensor_copy(same_b[:, 0:ET - 1], same_f[:, 1:ET]))
                dve.tensor_scalar(pen_f[:, :], same_f[:, :], BIG, -BIG, ALU.mult, ALU.add)
                dve.tensor_scalar(pen_b[:, :], same_b[:, :], BIG, -BIG, ALU.mult, ALU.add)
                dve.tensor_scalar(last[:, 0:ET - 1], same_b[:, 0:ET - 1], -1.0, 1.0, ALU.mult, ALU.add)
                chain.link(dve.tensor_tensor(last[:, ET - 1:ET], dst_f[:, ET - 1:ET], next_f[:, :], ALU.not_equal))
                dve.wait_ge(s_pool.sem, s_pool.at(7))
                chain.link(dve.tensor_copy(spare[:, :],
                                           spare_i[:, :, :].rearrange("p a b -> p (a b)")[:, 0:ET]))
                chain.link(dve.tensor_tensor(diff[:, :], dst_f[:, :], spare[:, :], ALU.subtract))
                dve.tensor_tensor(fixf[:, 0:1], dst_f[:, 0:1], next_f[:, :], ALU.not_equal)
                chain.link(dve.tensor_tensor(last[:, :], last[:, :], diff[:, :], ALU.mult))
                chain.link(dve.tensor_tensor(out_idx[:, :], last[:, :], spare[:, :], ALU.add))
                chain.link(dve.tensor_tensor(fixf[:, 1:2], fixf[:, 0:1], diff[:, 0:1], ALU.mult))
                chain.link(dve.tensor_tensor(fix_idx[:, :], fixf[:, 1:2], spare[:, 0:1], ALU.add))
                chain.link(dve.tensor_scalar(rep[:, 0, :], ones[0:P, 0:P], dst_f[:, 0:1], None, ALU.mult))
                chain.link(dve.tensor_scalar(rep[:, 1, :], ones[0:P, 0:P], dst_f[:, ET - 1:ET], None, ALU.mult))
                dve.wait_ge(s_pe.sem, s_pe.at(1))
                chain.link(dve.scalar_tensor_tensor(mask_f[:, :], turned[:, 0, :], dst_f[:, ET - 1:ET], tri_f[:, :],
                                                    ALU.is_equal, ALU.mult))
                chain.link(dve.scalar_tensor_tensor(mask_b[:, :], turned[:, 1, :], dst_f[:, 0:1], tri_b[:, :],
                                                    ALU.is_equal, ALU.mult))
                chain.link(dve.tensor_scalar(far_f[:, :], mask_b[:, :], BIG, -BIG, ALU.mult, ALU.add))
                chain.link(dve.tensor_scalar(far_b[:, :], mask_f[:, :], BIG, -BIG, ALU.mult, ALU.add))
                chain.done()

            @block.tensor
            def _(pe):
                pe.wait_ge(s_dve.sem, s_dve.at(14))
                pe.wait_ge(s_pool.sem, s_pool.at(3))
                pe.transpose(turned[:, 0, :], rep[:, 0, :], ident[0:P, 0:P])
                pe.transpose(turned[:, 1, :], rep[:, 1, :], ident[0:P, 0:P]).then_inc(s_pe.sem, 1)

        s_ld.base += 32
        s_pool.base += 7
        s_nx.base += 16
        s_dve.base += 18
        s_pe.base += 1

    def norm_stats(dve, link, x, bn, tmp, s_var):
        for k in range(K):
            ins = dve.bn_stats(bn[:, k, :], x[:, k, :])
        link(ins)
        dve.tensor_tensor(tmp[:, 0, :], bn[:, :, 1], bn[:, :, 4], ALU.add)
        dve.tensor_tensor(tmp[:, 2, :], bn[:, :, 2], bn[:, :, 5], ALU.add)
        link(dve.tensor_tensor(tmp[:, 1, :], bn[:, :, 1], bn[:, :, 4], ALU.subtract))
        link(dve.tensor_tensor(tmp[:, 1, :], tmp[:, 1, :], tmp[:, 1, :], ALU.mult))
        dve.scalar_tensor_tensor(tmp[:, 3, :], tmp[:, 1, :], D / 4.0, tmp[:, 2, :],
                                 ALU.mult, ALU.add).then_inc(s_var.sem, 1)

    def norm_scale(dve, link, tmp):
        link(dve.reciprocal(tmp[:, 5, :], tmp[:, 4, :]))
        return dve.scalar_tensor_tensor(tmp[:, 6, :], tmp[:, 0, :], -0.5, tmp[:, 5, :], ALU.mult, ALU.mult)

    def bn_coefficients(name, gram, n, gamma, beta, scale, shift, bias=None):
        with ExitStack() as ctx:
            diag = ctx.enter_context(nc.sbuf_tensor(f"{name}_diag", [D, D], F32))
            col = ctx.enter_context(nc.sbuf_tensor(f"{name}_col", [D, 12], F32))
            rep = ctx.enter_context(nc.sbuf_tensor(f"{name}_rep", [D, 2, P], F32))
            wide = ctx.enter_context(nc.psum_tensor(f"{name}_wide", [P, 2, D], F32))
            s_ld, s_dve = signal("load_a0"), signal("dve_chain")
            s_var, s_dev, s_pe = signal("var_ready"), signal("dev_ready"), signal("pe_done")
            n_ld, n_link = (32, 12) if bias is None else (48, 14)
            block = ctx.enter_context(nc.Block())

            @block.sync
            def _(sp):
                for k, v in [(0, gamma), (1, beta)] + ([(10, bias)] if bias is not None else []):
                    sp.dma_start(col[:, k:k + 1], v.rearrange("(d a) -> d a", a=1),
                                 allow_slow_non_contiguous=True).then_inc(s_ld.sem, 16)

            @block.vector
            def _(dve):
                c = Chain(dve, s_dve, n_link)
                c.link(dve.tensor_tensor(diag[:, :], gram[:, 0:D], ident[0:D, 0:D], ALU.mult))
                c.link(dve.tensor_reduce(col[:, 3:4], diag[:, :], AX.X, ALU.add))
                dve.tensor_scalar(col[:, 2:3], gram[:, D:AGG], 1.0 / n, None, ALU.mult)
                c.link(dve.tensor_scalar(col[:, 3:4], col[:, 3:4], 1.0 / n, None, ALU.mult))
                c.link(dve.tensor_tensor(col[:, 4:5], col[:, 2:3], col[:, 2:3], ALU.mult))
                dve.tensor_tensor(col[:, 5:6], col[:, 3:4], col[:, 4:5], ALU.subtract).then_inc(s_var.sem, 1)
                dve.wait_ge(s_dev.sem, s_dev.at(1))
                c.link(dve.reciprocal(col[:, 6:7], col[:, 5:6]))
                dve.wait_ge(s_ld.sem, s_ld.at(n_ld))
                c.link(dve.tensor_tensor(col[:, 7:8], col[:, 6:7], col[:, 0:1], ALU.mult))
                if bias is not None:
                    c.link(dve.tensor_tensor(col[:, 11:12], col[:, 2:3], col[:, 10:11], ALU.add))
                    c.link(dve.tensor_tensor(col[:, 2:3], col[:, 11:12], col[:, 10:11], ALU.subtract))
                c.link(dve.tensor_tensor(col[:, 8:9], col[:, 2:3], col[:, 7:8], ALU.mult))
                c.link(dve.tensor_tensor(col[:, 9:10], col[:, 1:2], col[:, 8:9], ALU.subtract))
                c.link(dve.tensor_scalar(rep[:, 0, :], ones[0:D, 0:P], col[:, 7:8], None, ALU.mult))
                c.link(dve.tensor_scalar(rep[:, 1, :], ones[0:D, 0:P], col[:, 9:10], None, ALU.mult))
                dve.wait_ge(s_pe.sem, s_pe.at(1))
                c.link(dve.tensor_copy(scale[:, :], wide[:, 0, :]))
                c.link(dve.tensor_copy(shift[:, :], wide[:, 1, :]))
                c.done()

            @block.scalar
            def _(act):
                act.wait_ge(s_var.sem, s_var.at(1))
                nc.scalar.activation(col[:, 5:6], col[:, 5:6], ACT.Sqrt, bias=eps_col[0:D, :]).then_inc(s_dev.sem, 1)

            @block.tensor
            def _(pe):
                pe.wait_ge(s_dve.sem, s_dve.at(n_link - 2))
                pe.transpose(wide[:, 0, :], rep[:, 0, :], ident[0:D, 0:D])
                pe.transpose(wide[:, 1, :], rep[:, 1, :], ident[0:D, 0:D]).then_inc(s_pe.sem, 1)

        s_ld.base += n_ld
        s_dve.base += n_link
        s_var.base += 1
        s_dev.base += 1
        s_pe.base += 1

    def gat_weights(name, wide, W, a_src, a_dst, heads, at_a, at_mean):
        width = W.shape[1]
        dh = width // heads
        with ExitStack() as ctx:
            w = ctx.enter_context(nc.sbuf_tensor(f"{name}_w", [D, heads, dh], F32))
            a = ctx.enter_context(nc.sbuf_tensor(f"{name}_a", [D, 2, heads, dh], F32))
            part = ctx.enter_context(nc.sbuf_tensor(f"{name}_part", [D, heads, dh], F32))
            s_ld, s_dve = signal("load_a0"), signal("dve_chain")
            block = ctx.enter_context(nc.Block())
            n_link = 4 + (2 if at_mean is not None else 0)

            @block.sync
            def _(sp):
                sp.dma_start(w[:, :, :], W.rearrange("c (h d) -> c h d", h=heads)).then_inc(s_ld.sem, 16)
                sp.dma_start(a[:, 0, :, :], a_src.partition_broadcast(D)).then_inc(s_ld.sem, 16)
                sp.dma_start(a[:, 1, :, :], a_dst.partition_broadcast(D)).then_inc(s_ld.sem, 16)

            @block.vector
            def _(dve):
                chain = Chain(dve, s_dve, n_link)
                dve.wait_ge(s_ld.sem, s_ld.at(48))
                for j in range(2):
                    chain.link(dve.tensor_tensor(part[:, :, :], w[:, :, :], a[:, j, :, :], ALU.mult))
                    chain.link(dve.tensor_reduce(wide[0:D, at_a + j * H:at_a + j * H + H], part[:, :, :], AX.X,
                                                 ALU.add))
                if at_mean is not None:
                    chain.link(dve.tensor_reduce(part[:, 0, :], w[:, :, :].rearrange("c h d -> c d h"), AX.X,
                                                 ALU.add))
                    chain.link(dve.tensor_scalar(wide[0:D, at_mean:at_mean + D], part[:, 0, :], 1.0 / heads, None,
                                                 ALU.mult))
                chain.done()

        s_ld.base += 48
        s_dve.base += n_link

    def node_phase(name, kind, loads, stores, width, weights, gat=None, held=None, bias=None, gamma=None,
                   beta=None, gram=None):
        own_rows = kind in ("first", "gat")
        L = 5 if kind == "layer" else 0
        N1 = {"first": 2, "gat": 0, "join": 1, "layer": L + 3, "gcn": 0, "last": 1}[kind]
        to_product = 2 if kind in ("first", "layer") else 1
        product_first = kind in ("first", "layer", "join")
        B = N1 + to_product + 1
        U = 8 if kind in ("first", "layer") else 4
        deep = 2 if held is not None else 4
        normed = kind != "gat" and kind != "gcn"
        row_w = ROW if own_rows else D
        fronts = {"first": 0, "gat": 0, "join": 1, "layer": 1, "gcn": 0, "last": 2}[kind]
        W3 = [P, K, D]
        with ExitStack() as ctx:
            def sb(nm, shape, dt=F32):
                return ctx.enter_context(nc.sbuf_tensor(f"{name}_{nm}", shape, dt))

            ins = [sb(f"in{j}", [P, deep, K, w]) for j, (_, w) in enumerate(loads)]
            R_h = {"first": 8, "join": 2}.get(kind, 4)
            h = sb("h", [P, R_h, K, row_w])
            h_out = {"first": 0, "gat": 0, "last": 1}.get(kind)
            rings = [R_h if j == h_out else deep if j == 0 and fronts else 2 if held is not None else 4
                     for j in range(len(stores))]
            outs = [h if j == h_out else sb(f"out{j}", [P, rings[j], K, w]) for j, (_, w) in enumerate(stores)]
            R_hT = 1 if kind == "join" else 2
            R_pT = 1 if kind == "last" else 2
            hT = sb("hT", [D + 1, R_hT, 2, HALF * P])
            wide = sb("wide", [D + 1, width])
            R_tmp = 8 if kind in ("first", "layer") else 4
            if normed:
                bn = sb("bn", [P, K, 6])
                tmp = sb("tmp", [P, R_tmp, 2 if kind == "layer" else 1, 7, K])
            if gamma is not None:
                gam, bet = sb("gam", [P, D]), sb("bet", [P, D])
            if bias is not None:
                bia = sb("bia", [P, D])
            if kind in ("layer", "gcn", "last"):
                R_mid = 8 if kind == "layer" else 4
                mid = sb("mid", [P, R_mid, K, D])
            if kind == "last":
                zeros = sb("zeros", [P, AGG])
            if kind == "first":
                blank = sb("blank", [P, 2, CLEAR * AGG])
                s_clear = signal("cleared")
            pT = ctx.enter_context(nc.psum_tensor(f"{name}_pT", [D, R_pT, 2, 512], F32))
            pO = ctx.enter_context(nc.psum_tensor(f"{name}_pO", [P, 2, K, 128], F32))

            s_in = [[signal(f"load_{c}{r}") for r in range(deep)] for c in "abc"[:len(loads)]]
            s_out = [[signal(f"store_{c}{r}") for r in range(rings[j])] for j, c in enumerate("abc"[:len(stores)])]
            s_w, s_set, s_front, s_pool = signal("weights"), signal("setup"), signal("front"), signal("pool_ready")
            s_var, s_dev, s_scale = signal("var_ready"), signal("dev_ready"), signal("scale_ready")
            s_var0, s_dev0, s_scale0 = signal("var0_ready"), signal("dev0_ready"), signal("scale0_ready")
            s_norm, s_h, s_tr, s_hT = signal("normed"), signal("h_ready"), signal("turned"), signal("hT_ready")
            s_mm, s_ev, s_ev2 = signal("product_ready"), signal("product_used"), signal("product_used2")
            s_dve, s_dve0, s_pc = signal("dve_chain"), signal("dve_chain0"), signal("pool_chain")
            s_hb, s_gram, s_affine = signal("h_bias"), signal("summed"), signal("affine_ready")
            s_dves, s_dves0 = signal("scale_chain"), signal("scale_chain0")
            used = {"first": s_h, "gat": s_h, "join": s_front, "layer": s_front, "gcn": s_pool, "last": s_front}[kind]

            n_w = sum((m is not None) + (v is not None) for _, m, v in weights) \
                + 2 * (gamma is not None) + (bias is not None)
            with nc.Block() as setup:
                @setup.sync
                def _(sp):
                    sp.wait_ge(s_set.sem, s_set.at(1))
                    for at, m, v in weights:
                        if m is not None:
                            sp.dma_start(wide[0:D, at:at + D], m).then_inc(s_w.sem, 16)
                        if v is not None:
                            sp.dma_start(wide[D:D + 1, at:at + D], row1(v)).then_inc(s_w.sem, 16)
                    if gamma is not None:
                        sp.dma_start(gam[:, :], gamma.partition_broadcast(P)).then_inc(s_w.sem, 16)
                        sp.dma_start(bet[:, :], beta.partition_broadcast(P)).then_inc(s_w.sem, 16)
                    if bias is not None:
                        sp.dma_start(bia[:, :], bias.partition_broadcast(P)).then_inc(s_w.sem, 16)
                    if n_w:
                        sp.wait_ge(s_w.sem, s_w.at(16 * n_w))

                @setup.vector
                def _(dve):
                    dve.memset(hT[:, :, :, :], 1.0)
                    if kind == "last":
                        dve.memset(outs[2][:, :, :, :], 1.0)
                        dve.memset(zeros[:, :], 0.0)
                    if kind == "first":
                        dve.memset(blank[:, :, :], 0.0)
                    dve.memset(wide[:, :], 0.0).then_inc(s_set.sem, 1)
            s_set.base += 1
            s_w.base += 16 * n_w
            if gat is not None:
                gat_weights(name, wide, *gat)

            x_in = [t[:, :, :, 0:D] for t in ins]
            block = ctx.enter_context(nc.Block())

            def over(v):
                return v[:, :].unsqueeze(1).broadcast_to(W3)

            def dinv_of(t):
                return dinv[:, bass.ds(t.s * K, K)].unsqueeze(2).broadcast_to(W3)

            def buf_in(j, t):
                return x_in[j][:, t.c % deep]

            def buf_out(j, t):
                return outs[j][:, t.c % rings[j]]

            def buf_h(t):
                return h[:, t.c % R_h]

            def arrived(eng, t, which):
                for j in which:
                    sg = s_in[j][t.c % deep]
                    eng.wait_ge(sg.sem, sg.at(16 * (t.turn(deep) + 1)))

            def stored(eng, t, j):
                R = rings[j]
                if t.after(R):
                    eng.wait_ge(s_out[j][t.c % R].sem, s_out[j][t.c % R].at(16 * t.turn(R)))

            @block.sync
            def _(sp):
                def load(t, which, used):
                    if t.after(deep):
                        sp.wait_ge(used.sem, used.at(t.s - deep + 1))
                        sp.nop(nofuse=True)
                    for j in which:
                        table, w = loads[j]
                        sp.dma_start(ins[j][:, t.c % deep, :, :],
                                     rows(table, t.s, w)).then_inc(s_in[j][t.c % deep].sem, 16)

                def load_early(t):
                    load(t, (0, 1), s_pool)

                def load_late(t):
                    load(t, (2,), s_front)

                def load_all(t):
                    load(t, range(len(loads)), used)

                def store_front(t):
                    sp.wait_ge(s_front.sem, s_front.at(t.s + 1))
                    sp.nop(nofuse=True)
                    sp.dma_start(rows(stores[0][0], t.s), buf_out(0, t)).then_inc(s_out[0][t.c % rings[0]].sem, 16)

                def store_h(t):
                    if kind == "last":
                        sp.wait_ge(s_h.sem, s_h.at(t.s + 1))
                        sp.nop(nofuse=True)
                        sp.dma_start(rows(stores[1][0], t.s), buf_h(t)).then_inc(s_out[1][t.c % R_h].sem, 16)

                def store_back(t):
                    if kind != "last":
                        sp.wait_ge(s_ev.sem, s_ev.at(t.s + 1))
                        sp.nop(nofuse=True)
                    if kind in ("join", "last"):
                        sp.wait_ge(s_ev2.sem, s_ev2.at(t.s + 1))
                        sp.nop(nofuse=True)
                    for j in range(fronts, len(stores)):
                        sp.dma_start(rows(stores[j][0], t.s), buf_out(j, t)).then_inc(s_out[j][t.c % rings[j]].sem, 16)

                stages = ([(0, load_early), (4, load_late)] if kind == "layer" else [(0, load_all)]) \
                    + ([(L + 1, store_front)] if fronts else []) + ([(N1 + 1, store_h)] if kind == "last" else []) \
                    + [(B + (1 if kind in ("first", "layer") else 2), store_back)]
                pipeline(sp, NSTEP, stages, U)
                for sg in s_out:
                    for r, x in enumerate(sg):
                        sp.wait_ge(x.sem, x.at(16 * len(range(r, NSTEP, len(sg)))))

            @block.vector
            def _(dve):
                def stream_free(t):
                    stored(dve, t, 0)
                    if t.after(rings[0]):
                        dve.wait_ge(s_h.sem, s_h.at(t.s - rings[0] + 1))

                def front(t):
                    if kind == "first":
                        arrived(dve, t, (0,))
                        norm_stats(dve, Chain(dve, s_dve, 3, t.s).link, buf_in(0, t), bn, tmp[:, t.c % R_tmp, 0], s_var)
                    if kind == "gat":
                        arrived(dve, t, (0,))
                        dve.wait_ge(s_pool.sem, s_pool.at(t.s + 1))
                        stored(dve, t, 0)
                        dve.scalar_tensor_tensor(buf_h(t)[:, :, 0:D], held[:, bass.ds(t.s * K, K), :], 0.0,
                                                 buf_in(0, t), ALU.max, ALU.add).then_inc(s_h.sem, 1)
                    if kind == "join":
                        c = Chain(dve, s_dve, 4, t.s)
                        arrived(dve, t, (0, 1))
                        dve.wait_ge(s_pool.sem, s_pool.at(t.s + 1))
                        o = held[:, bass.ds(t.s * K, K), :]
                        c.link(dve.scalar_tensor_tensor(o, o, 0.0, buf_in(0, t), ALU.max, ALU.add))
                        stream_free(t)
                        dve.tensor_tensor(buf_out(0, t), o, buf_in(1, t), ALU.add).then_inc(s_front.sem, 1)
                        dve.wait_ge(s_front.sem, s_front.at(t.s + 1))
                        norm_stats(dve, c.link, buf_out(0, t), bn, tmp[:, t.c % R_tmp, 0], s_var)
                    if kind == "gcn":
                        dve.wait_ge(s_pool.sem, s_pool.at(t.s + 1))
                        dve.tensor_tensor(buf_h(t), mid[:, t.c % R_mid], over(bia), ALU.add).then_inc(s_front.sem, 1)
                    if kind == "last":
                        c = Chain(dve, s_dve, 4, t.s)
                        dve.wait_ge(s_pool.sem, s_pool.at(t.s + 1))
                        c.link(dve.tensor_tensor(mid[:, t.c % R_mid], mid[:, t.c % R_mid], over(bia), ALU.add))
                        arrived(dve, t, (2,))
                        stream_free(t)
                        dve.scalar_tensor_tensor(buf_out(0, t), mid[:, t.c % R_mid], 0.0, buf_in(2, t), ALU.max,
                                                 ALU.add).then_inc(s_front.sem, 1)
                        dve.wait_ge(s_front.sem, s_front.at(t.s + 1))
                        norm_stats(dve, c.link, buf_out(0, t), bn, tmp[:, t.c % R_tmp, 0], s_var)
                    if kind == "layer":
                        c = Chain(dve, s_dve, 3, t.s)
                        dve.wait_ge(s_affine.sem, s_affine.at(t.s + 1))
                        arrived(dve, t, (2,))
                        stream_free(t)
                        dve.scalar_tensor_tensor(buf_out(0, t), mid[:, t.c % R_mid], 0.0, buf_in(2, t), ALU.max,
                                                 ALU.add).then_inc(s_front.sem, 1)
                        dve.wait_ge(s_front.sem, s_front.at(t.s + 1))
                        norm_stats(dve, c.link, buf_out(0, t), bn, tmp[:, t.c % R_tmp, 1], s_var)

                def scale(t):
                    c = Chain(dve, s_dves, 1, t.s)
                    dve.wait_ge(s_dev.sem, s_dev.at(t.s + 1))
                    norm_scale(dve, c.link, tmp[:, t.c % R_tmp, min(L, 1)]).then_inc(s_scale.sem, 1)

                def inner_norm(t):
                    c = Chain(dve, s_dve0, 3, t.s)
                    dve.wait_ge(s_pool.sem, s_pool.at(t.s + 1))
                    norm_stats(dve, c.link, mid[:, t.c % R_mid], bn, tmp[:, t.c % R_tmp, 0], s_var0)

                def inner_scale(t):
                    c = Chain(dve, s_dves0, 1, t.s)
                    dve.wait_ge(s_dev0.sem, s_dev0.at(t.s + 1))
                    norm_scale(dve, c.link, tmp[:, t.c % R_tmp, 0]).then_inc(s_scale0.sem, 1)

                def back(t):
                    ps = pO[:, t.b, :, :]
                    dve.wait_ge(s_mm.sem, s_mm.at(t.s + 1))
                    if own_rows:
                        dve.tensor_copy(buf_h(t)[:, :, D:ROW], ps[:, :, 0:2 * H])
                        stored(dve, t, 1)
                        dve.tensor_copy(buf_out(1, t), ps[:, :, 2 * H:ROW]).then_inc(s_ev.sem, 1)
                    if kind == "join":
                        dve.wait_ge(s_hb.sem, s_hb.at(t.s + 1))
                        dve.tensor_tensor(buf_out(2, t), ps[:, :, 0:D], buf_out(2, t), ALU.add)\
                            .then_inc(s_ev.sem, 1)
                    if kind in ("layer", "gcn"):
                        stored(dve, t, fronts)
                        dve.tensor_tensor(buf_out(fronts, t), ps[:, :, 0:D], dinv_of(t), ALU.mult)\
                            .then_inc(s_ev.sem, 1)

                stages = {
                    "first": [(2, scale), (B, back), (0, front)],
                    "gat": [(0, front), (B, back)],
                    "join": [(1, scale), (0, front), (B, back)],
                    "layer": [(2, inner_scale), (L + 2, scale), (B, back), (0, inner_norm), (L, front)],
                    "gcn": [(0, front), (B, back)],
                    "last": [(1, scale), (0, front)],
                }[kind]
                pipeline(dve, NSTEP, stages, U)

            @block.scalar
            def _(act):
                def root(t, j, var, dev):
                    act.wait_ge(var.sem, var.at(t.s + 1))
                    nc.scalar.activation(tmp[:, t.c % R_tmp, j, 4, :], tmp[:, t.c % R_tmp, j, 3, :], ACT.Sqrt, scale=1.0 / D,
                                         bias=eps_col[:, :]).then_inc(dev.sem, 1)

                def apply(t, j, x, y, func, ready, done):
                    act.wait_ge(ready.sem, ready.at(t.s + 1))
                    for k in range(K):
                        last = nc.scalar.activation(y[:, k, 0:D], x[:, k, 0:D], func,
                                                    scale=tmp[:, t.c % R_tmp, j, 5, k:k + 1],
                                                    bias=tmp[:, t.c % R_tmp, j, 6, k:k + 1])
                    last.then_inc(done.sem, 1)

                def root_last(t):
                    root(t, min(L, 1), s_var, s_dev)

                def norm_last(t):
                    if h_out is not None:
                        stored(act, t, h_out)
                    if kind == "join" and t.after(2):
                        act.wait_ge(s_hb.sem, s_hb.at(t.s - 1))
                    x = buf_in(0, t) if kind == "first" else buf_out(0, t)
                    apply(t, min(L, 1), x, buf_h(t), ACT.Relu, s_scale, s_h)

                def root_inner(t):
                    root(t, 0, s_var0, s_dev0)

                def norm_inner(t):
                    apply(t, 0, mid[:, t.c % R_mid], mid[:, t.c % R_mid], ACT.Identity, s_scale0, s_norm)

                def relu(t):
                    act.wait_ge(s_front.sem, s_front.at(t.s + 1))
                    nc.scalar.activation(buf_h(t), buf_h(t), ACT.Relu).then_inc(s_h.sem, 1)

                def evacuate(t):
                    act.wait_ge(s_tr.sem, s_tr.at(t.s + 1))
                    if t.after(R_hT):
                        act.wait_ge(s_mm.sem, s_mm.at(t.s + 1 - R_hT))
                    nc.scalar.copy(hT[0:D, t.c % R_hT, :, :], pT[:, t.c % R_pT, :, 0:HALF * P]).then_inc(s_hT.sem, 1)

                def back(t):
                    if kind == "join":
                        stored(act, t, 1)
                        act.wait_ge(s_ev.sem, s_ev.at(t.s + 1))
                        nc.scalar.copy(buf_out(1, t), pO[:, t.b, :, 0:ROW]).then_inc(s_ev2.sem, 1)
                    else:
                        stored(act, t, 2)
                        if t.after(2):
                            act.wait_ge(s_gram.sem, s_gram.at(t.s - 1))
                        act.wait_ge(s_mm.sem, s_mm.at(t.s + 1))
                        nc.scalar.activation(buf_out(2, t)[:, :, 0:D], pO[:, t.b, :, 0:D], ACT.Relu)\
                            .then_inc(s_ev2.sem, 1)

                stages = {
                    "first": [(1, root_last), (3, evacuate), (2, norm_last)],
                    "gat": [(1, evacuate)],
                    "join": [(2, evacuate), (1, norm_last), (0, root_last), (B, back)],
                    "layer": [(1, root_inner), (L + 1, root_last), (3, norm_inner), (N1 + 1, evacuate),
                              (N1, norm_last)],
                    "gcn": [(0, relu), (1, evacuate)],
                    "last": [(1, norm_last), (2, evacuate), (0, root_last), (B, back)],
                }[kind]
                pipeline(act, NSTEP, stages, U)

            @block.tensor
            def _(pe):
                def turn(t):
                    pe.wait_ge(s_h.sem, s_h.at(t.s + 1))
                    if t.after(R_pT):
                        pe.wait_ge(s_hT.sem, s_hT.at(t.s + 1 - R_pT))
                    for k in range(K):
                        last = pe.transpose(pT[:, t.c % R_pT, k // HALF, (k % HALF) * P:(k % HALF + 1) * P],
                                            buf_h(t)[:, k, 0:D], ident[0:P, 0:P])
                    last.then_inc(s_tr.sem, 1)

                def product(t):
                    pe.wait_ge(s_hT.sem, s_hT.at(t.s + 1))
                    if t.after(2):
                        if kind != "last":
                            pe.wait_ge(s_ev.sem, s_ev.at(t.s - 1))
                        if kind in ("join", "last"):
                            pe.wait_ge(s_ev2.sem, s_ev2.at(t.s - 1))
                    for k in range(K):
                        last = pe.matmul(pO[:, t.b, k, 0:width],
                                         hT[:, t.c % R_hT, k // HALF, (k % HALF) * P:(k % HALF + 1) * P],
                                         wide[:, :], start=True, stop=True)
                    last.then_inc(s_mm.sem, 1)

                def sums_of(t):
                    pe.wait_ge(s_ev2.sem, s_ev2.at(t.s + 1))
                    gram_step(pe, gram, buf_out(2, t)).then_inc(s_gram.sem, 1)

                if kind == "last":
                    gram_edge(pe, gram, zeros, True)
                both = [(N1, turn), (N1 + to_product, product)]
                pipeline(pe, NSTEP, (both[::-1] if product_first else both)
                         + ([(B + 1, sums_of)] if kind == "last" else []), U)
                if kind == "last":
                    gram_edge(pe, gram, zeros, False)

            if kind == "first":
                @block.gpsimd
                def _(pool):
                    table = t_agg.rearrange("(p t) d -> p (t d)", t=(N + SPARE) // P)
                    w = 2 * CLEAR * AGG
                    for c in range(8):
                        if c:
                            pool.wait_ge(s_h.sem, s_h.at(6 * c))
                        pool.dma_start(table[:, c * w:(c + 1) * w].rearrange("p (a w) -> p a w", a=2),
                                       blank[:, :, :]).then_inc(s_clear.sem, 16)
                    pool.wait_ge(s_clear.sem, s_clear.at(16 * 8))
            else:
                @block.gpsimd
                def _(pool):
                    def batch_norm(t):
                        c = Chain(pool, s_pc, 1, t.s)
                        o = held[:, bass.ds(t.s * K, K), :]
                        c.link(pool.tensor_tensor(o, o, over(bn_s), ALU.mult))
                        pool.nop(nofuse=True)
                        pool.tensor_tensor(o, o, over(bn_t), ALU.add).then_inc(s_pool.sem, 1)

                    def add_bias(t):
                        pool.wait_ge(s_h.sem, s_h.at(t.s + 1))
                        stored(pool, t, 2)
                        pool.tensor_tensor(buf_out(2, t), buf_h(t), over(bia), ALU.add).then_inc(s_hb.sem, 1)

                    def affine(t):
                        c = Chain(pool, s_pc, 1, t.s)
                        pool.wait_ge(s_norm.sem, s_norm.at(t.s + 1))
                        c.link(pool.tensor_tensor(mid[:, t.c % R_mid], mid[:, t.c % R_mid], over(gam), ALU.mult))
                        pool.nop(nofuse=True)
                        pool.tensor_tensor(mid[:, t.c % R_mid], mid[:, t.c % R_mid], over(bet), ALU.add)\
                            .then_inc(s_affine.sem, 1)

                    def add_aggregate(t):
                        arrived(pool, t, (0, 1))
                        if t.after(R_mid):
                            pool.wait_ge(s_front.sem, s_front.at(t.s + 1 - R_mid))
                        ins_ = pool.tensor_tensor(mid[:, t.c % R_mid], buf_in(0, t), buf_in(1, t), ALU.add)
                        if kind == "layer":
                            ins_.then_inc(s_pool.sem, 1)
                        else:
                            Chain(pool, s_pc, 1, t.s).link(ins_)
                            pool.nop(nofuse=True)
                            pool.tensor_tensor(mid[:, t.c % R_mid], mid[:, t.c % R_mid], dinv_of(t), ALU.mult)\
                                .then_inc(s_pool.sem, 1)

                    pipeline(pool, NSTEP, {"gat": [(0, batch_norm)], "join": [(0, batch_norm), (3, add_bias)],
                                            "layer": [(0, add_aggregate), (4, affine)]}
                             .get(kind, [(0, add_aggregate)]), U)

        for sg in s_in + s_out:
            for r, x in enumerate(sg):
                x.base += 16 * len(range(r, NSTEP, len(sg)))
        once = [s_tr, s_hT, s_mm, s_h]
        if normed:
            once += [s_var, s_dev, s_scale, s_dves]
            s_dve.base += {"first": 3, "join": 4, "layer": 3, "last": 4}[kind] * NSTEP
        if kind != "last":
            once += [s_ev]
        if kind in ("join", "last"):
            once += [s_ev2]
        if kind not in ("first", "gat"):
            once += [s_front]
        if kind != "first":
            once += [s_pool]
        if kind != "first":
            once += [s_pc]
        if kind == "join":
            once += [s_hb]
        if kind == "last":
            once += [s_gram]
        if kind == "layer":
            once += [s_var0, s_dev0, s_scale0, s_norm, s_dves0, s_affine]
            s_dve0.base += 3 * NSTEP
        for x in once:
            x.base += NSTEP

    def gram_step(pe, gram, x):
        for k in range(K):
            last = pe.matmul(gram, x[:, k, 0:D], x[:, k, 0:AGG], start=False, stop=False)
        return last

    def gram_edge(pe, gram, zeros, start):
        pe.matmul(gram, zeros[:, 0:D], zeros[:, :], start=start, stop=not start)

    def aggregate_phase(name, held, with_count, gram):
        with ExitStack() as ctx:
            c = ctx.enter_context(nc.sbuf_tensor(f"{name}_c", [P, 4, K, AGG], F32))
            zeros = ctx.enter_context(nc.sbuf_tensor(f"{name}_zeros", [P, AGG], F32))
            s_y = [signal(f"store_a{b}") for b in range(4)]
            s_c = [signal(f"store_b{b}") for b in range(4)]
            s_h, s_st, s_z, s_cp = signal("h_ready"), signal("summed"), signal("setup"), signal("pool_ready")
            s_dve, s_root, s_one = signal("dve_chain"), signal("dev_ready"), signal("front")
            block = ctx.enter_context(nc.Block())

            @block.sync
            def _(sp):
                def load(t):
                    if t.after(4):
                        sp.wait_ge(s_cp.sem, s_cp.at(t.s - 3))
                        sp.nop(nofuse=True)
                        sp.wait_ge(s_st.sem, s_st.at(t.s - 3))
                        sp.nop(nofuse=True)
                    sp.dma_start(held[:, bass.ds(t.s * K, K), :], rows(d_y, t.s)).then_inc(s_y[t.c % 4].sem, 16)
                    sp.dma_start(c[:, t.c % 4], rows(t_agg, t.s)).then_inc(s_c[t.c % 4].sem, 16)

                pipeline(sp, NSTEP, [(0, load)], 4)

            @block.vector
            def _(dve):
                dve.memset(zeros[:, :], 0.0).then_inc(s_z.sem, 1)

                def add(t):
                    dve.wait_ge(s_y[t.c % 4].sem, s_y[t.c % 4].at(16 * (t.turn(4) + 1)))
                    dve.wait_ge(s_c[t.c % 4].sem, s_c[t.c % 4].at(16 * (t.turn(4) + 1)))
                    if with_count:
                        dve.tensor_copy(count[:, bass.ds(t.s * K, K)], c[:, t.c % 4, :, D]).then_inc(s_dve.sem, 1)
                        dve.wait_ge(s_dve.sem, s_dve.at(t.s + 1))
                    dve.memset(c[:, t.c % 4, :, D], 1.0)
                    dve.tensor_tensor(c[:, t.c % 4, :, 0:D], c[:, t.c % 4, :, 0:D], held[:, bass.ds(t.s * K, K), :],
                                      ALU.add).then_inc(s_h.sem, 1)

                pipeline(dve, NSTEP, [(0, add)], 4)
                if with_count:
                    dve.tensor_scalar(dinv[:, :], count[:, :], 1.0, None, ALU.add).then_inc(s_one.sem, 1)
                    dve.wait_ge(s_root.sem, s_root.at(1))
                    dve.reciprocal(dinv[:, :], dinv[:, :])

            @block.scalar
            def _(act):
                def keep(t):
                    act.wait_ge(s_h.sem, s_h.at(t.s + 1))
                    nc.scalar.copy(held[:, bass.ds(t.s * K, K), :], c[:, t.c % 4, :, 0:D]).then_inc(s_cp.sem, 1)

                pipeline(act, NSTEP, [(0, keep)], 4)
                if with_count:
                    act.wait_ge(s_one.sem, s_one.at(1))
                    nc.scalar.activation(dinv[:, :], dinv[:, :], ACT.Sqrt).then_inc(s_root.sem, 1)

            @block.tensor
            def _(pe):
                pe.wait_ge(s_z.sem, s_z.at(1))
                gram_edge(pe, gram, zeros, True)

                def add_up(t):
                    pe.wait_ge(s_h.sem, s_h.at(t.s + 1))
                    gram_step(pe, gram, c[:, t.c % 4]).then_inc(s_st.sem, 1)

                pipeline(pe, NSTEP, [(0, add_up)], 4)
                gram_edge(pe, gram, zeros, False)

        for sg in s_y, s_c:
            for r, x in enumerate(sg):
                x.base += 16 * len(range(r, NSTEP, 4))
        s_z.base += 1
        for x in (s_h, s_st, s_cp):
            x.base += NSTEP
        if with_count:
            s_root.base += 1
            s_one.base += 1
            s_dve.base += NSTEP

    GATHER = bass.IndirectOffsetOnAxis

    def gather_step(pool, chain, s, parts):
        for idx, ring_idx, _, _, _, _ in parts:
            ins = pool.tensor_copy(ring_idx, idx[:, bass.ds(s * K, K)])
            chain.k += 1
            ins.then_inc(chain.sig.sem, 1)
        pool.wait_ge(chain.sig.sem, chain.sig.at(chain.per * s + chain.k))
        pool.nop(nofuse=True)
        for _, ring_idx, table, ring, w, sig in parts:
            for k in range(K):
                pool.indirect_dma_start(out=ring[:, k, 0:w], out_offset=None, in_=table,
                                        in_offset=GATHER(ap=ring_idx[:, k:k + 1], axis=0)).then_inc(sig.sem, 16)

    def scatter_step(pool, chain, ring_idx, sums, sig, step):
        chain.link(pool.tensor_copy(ring_idx, out_idx[:, bass.ds(step * K, K)]))
        pool.nop(nofuse=True)
        for k in range(K):
            pool.indirect_dma_start(out=t_agg, out_offset=GATHER(ap=ring_idx[:, k:k + 1], axis=0),
                                    in_=sums[:, k, :], in_offset=None).then_inc(sig.sem, 16)

    def run_sums(dve, chain, s, b, ks, sums, same, msg, s_m):
        for k in ks:
            prev = sums[:, b, k - 1, :] if k else sums[:, 1 - b, K - 1, :]
            ins = dve.scalar_tensor_tensor(sums[:, b, k, :], prev, same[:, b, k:k + 1], msg[:, k, :],
                                           ALU.mult, ALU.add)
            if k < K - 1:
                chain.link(ins)
            else:
                ins.then_inc(s_m.sem, 1)
                dve.wait_ge(s_m.sem, s_m.at(s + 1))

    def close_segments(name, tail):
        with ExitStack() as ctx:
            carry = ctx.enter_context(nc.sbuf_tensor(f"{name}_before", [P, AGG], F32))
            row = ctx.enter_context(nc.sbuf_tensor(f"{name}_row", [P, 2, AGG], F32))
            pc = ctx.enter_context(nc.psum_tensor(f"{name}_pc", [P, AGG], F32))
            s_pe, s_dve, s_g, s_s = signal("pe_done"), signal("dve_chain"), signal("gather_a0"), signal("scatter_0")
            block = ctx.enter_context(nc.Block())

            @block.tensor
            def _(pe):
                pe.matmul(pc[:, :], mask_f[:, :], tail, start=True, stop=True).then_inc(s_pe.sem, 1)

            @block.vector
            def _(dve):
                dve.wait_ge(s_pe.sem, s_pe.at(1))
                dve.tensor_copy(carry[:, :], pc[:, :]).then_inc(s_dve.sem, 1)
                dve.wait_ge(s_g.sem, s_g.at(16))
                dve.wait_ge(s_dve.sem, s_dve.at(1))
                dve.tensor_tensor(row[:, 1, :], row[:, 0, :], carry[:, :], ALU.add).then_inc(s_dve.sem, 1)

            @block.gpsimd
            def _(pool):
                pool.indirect_dma_start(out=row[:, 0, :], out_offset=None, in_=t_agg,
                                        in_offset=GATHER(ap=fix_idx[:, :], axis=0)).then_inc(s_g.sem, 16)
                pool.wait_ge(s_dve.sem, s_dve.at(2))
                pool.nop(nofuse=True)
                pool.indirect_dma_start(out=t_agg, out_offset=GATHER(ap=fix_idx[:, :], axis=0), in_=row[:, 1, :],
                                        in_offset=None).then_inc(s_s.sem, 16)
                pool.wait_ge(s_s.sem, s_s.at(16))

        s_pe.base += 1
        s_dve.base += 2
        s_g.base += 16
        s_s.base += 16

    def softmax(name, e, e_self, alpha, factor):
        with ExitStack() as ctx:
            def sb(nm, shape):
                return ctx.enter_context(nc.sbuf_tensor(f"{name}_{nm}", shape, F32))

            fw, bw, den = sb("fw", [P, H, ET]), sb("bw", [P, H, ET]), sb("den", [P, H, ET])
            rep, cand = sb("rep", [P, 2, H, P]), sb("cand", [P, 2, H, P])
            ends, carry = sb("ends", [P, 2, H]), sb("carry", [P, 2, H])
            turned = ctx.enter_context(nc.psum_tensor(f"{name}_turned", [P, 2, 512], F32))
            summed = ctx.enter_context(nc.psum_tensor(f"{name}_summed", [P, 2, H], F32))
            s_dve, s_pe, s_exp = signal("dve_chain"), signal("pe_done"), signal("act_done")
            n_link = 18
            block = ctx.enter_context(nc.Block())

            @block.vector
            def _(dve):
                c = Chain(dve, s_dve, n_link)

                def scans(data, gate_f, gate_b, op0, op1, init):
                    for h in range(H):
                        a, b = (init, init) if isinstance(init, float) else (init[:, 0, h:h + 1], init[:, 1, h:h + 1])
                        dve.tensor_tensor_scan(fw[:, h, :], gate_f[:, :], data[:, h, :], a, op0, op1)
                        last = dve.tensor_tensor_scan(bw[:, h, ::-1], gate_b[:, ::-1], data[:, h, ::-1], b, op0, op1)
                    return last

                dve.scalar_tensor_tensor(e, e, SLOPE, e, ALU.mult, ALU.max)
                c.link(dve.scalar_tensor_tensor(e_self, e_self, SLOPE, e_self, ALU.mult, ALU.max))
                c.link(scans(e, pen_f, pen_b, ALU.add, ALU.max, -BIG))
                for h in range(H):
                    dve.tensor_scalar(rep[:, 0, h, :], ones[0:P, 0:P], fw[:, h, ET - 1:ET], None, ALU.mult)
                    last = dve.tensor_scalar(rep[:, 1, h, :], ones[0:P, 0:P], bw[:, h, 0:1], None, ALU.mult)
                c.link(last)
                dve.wait_ge(s_pe.sem, s_pe.at(1))
                for j, far in enumerate((far_f, far_b)):
                    last = dve.tensor_tensor(cand[:, j, :, :], turned[:, j, 0:H * P].rearrange("p (h q) -> p h q", h=H),
                                             far[:, :].unsqueeze(1).broadcast_to([P, H, P]), ALU.add)
                c.link(last)
                c.link(dve.tensor_reduce(carry[:, :, :], cand[:, :, :, :], AX.X, ALU.max))
                c.link(scans(e, pen_f, pen_b, ALU.add, ALU.max, carry))
                c.link(dve.tensor_tensor(fw[:, :, :], fw[:, :, :], bw[:, :, :], ALU.max))
                c.link(dve.tensor_tensor(fw[:, :, :], fw[:, :, :], e_self, ALU.max))
                dve.tensor_tensor(e, e, fw[:, :, :], ALU.subtract)
                c.link(dve.tensor_tensor(e_self, e_self, fw[:, :, :], ALU.subtract))
                dve.wait_ge(s_exp.sem, s_exp.at(1))
                c.link(scans(e, same_f, same_b, ALU.mult, ALU.add, 0.0))
                dve.tensor_copy(ends[:, 0, :], fw[:, :, ET - 1])
                c.link(dve.tensor_copy(ends[:, 1, :], bw[:, :, 0]))
                dve.wait_ge(s_pe.sem, s_pe.at(2))
                c.link(dve.tensor_copy(carry[:, :, :], summed[:, :, :]))
                c.link(scans(e, same_f, same_b, ALU.mult, ALU.add, carry))
                c.link(dve.tensor_tensor(den[:, :, :], fw[:, :, :], bw[:, :, :], ALU.add))
                c.link(dve.tensor_tensor(den[:, :, :], den[:, :, :], e, ALU.subtract))
                c.link(dve.scalar_tensor_tensor(den[:, :, :], den[:, :, :], 1e-16, e_self, ALU.add, ALU.add))
                c.link(dve.reciprocal(den[:, :, :], den[:, :, :]))
                c.link(dve.scalar_tensor_tensor(alpha, e, factor, den[:, :, :], ALU.mult, ALU.mult))
                c.done()

            @block.scalar
            def _(act):
                act.wait_ge(s_dve.sem, s_dve.at(9))
                nc.scalar.activation(e, e, ACT.Exp)
                nc.scalar.activation(e_self, e_self, ACT.Exp).then_inc(s_exp.sem, 1)

            @block.tensor
            def _(pe):
                pe.wait_ge(s_dve.sem, s_dve.at(3))
                for j in range(2):
                    for h in range(H):
                        last = pe.transpose(turned[:, j, h * P:(h + 1) * P], rep[:, j, h, :], ident[0:P, 0:P])
                last.then_inc(s_pe.sem, 1)
                pe.wait_ge(s_dve.sem, s_dve.at(11))
                pe.matmul(summed[:, 0, :], mask_f[:, :], ends[:, 0, :], start=True, stop=True)
                pe.matmul(summed[:, 1, :], mask_b[:, :], ends[:, 1, :], start=True, stop=True).then_inc(s_pe.sem, 1)

        s_dve.base += n_link
        s_pe.base += 2
        s_exp.base += 1

    def gat_edges(name, table, W):
        with ExitStack() as outer:
            def sbo(nm, shape, dt=F32):
                return outer.enter_context(nc.sbuf_tensor(f"{name}_{nm}", shape, dt))

            if W is None:
                z = sbo("z", [P, ET, D])
            else:
                zT = sbo("zT", [D, 2 * ESTEP, HALF * P])
            e, e_self, alpha = sbo("e", [P, H, ET]), sbo("es", [P, H, ET]), sbo("alpha", [P, H, ET])
            with ExitStack() as ctx:
                xs = ctx.enter_context(nc.sbuf_tensor(f"{name}_xs", [P, 2, K, ROW], F32))
                xd = ctx.enter_context(nc.sbuf_tensor(f"{name}_xd", [P, 2, K, ROW], F32))
                idx = ctx.enter_context(nc.sbuf_tensor(f"{name}_idx", [P, 2, 2, K], I32))
                s_g = [[signal(f"gather_{c}{b}") for b in range(2)] for c in "ab"]
                s_pool, s_used = signal("pool_chain"), signal("inputs_used")
                s_tr, s_hT = signal("turned"), signal("hT_ready")
                if W is not None:
                    zr = ctx.enter_context(nc.sbuf_tensor(f"{name}_zr", [P, 2, K, D], F32))
                    pT = ctx.enter_context(nc.psum_tensor(f"{name}_pT", [D, 2, 2, 512], F32))
                block = ctx.enter_context(nc.Block())

                @block.gpsimd
                def _(pool):
                    def body(s, b, q, first):
                        if first is None:
                            pool.wait_ge(s_used.sem, s_used.at(s - 1))
                        gather_step(pool, Chain(pool, s_pool, 2, s), s,
                                    [(src_idx, idx[:, b, 0, :], table, xs[:, b], ROW, s_g[0][b]),
                                     (dst_idx, idx[:, b, 1, :], table, xd[:, b], ROW, s_g[1][b])])

                    steps(pool, ESTEP, body)

                @block.vector
                def _(dve):
                    def body(s, b, q, first):
                        for sg in s_g:
                            dve.wait_ge(sg[b].sem, sg[b].at(16 * K * (q + 1)))
                        at = bass.ds(s * K, K)
                        if W is not None and first is None:
                            dve.wait_ge(s_tr.sem, s_tr.at(s - 1))
                        dve.tensor_tensor(z[:, at, :] if W is None else zr[:, b], xs[:, b, :, 0:D],
                                          xd[:, b, :, 0:D], ALU.subtract)
                        dve.tensor_tensor(e[:, :, at], xs[:, b, :, D:D + H].rearrange("p k h -> p h k"),
                                          xd[:, b, :, D + H:ROW].rearrange("p k h -> p h k"), ALU.add)
                        dve.tensor_tensor(e_self[:, :, at], xd[:, b, :, D:D + H].rearrange("p k h -> p h k"),
                                          xd[:, b, :, D + H:ROW].rearrange("p k h -> p h k"),
                                          ALU.add).then_inc(s_used.sem, 1)

                    steps(dve, ESTEP, body)

                if W is not None:
                    @block.tensor
                    def _(pe):
                        def turn(t):
                            pe.wait_ge(s_used.sem, s_used.at(t.s + 1))
                            if t.after(2):
                                pe.wait_ge(s_hT.sem, s_hT.at(t.s - 1))
                            for k in range(K):
                                last = pe.transpose(pT[:, t.b, k // HALF, (k % HALF) * P:(k % HALF + 1) * P],
                                                    zr[:, t.b, k, :], ident[0:P, 0:P])
                            last.then_inc(s_tr.sem, 1)

                        pipeline(pe, ESTEP, [(0, turn)])

                    @block.scalar
                    def _(act):
                        def keep(t):
                            act.wait_ge(s_tr.sem, s_tr.at(t.s + 1))
                            nc.scalar.copy(zT[:, bass.ds(2 * t.s, 2), :],
                                           pT[:, t.b, :, 0:HALF * P]).then_inc(s_hT.sem, 1)

                        pipeline(act, ESTEP, [(0, keep)])

            if W is not None:
                s_tr.base += ESTEP
                s_hT.base += ESTEP
            for sg in s_g:
                sg[0].base += 16 * K * ((ESTEP + 1) // 2)
                sg[1].base += 16 * K * (ESTEP // 2)
            s_pool.base += 2 * ESTEP
            s_used.base += ESTEP

            softmax(name, e[:, :, :], e_self[:, :, :], alpha[:, :, :], 1.0 / H if W is not None else 1.0)

            sums = sbo("sums", [P, 2, K, AGG])
            with ExitStack() as ctx:
                def sb(nm, shape, dt=F32):
                    return ctx.enter_context(nc.sbuf_tensor(f"{name}_{nm}", shape, dt))

                idx = sb("sidx", [P, 2, K], I32)
                al = sb("al", [P, 2, K, H])
                msg = sb("msg", [P, 2, K, AGG])
                same = sb("same", [P, 4, K])
                s_sc = [signal(f"scatter_{b}") for b in range(2)]
                s_pool, s_dve, s_m, s_set = signal("pool_chain"), signal("dve_chain"), signal("sums_ready"), signal("setup")
                s_zc, s_tr, s_hT, s_mm = signal("h_ready"), signal("turned"), signal("hT_ready"), signal("product_ready")
                s_ev, s_w, s_al, s_part = signal("product_used"), signal("weights"), signal("front"), signal("normed")
                if W is not None:
                    zc = sb("zc", [D, 2, 2, HALF * P])
                    w = sb("w", [D, H * D])
                    pY = ctx.enter_context(nc.psum_tensor(f"{name}_pY", [P, K, 512], F32))
                    links = 2 * (H - 2) + (K - 1)
                else:
                    links = 2 + 1 + (K - 1)
                block = ctx.enter_context(nc.Block())

                @block.gpsimd
                def _(pool):
                    def body(s, b, q, first):
                        pool.wait_ge(s_m.sem, s_m.at(s + 1))
                        scatter_step(pool, Chain(pool, s_pool, 1, s), idx[:, b, :], sums[:, b], s_sc[b], s)

                    steps(pool, ESTEP, body)
                    pool.wait_ge(s_sc[0].sem, s_sc[0].at(16 * K * ((ESTEP + 1) // 2)))
                    pool.wait_ge(s_sc[1].sem, s_sc[1].at(16 * K * (ESTEP // 2)))

                @block.vector
                def _(dve):
                    dve.memset(msg[:, :, :, :], 1.0)
                    dve.memset(sums[:, :, :, :], 0.0).then_inc(s_set.sem, 1)
                    dve.wait_ge(s_set.sem, s_set.at(1))

                    def body(s, b, q, first):
                        c = Chain(dve, s_dve, links, s)
                        at = bass.ds(s * K, K)
                        c.link(dve.tensor_copy(al[:, b, :, :], alpha[:, :, at].rearrange("p h k -> p k h")))
                        c.link(dve.tensor_copy(same[:, b, :], same_f[:, at]))
                        if first is None:
                            dve.wait_ge(s_sc[b].sem, s_sc[b].at(16 * K * q))
                        c.link(dve.tensor_tensor(
                            msg[:, b, :, 0:D].rearrange("p k (h c) -> p k h c", h=H),
                            z[:, at, :].rearrange("p k (h c) -> p k h c", h=H),
                            al[:, b, :, :].unsqueeze(3).broadcast_to([P, K, H, DH]), ALU.mult))
                        run_sums(dve, c, s, b, range(K), sums, same, msg[:, b], s_m)
                        c.done()

                    def gates(t):
                        at = bass.ds(t.s * K, K)
                        dve.tensor_copy(al[:, t.b, :, :], alpha[:, :, at].rearrange("p h k -> p k h"))
                        dve.tensor_copy(same[:, t.c % 4, :], same_f[:, at]).then_inc(s_al.sem, 1)

                    def one_sum(c, t, k):
                        if k == 0:
                            if t.after(1):
                                dve.wait_ge(s_m.sem, s_m.at(t.s))
                            if t.after(2):
                                dve.wait_ge(s_sc[t.b].sem, s_sc[t.b].at(16 * K * t.q))
                        else:
                            dve.wait_ge(s_dve.sem, c.before)
                        prev = sums[:, t.b, k - 1, :] if k else sums[:, 1 - t.b, K - 1, :]
                        ins = dve.scalar_tensor_tensor(sums[:, t.b, k, :], prev, same[:, t.c % 4, k:k + 1],
                                                       msg[:, t.b, k, :], ALU.mult, ALU.add)
                        if k < K - 1:
                            c.k += 1
                            ins.then_inc(s_dve.sem, 1)
                            c.before = s_dve.at(c.per * c.step + c.k)
                        else:
                            ins.then_inc(s_m.sem, 1)

                    def heads(t):
                        c = Chain(dve, s_dve, links, t.s)
                        c.k = 0 if t.c == 0 else -(HALF - 1)
                        dve.wait_ge(s_al.sem, s_al.at(t.s + 1))
                        for g in range(2):
                            ago = (t, 0) if g else (t.before, HALF) if t.c else None
                            c.before = s_dve.at(c.per * c.step + c.k) if t.c or g else None
                            dve.wait_ge(s_part.sem, s_part.at(2 * t.s + g + 1))
                            for h in range(1, H):
                                for k in range(g * HALF, (g + 1) * HALF):
                                    ins = dve.scalar_tensor_tensor(
                                        msg[:, t.b, k, 0:D], pY[:, k, h * D:(h + 1) * D], al[:, t.b, k, h:h + 1],
                                        msg[:, t.b, k, 0:D], ALU.mult, ALU.add)
                                if h < H - 1:
                                    c.k += 1
                                    ins.then_inc(s_dve.sem, 1)
                                    head = s_dve.at(c.per * c.step + c.k)
                                    if ago:
                                        one_sum(c, ago[0], ago[1] + h - 1)
                                    dve.wait_ge(s_dve.sem, head)
                                else:
                                    ins.then_inc(s_ev.sem, 1)
                            if ago:
                                one_sum(c, ago[0], ago[1] + 2)
                                one_sum(c, ago[0], ago[1] + 3)
                            dve.wait_ge(s_ev.sem, s_ev.at(2 * t.s + g + 1))

                    if W is None:
                        steps(dve, ESTEP, body)
                    else:
                        pipeline(dve, ESTEP, [(0, gates), (1, heads)], 4)
                        c = Chain(dve, s_dve, links, ESTEP)
                        c.k = -(HALF - 1)
                        c.before = s_dve.at(c.per * c.step + c.k)
                        for k in range(HALF, K):
                            one_sum(c, Step(None, ESTEP - 1, 4), k)
                        dve.wait_ge(s_m.sem, s_m.at(ESTEP))

                if W is not None:
                    @block.sync
                    def _(sp):
                        sp.dma_start(w[:, :], W).then_inc(s_w.sem, 16)

                    @block.scalar
                    def _(act):
                        act.wait_ge(s_set.sem, s_set.at(1))

                        def fetch(t):
                            if t.after(2):
                                act.wait_ge(s_mm.sem, s_mm.at(2 * (t.s - 1)))
                            nc.scalar.copy(zc[:, t.b], zT[:, bass.ds(2 * t.s, 2), :]).then_inc(s_zc.sem, 1)

                        def head0(t):
                            act.wait_ge(s_al.sem, s_al.at(t.s + 1))
                            if t.after(2):
                                act.wait_ge(s_m.sem, s_m.at(t.s - 1))
                            for g in range(2):
                                act.wait_ge(s_mm.sem, s_mm.at(2 * t.s + g + 1))
                                for k in range(g * HALF, (g + 1) * HALF):
                                    last = nc.scalar.activation(msg[:, t.b, k, 0:D], pY[:, k, 0:D], ACT.Copy,
                                                                scale=al[:, t.b, k, 0:1])
                                last.then_inc(s_part.sem, 1)

                        pipeline(act, ESTEP, [(0, fetch), (1, head0)])

                    @block.tensor
                    def _(pe):
                        pe.wait_ge(s_w.sem, s_w.at(16))

                        def product(t):
                            pe.wait_ge(s_zc.sem, s_zc.at(t.s + 1))
                            for g in range(2):
                                if t.after(1):
                                    pe.wait_ge(s_ev.sem, s_ev.at(2 * (t.s - 1) + g + 1))
                                for k in range(g * HALF, (g + 1) * HALF):
                                    last = pe.matmul(pY[:, k, 0:H * D],
                                                     zc[:, t.b, g, (k % HALF) * P:(k % HALF + 1) * P], w[:, :],
                                                     start=True, stop=True)
                                last.then_inc(s_mm.sem, 1)

                        pipeline(pe, ESTEP, [(0, product)])

            s_sc[0].base += 16 * K * ((ESTEP + 1) // 2)
            s_sc[1].base += 16 * K * (ESTEP // 2)
            s_pool.base += ESTEP
            s_dve.base += links * ESTEP
            s_m.base += ESTEP
            s_set.base += 1
            if W is not None:
                s_w.base += 16
                s_zc.base += ESTEP
                s_al.base += ESTEP
                s_part.base += 2 * ESTEP
                s_mm.base += 2 * ESTEP
                s_ev.base += 2 * ESTEP
            close_segments(name + "_close", sums[:, (ESTEP - 1) % 2, K - 1, :])

    def gcn_edges(name, table, mlp=None):
        with ExitStack() as ctx:
            def sb(nm, shape, dt=F32):
                return ctx.enter_context(nc.sbuf_tensor(f"{name}_{nm}", shape, dt))

            sums = sb("sums", [P, 2, K, AGG])
            x = sb("x", [P, 2, K, AGG])
            same = sb("same", [P, 2, K])
            idx = sb("idx", [P, 2, 2, K], I32)
            s_g = [signal(f"gather_a{b}") for b in range(2)]
            s_sc = [signal(f"scatter_{b}") for b in range(2)]
            s_pool, s_dve, s_m, s_set = signal("pool_chain"), signal("dve_chain"), signal("sums_ready"), signal("setup")
            links = 1 + (K - 1)
            with nc.Block() as block:
                @block.gpsimd
                def _(pool):
                    pool.wait_ge(s_set.sem, s_set.at(1))
                    pool.nop(nofuse=True)

                    def body(s, b, q, first):
                        c = Chain(pool, s_pool, 2, s)
                        c.k = 0 if first == 0 else -1
                        gather_step(pool, c, s, [(src_idx, idx[:, b, 0, :], table, x[:, b], D, s_g[b])])
                        if first != 0:
                            pool.wait_ge(s_m.sem, s_m.at(s))
                            scatter_step(pool, c, idx[:, 1 - b, 1, :], sums[:, 1 - b], s_sc[1 - b], s - 1)

                    steps(pool, ESTEP, body)
                    pool.wait_ge(s_m.sem, s_m.at(ESTEP))
                    b = (ESTEP - 1) % 2
                    c = Chain(pool, s_pool, 2, ESTEP)
                    c.k = -1
                    scatter_step(pool, c, idx[:, b, 1, :], sums[:, b], s_sc[b], ESTEP - 1)
                    pool.wait_ge(s_sc[0].sem, s_sc[0].at(16 * K * ((ESTEP + 1) // 2)))
                    pool.wait_ge(s_sc[1].sem, s_sc[1].at(16 * K * (ESTEP // 2)))

                @block.vector
                def _(dve):
                    if mlp is not None:
                        mlp.prepare_shift(dve)
                    dve.memset(sums[:, :, :, :], 0.0)
                    dve.memset(x[:, :, :, :], 1.0).then_inc(s_set.sem, 1)
                    dve.wait_ge(s_set.sem, s_set.at(1))

                    def body(s, b, q, first):
                        c = Chain(dve, s_dve, links, s)
                        c.link(dve.tensor_copy(same[:, b, :], same_f[:, bass.ds(s * K, K)]))
                        dve.wait_ge(s_g[b].sem, s_g[b].at(16 * K * (q + 1)))
                        if first is None:
                            dve.wait_ge(s_sc[b].sem, s_sc[b].at(16 * K * q))
                        run_sums(dve, c, s, b, range(K), sums, same, x[:, b], s_m)
                        c.done()

                    steps(dve, ESTEP, body)
                    if mlp is not None:
                        mlp.coefficients(dve)

                if mlp is not None:
                    @block.sync
                    def _(sp):
                        mlp.load(sp)

                    @block.scalar
                    def _(act):
                        mlp.features(act)

                    @block.tensor
                    def _(pe):
                        mlp.products(pe)

                    mlp.count_up()

            for sg in (s_g, s_sc):
                sg[0].base += 16 * K * ((ESTEP + 1) // 2)
                sg[1].base += 16 * K * (ESTEP // 2)
            s_pool.base += 2 * ESTEP
            s_dve.base += links * ESTEP
            s_m.base += ESTEP
            s_set.base += 1
            close_segments(name + "_close", sums[:, (ESTEP - 1) % 2, K - 1, :])

    class EdgeMlp:

        def __init__(self, ctx, name, wmsg):
            def sb(nm, shape, dt=F32):
                return ctx.enter_context(nc.sbuf_tensor(f"{name}_{nm}", shape, dt))

            attr = sb("attr", [P, ET, 4])
            now = sb("now", [P, 2, K, 4])
            aT = sb("aT", [4, 2, 2, HALF * P])
            we = sb("we", [4, D])
            r = sb("r", [D, 2, HALF * P])
            r2 = sb("r2", [D, HALF * P])
            acc = sb("acc", [D, 2, 2 * ESTEP])
            cols = sb("cols", [D, 12])
            shift = sb("shift", [D, AGG])
            wraw = sb("wraw", [D, D])
            bm = sb("bm", [AGG, D])
            pT = ctx.enter_context(nc.psum_tensor(f"{name}_pT", [4, 2, 512], F32))
            pY = ctx.enter_context(nc.psum_tensor(f"{name}_pY", [D, 2, 512], F32))
            pC = ctx.enter_context(nc.psum_tensor(f"{name}_pC", [AGG, D], F32))
            s_ld, s_now, s_tr, s_hT = signal("mlp_load"), signal("h_ready"), signal("turned"), signal("hT_ready")
            s_mm, s_ev, s_dve, s_dev = signal("product_ready"), signal("product_used"), signal("mlp_chain"), signal("mlp_dev")
            s_pe, s_set, s_acc = signal("mlp_done"), signal("mlp_setup"), signal("squared")

            def load(sp):
                column = lambda v: v.rearrange("(d a) -> d a", a=1)
                sp.dma_start(attr[:, :, :], A["edge_attr_4"].rearrange("(p t) c -> p t c", t=ET)).then_inc(s_ld.sem, 16)
                sp.dma_start(we[:, :], A["L3_gnn_W_edge"]).then_inc(s_ld.sem, 16)
                for i, nm in enumerate(("b_edge", "g_edge", "beta_edge")):
                    sp.dma_start(cols[:, i:i + 1], column(A[f"L3_gnn_{nm}"]),
                                 allow_slow_non_contiguous=True).then_inc(s_ld.sem, 16)
                sp.dma_start(wraw[:, :], A["L3_gnn_W_msg"][2 * D:3 * D, :]).then_inc(s_ld.sem, 16)
                sp.dma_start(bm[D:AGG, :], row1(A["L3_gnn_b_msg"])).then_inc(s_ld.sem, 16)

            def prepare_shift(dve):
                dve.memset(shift[:, :], 0.0).then_inc(s_set.sem, 1)

            def coefficients(dve):
                dve.wait_ge(s_set.sem, s_set.at(1))
                dve.wait_ge(s_ld.sem, s_ld.at(16 * 7))
                c = Chain(dve, s_dve, 10)
                dve.wait_ge(s_acc.sem, s_acc.at(2 * ESTEP))
                c.link(dve.tensor_reduce(cols[:, 3:5], acc[:, :, :], AX.X, ALU.add))
                c.link(dve.tensor_scalar(cols[:, 3:5], cols[:, 3:5], 1.0 / E, None, ALU.mult))
                c.link(dve.tensor_tensor(cols[:, 5:6], cols[:, 3:4], cols[:, 3:4], ALU.mult))
                c.link(dve.tensor_tensor(cols[:, 6:7], cols[:, 4:5], cols[:, 5:6], ALU.subtract))
                dve.wait_ge(s_dev.sem, s_dev.at(1))
                c.link(dve.reciprocal(cols[:, 7:8], cols[:, 6:7]))
                c.link(dve.tensor_tensor(cols[:, 8:9], cols[:, 7:8], cols[:, 1:2], ALU.mult))
                c.link(dve.tensor_tensor(cols[:, 9:10], cols[:, 3:4], cols[:, 8:9], ALU.mult))
                c.link(dve.tensor_tensor(shift[:, D:AGG], cols[:, 2:3], cols[:, 9:10], ALU.subtract))
                c.link(dve.tensor_scalar(wmsg[0:D, :], wraw[:, :], cols[:, 8:9], None, ALU.mult))
                dve.wait_ge(s_pe.sem, s_pe.at(1))
                c.link(dve.tensor_tensor(wmsg[D:AGG, :], pC[D:AGG, :], bm[D:AGG, :], ALU.add))
                c.done()

            def features(act):
                act.wait_ge(s_ld.sem, s_ld.at(16 * 7))

                def step(t):
                    nc.scalar.copy(now[:, t.b], attr[:, bass.ds(t.s * K, K), :]).then_inc(s_now.sem, 1)
                    for h in range(2):
                        act.wait_ge(s_tr.sem, s_tr.at(2 * t.s + h + 1))
                        if t.after(2):
                            act.wait_ge(s_mm.sem, s_mm.at(2 * (t.s - 1)))
                        nc.scalar.copy(aT[:, t.b, h, :], pT[:, h, 0:HALF * P]).then_inc(s_hT.sem, 1)
                    for h in range(2):
                        act.wait_ge(s_mm.sem, s_mm.at(2 * t.s + h + 1))
                        if t.after(1) or h:
                            act.wait_ge(s_acc.sem, s_acc.at(2 * t.s + h))
                        nc.scalar.activation(r[:, h, :], pY[:, h, 0:HALF * P], ACT.Relu, bias=cols[:, 0:1],
                                             accum_out=acc[:, 0, bass.ds(2 * t.s + h, 1)]).then_inc(s_ev.sem, 1)
                        act.wait_ge(s_ev.sem, s_ev.at(2 * t.s + h + 1))
                        nc.scalar.activation(r2[:, :], r[:, h, :], ACT.Square,
                                             accum_out=acc[:, 1, bass.ds(2 * t.s + h, 1)]).then_inc(s_acc.sem, 1)

                pipeline(act, ESTEP, [(0, step)])
                act.wait_ge(s_dve.sem, s_dve.at(4))
                nc.scalar.activation(cols[:, 6:7], cols[:, 6:7], ACT.Sqrt,
                                     bias=eps_col[0:D, :]).then_inc(s_dev.sem, 1)

            def products(pe):
                pe.wait_ge(s_ld.sem, s_ld.at(16 * 7))

                def step(t):
                    pe.wait_ge(s_now.sem, s_now.at(t.s + 1))
                    for h in range(2):
                        if t.after(1):
                            pe.wait_ge(s_hT.sem, s_hT.at(2 * t.s))
                        for k in range(HALF):
                            last = pe.transpose(pT[:, h, k * P:(k + 1) * P], now[:, t.b, h * HALF + k, :],
                                                ident[0:P, 0:P])
                        last.then_inc(s_tr.sem, 1)
                    for h in range(2):
                        pe.wait_ge(s_hT.sem, s_hT.at(2 * t.s + h + 1))
                        if t.after(1):
                            pe.wait_ge(s_ev.sem, s_ev.at(2 * t.s))
                        pe.matmul(pY[:, h, 0:HALF * P], we[:, :], aT[:, t.b, h, :], start=True,
                                  stop=True).then_inc(s_mm.sem, 1)

                pipeline(pe, ESTEP, [(0, step)])
                pe.wait_ge(s_dve.sem, s_dve.at(8))
                pe.matmul(pC[:, :], shift[:, :], wraw[:, :], start=True, stop=True).then_inc(s_pe.sem, 1)

            def count_up():
                s_ld.base += 16 * 7
                s_now.base += ESTEP
                for sg in (s_tr, s_hT, s_mm, s_ev, s_acc):
                    sg.base += 2 * ESTEP
                s_dve.base += 10
                s_dev.base += 1
                s_pe.base += 1
                s_set.base += 1

            self.load, self.prepare_shift, self.coefficients = load, prepare_shift, coefficients
            self.features, self.products, self.count_up = features, products, count_up

    def message_edges(name, wmsg, gram):
        with ExitStack() as ctx:
            def sb(nm, shape, dt=F32):
                return ctx.enter_context(nc.sbuf_tensor(f"{name}_{nm}", shape, dt))

            attr = sb("attr", [P, ET, 4])
            now = sb("now", [P, 2, K, 4])
            aT = sb("aT", [4, 2, HALF * P])
            we = sb("we", [4, D])
            be = sb("be", [D, 1])
            w = sb("w", [D, 2, D])
            f = sb("f", [AGG, 2, HALF * P])
            x = sb("x", [P, 2, 2, K, D])
            xT = sb("xT", [D, 2, 2, HALF * P])
            msg = sb("msg", [P, 2, K, AGG])
            zeros = sb("zeros", [P, AGG])
            sums = sb("sums", [P, 2, K, AGG])
            stream, nf = sb("stream", [P, 2, 2 * K, D]), sb("nf", [P, 2, 2 * K, AGG])
            s_bi = [signal(f"base_load_{b}") for b in range(2)]
            s_bo = [signal(f"base_store_{b}") for b in range(2)]
            s_base, s_bc = signal("base_ready"), signal("base_chain")
            same = sb("same", [P, 2, K])
            idx = sb("idx", [P, 2, 3, K], I32)
            banks = ctx.enter_context(ExitStack())
            pA = banks.enter_context(nc.psum_tensor(f"{name}_pA", [D, 512], F32))
            pX = banks.enter_context(nc.psum_tensor(f"{name}_pX", [D, 2, 2, 512], F32))
            pM = banks.enter_context(nc.psum_tensor(f"{name}_pM", [P, 2, 512], F32))
            s_g = [[signal(f"gather_{c}{b}") for b in range(2)] for c in "ab"]
            s_sc = [signal(f"scatter_{b}") for b in range(2)]
            s_pool, s_dve, s_m, s_set = signal("pool_chain"), signal("dve_chain"), signal("sums_ready"), signal("setup")
            s_ld, s_now, s_ta, s_aT = signal("load_a0"), signal("h_ready"), signal("turned"), signal("hT_ready")
            s_ea, s_f, s_tx, s_xT = signal("edge_product"), signal("features"), signal("rows_turned"), signal("rows_ready")
            s_mm, s_relu, s_st = signal("product_ready"), signal("normed"), signal("summed")
            links = 1 + (K - 1)
            with nc.Block() as block:
                @block.sync
                def _(sp):
                    sp.dma_start(attr[:, :, :], A["edge_attr_4"].rearrange("(p t) c -> p t c", t=ET))\
                        .then_inc(s_ld.sem, 16)
                    sp.dma_start(we[:, :], A["L3_gnn_W_edge"]).then_inc(s_ld.sem, 16)
                    sp.dma_start(be[:, :], A["L3_gnn_b_edge"].rearrange("(d a) -> d a", a=1),
                                 allow_slow_non_contiguous=True).then_inc(s_ld.sem, 16)
                    for j in range(2):
                        sp.dma_start(w[:, j, :], A["L3_gnn_W_msg"][j * D:(j + 1) * D, :]).then_inc(s_ld.sem, 16)

                    def load(t):
                        if t.after(2):
                            sp.wait_ge(s_bo[t.b].sem, s_bo[t.b].at(16 * t.q))
                            sp.nop(nofuse=True)
                        sp.dma_start(stream[:, t.b], rows(d_xc, t.s, tiles=2 * K)).then_inc(s_bi[t.b].sem, 16)
                        sp.dma_start(nf[:, t.b], rows(d_nf, t.s, tiles=2 * K)).then_inc(s_bi[t.b].sem, 16)

                    def store(t):
                        sp.wait_ge(s_base.sem, s_base.at(t.s + 1))
                        sp.nop(nofuse=True)
                        sp.dma_start(rows(d_base, t.s, tiles=2 * K), stream[:, t.b]).then_inc(s_bo[t.b].sem, 16)

                    pipeline(sp, ESTEP, [(0, load), (1, store)])
                    sp.wait_ge(s_bo[0].sem, s_bo[0].at(16 * ((ESTEP + 1) // 2)))
                    sp.wait_ge(s_bo[1].sem, s_bo[1].at(16 * (ESTEP // 2)))

                @block.gpsimd
                def _(pool):
                    def gather(t):
                        if t.after(2):
                            pool.wait_ge(s_tx.sem, s_tx.at(2 * (t.s - 1)))
                        c = Chain(pool, s_pool, 3, t.s)
                        c.k = -1 if t.c else 0
                        gather_step(pool, c, t.s, [(src_idx, idx[:, t.b, 0, :], t_h3, x[:, t.b, 0], D, s_g[0][t.b]),
                                                   (dst_idx, idx[:, t.b, 1, :], t_h3, x[:, t.b, 1], D, s_g[1][t.b])])

                    def scatter(t):
                        pool.wait_ge(s_m.sem, s_m.at(t.s + 1))
                        c = Chain(pool, s_pool, 3, t.s)
                        c.k = 2 if t.c == ESTEP - 1 else 4
                        scatter_step(pool, c, idx[:, t.b, 2, :], sums[:, t.b], s_sc[t.b], t.s)

                    pipeline(pool, ESTEP, [(0, gather), (1, scatter)])
                    pool.wait_ge(s_sc[0].sem, s_sc[0].at(16 * K * ((ESTEP + 1) // 2)))
                    pool.wait_ge(s_sc[1].sem, s_sc[1].at(16 * K * (ESTEP // 2)))

                @block.vector
                def _(dve):
                    dve.memset(sums[:, :, :, :], 0.0)
                    dve.memset(f[:, :, :], 1.0)
                    dve.memset(zeros[:, :], 0.0)
                    dve.memset(msg[:, :, :, :], 1.0).then_inc(s_set.sem, 1)
                    dve.wait_ge(s_set.sem, s_set.at(1))

                    def rows_back(t):
                        for j in range(2):
                            dve.wait_ge(s_tx.sem, s_tx.at(2 * t.s + j + 1))
                            if t.after(1):
                                dve.wait_ge(s_mm.sem, s_mm.at(t.s))
                            dve.tensor_copy(xT[:, j], pX[:, j, :, 0:HALF * P]).then_inc(s_xT.sem, 1)

                    def run(t):
                        c = Chain(dve, s_dve, links, t.s)
                        c.link(dve.tensor_copy(same[:, t.b, :], same_f[:, bass.ds(t.s * K, K)]))
                        dve.wait_ge(s_relu.sem, s_relu.at(t.s + 1))
                        if t.after(2):
                            dve.wait_ge(s_sc[t.b].sem, s_sc[t.b].at(16 * K * t.q))
                        run_sums(dve, c, t.s, t.b, range(K), sums, same, msg[:, t.b], s_m)
                        c.done()

                    def base(t):
                        c = Chain(dve, s_bc, 1, t.s)
                        over = lambda v: v[:, :].unsqueeze(1).broadcast_to([P, 2 * K, D])
                        dve.wait_ge(s_bi[t.b].sem, s_bi[t.b].at(32 * (t.q + 1)))
                        dve.tensor_tensor(nf[:, t.b, :, 0:D], nf[:, t.b, :, 0:D], over(bn_s), ALU.mult)
                        c.link(dve.tensor_tensor(stream[:, t.b], stream[:, t.b], over(bn_t), ALU.add))
                        dve.tensor_tensor(stream[:, t.b], stream[:, t.b], nf[:, t.b, :, 0:D],
                                          ALU.add).then_inc(s_base.sem, 1)

                    pipeline(dve, ESTEP, [(0, rows_back), (0, run), (0, base)])

                @block.scalar
                def _(act):
                    act.wait_ge(s_ld.sem, s_ld.at(80))
                    act.wait_ge(s_set.sem, s_set.at(1))

                    def features(t):
                        nc.scalar.copy(now[:, t.b], attr[:, bass.ds(t.s * K, K), :]).then_inc(s_now.sem, 1)
                        for j in range(2):
                            act.wait_ge(s_ta.sem, s_ta.at(2 * t.s + j + 1))
                            nc.scalar.copy(aT[:, j, :], pA[0:4, 0:HALF * P]).then_inc(s_aT.sem, 1)
                            act.wait_ge(s_ea.sem, s_ea.at(2 * t.s + j + 1))
                            if t.after(1):
                                act.wait_ge(s_mm.sem, s_mm.at(t.s))
                            nc.scalar.activation(f[0:D, j, :], pA[:, 0:HALF * P], ACT.Relu,
                                                 bias=be[:, :]).then_inc(s_f.sem, 1)

                    def relu(t):
                        act.wait_ge(s_mm.sem, s_mm.at(t.s + 1))
                        if t.after(2):
                            act.wait_ge(s_st.sem, s_st.at(t.s - 1))
                            act.wait_ge(s_m.sem, s_m.at(t.s - 1))
                        nc.scalar.activation(msg[:, t.b, :, 0:D].rearrange("p (a k) c -> p a k c", a=2),
                                             pM[:, :, 0:HALF * D].rearrange("p a (k c) -> p a k c", k=HALF),
                                             ACT.Relu).then_inc(s_relu.sem, 1)

                    pipeline(act, ESTEP, [(0, features), (0, relu)])

                @block.tensor
                def _(pe):
                    pe.wait_ge(s_ld.sem, s_ld.at(80))
                    pe.wait_ge(s_set.sem, s_set.at(1))
                    gram_edge(pe, gram, zeros, True)

                    def features(t):
                        pe.wait_ge(s_now.sem, s_now.at(t.s + 1))
                        for j in range(2):
                            if t.after(1) or j:
                                pe.wait_ge(s_f.sem, s_f.at(2 * t.s + j))
                            for k in range(HALF):
                                last = pe.transpose(pA[0:4, k * P:(k + 1) * P], now[:, t.b, j * HALF + k, :],
                                                    ident[0:P, 0:P])
                            last.then_inc(s_ta.sem, 1)
                            pe.wait_ge(s_aT.sem, s_aT.at(2 * t.s + j + 1))
                            pe.matmul(pA[:, 0:HALF * P], we[:, :], aT[:, j, :], start=True,
                                      stop=True).then_inc(s_ea.sem, 1)

                    def turn(t):
                        for j in range(2):
                            pe.wait_ge(s_g[j][t.b].sem, s_g[j][t.b].at(16 * K * (t.q + 1)))
                            if t.after(1):
                                pe.wait_ge(s_xT.sem, s_xT.at(2 * (t.s - 1) + j + 1))
                            for k in range(K):
                                last = pe.transpose(pX[:, j, k // HALF, (k % HALF) * P:(k % HALF + 1) * P],
                                                    x[:, t.b, j, k, :], ident[0:P, 0:P])
                            last.then_inc(s_tx.sem, 1)

                    def product(t):
                        pe.wait_ge(s_f.sem, s_f.at(2 * t.s + 2))
                        pe.wait_ge(s_xT.sem, s_xT.at(2 * t.s + 2))
                        if t.after(1):
                            pe.wait_ge(s_relu.sem, s_relu.at(t.s))
                        for k in range(K):
                            a, at = k // HALF, slice((k % HALF) * P, (k % HALF + 1) * P)
                            o = pM[:, a, (k % HALF) * D:(k % HALF + 1) * D]
                            pe.matmul(o, f[:, a, at], wmsg[:, :], start=True, stop=False)
                            pe.matmul(o, xT[:, 0, a, at], w[:, 0, :], start=False, stop=False)
                            last = pe.matmul(o, xT[:, 1, a, at], w[:, 1, :], start=False, stop=True)
                        last.then_inc(s_mm.sem, 1)

                    def total(t):
                        pe.wait_ge(s_relu.sem, s_relu.at(t.s + 1))
                        gram_step(pe, gram, msg[:, t.b]).then_inc(s_st.sem, 1)

                    pipeline(pe, ESTEP, [(0, features), (0, turn), (1, total), (0, product)])
                    gram_edge(pe, gram, zeros, False)

            for sg in s_g + [s_sc]:
                sg[0].base += 16 * K * ((ESTEP + 1) // 2)
                sg[1].base += 16 * K * (ESTEP // 2)
            for b in range(2):
                s_bi[b].base += 32 * len(range(b, ESTEP, 2))
                s_bo[b].base += 16 * len(range(b, ESTEP, 2))
            s_base.base += ESTEP
            s_bc.base += ESTEP
            s_pool.base += 3 * ESTEP
            s_dve.base += links * ESTEP
            s_ld.base += 80
            s_set.base += 1
            for x_ in (s_m, s_now, s_mm, s_relu, s_st):
                x_.base += ESTEP
            for x_ in (s_ta, s_aT, s_ea, s_f, s_tx, s_xT):
                x_.base += 2 * ESTEP
            banks.close()
            close_segments(name + "_close", sums[:, (ESTEP - 1) % 2, K - 1, :])

    def last_sum(name):
        with ExitStack() as ctx:
            def sb(nm, shape, dt=F32):
                return ctx.enter_context(nc.sbuf_tensor(f"{name}_{nm}", shape, dt))

            x, c = sb("x", [P, 4, K, D]), sb("c", [P, 4, K, AGG])
            y, part = sb("y", [P, 4, K, D]), sb("part", [P, 4, K, D])
            s_in = [[signal(f"load_{j}{b}") for b in range(4)] for j in "ab"]
            s_out = [signal(f"store_a{b}") for b in range(4)]
            s_dve, s_ev, s_pool = signal("dve_chain"), signal("product_used"), signal("pool_ready")
            wide = lambda v: v[:, :].unsqueeze(1).broadcast_to([P, K, D])
            with nc.Block() as block:
                @block.sync
                def _(sp):
                    def load(t):
                        r = t.c % 4
                        if t.after(4):
                            sp.wait_ge(s_ev.sem, s_ev.at(t.s - 3))
                            sp.nop(nofuse=True)
                        sp.dma_start(x[:, r], rows(d_base, t.s)).then_inc(s_in[0][r].sem, 16)
                        sp.dma_start(c[:, r], rows(t_agg, t.s)).then_inc(s_in[1][r].sem, 16)

                    def store(t):
                        sp.wait_ge(s_ev.sem, s_ev.at(t.s + 1))
                        sp.nop(nofuse=True)
                        sp.dma_start(rows(out, t.s), y[:, t.c % 4]).then_inc(s_out[t.c % 4].sem, 16)

                    pipeline(sp, NSTEP, [(0, load), (3, store)], 4)
                    for r in range(4):
                        sp.wait_ge(s_out[r].sem, s_out[r].at(16 * len(range(r, NSTEP, 4))))

                @block.gpsimd
                def _(pool):
                    def shifts(t):
                        if t.after(4):
                            pool.wait_ge(s_ev.sem, s_ev.at(t.s - 3))
                        cn = count[:, bass.ds(t.s * K, K)].unsqueeze(2).broadcast_to([P, K, D])
                        pool.tensor_tensor(part[:, t.c % 4], cn, wide(bm_t), ALU.mult).then_inc(s_pool.sem, 1)

                    pipeline(pool, NSTEP, [(0, shifts)], 4)

                @block.vector
                def _(dve):
                    def add_up(t):
                        r = t.c % 4
                        chain = Chain(dve, s_dve, 1, t.s)
                        for sg in s_in:
                            dve.wait_ge(sg[r].sem, sg[r].at(16 * (t.turn(4) + 1)))
                        dve.tensor_tensor(c[:, r, :, 0:D], c[:, r, :, 0:D], wide(bm_s), ALU.mult)
                        dve.wait_ge(s_pool.sem, s_pool.at(t.s + 1))
                        chain.link(dve.tensor_tensor(x[:, r], x[:, r], part[:, r], ALU.add))
                        if t.after(4):
                            dve.wait_ge(s_out[r].sem, s_out[r].at(16 * t.turn(4)))
                        dve.tensor_tensor(y[:, r], x[:, r], c[:, r, :, 0:D], ALU.add).then_inc(s_ev.sem, 1)

                    pipeline(dve, NSTEP, [(0, add_up)], 4)

    prepare()
    node_phase("first", "first", [(A["x"], D)], [(t_h0, ROW), (d_y, D)], ROW,
               [],
               gat=(A["L0_gnn_W"][0], A["L0_gnn_att_src"][0], A["L0_gnn_att_dst"][0], H, 0, 2 * H))
    gat_edges("edges0", t_h0, A["L0_gnn_W"][0])

    def gram_bank(ctx, name):
        return ctx.enter_context(nc.psum_tensor(name, [D, AGG], F32))[:, :]

    for layer in range(2):
        with ExitStack() as ctx:
            held = ctx.enter_context(nc.sbuf_tensor(f"held{layer}", [P, NT, D], F32))
            with ExitStack() as c2:
                gram = gram_bank(c2, f"gram{layer}")
                aggregate_phase(f"agg{layer}", held, layer == 0, gram)
                bn_coefficients(f"bn{layer}", gram, N, A["L0_gnn_gamma"][layer], A["L0_gnn_beta"][layer], bn_s, bn_t,
                                A["L0_gnn_bias"][layer])
            if layer == 0:
                node_phase("second", "gat", [(t_h0, D)], [(t_x1, ROW), (d_y, D)], ROW,
                           [], held=held,
                           gat=(A["L0_gnn_W"][1], A["L0_gnn_att_src"][1], A["L0_gnn_att_dst"][1], H, 0, 2 * H))
            else:
                node_phase("third", "join", [(t_x1, D), (A["x"], D)], [(d_xa, D), (t_g, ROW), (d_r, D)], ROW,
                           [(0, A["L1_gnn_W"], None)], held=held, bias=A["L1_gnn_bias"],
                           gat=(A["L1_gnn_W"], A["L1_gnn_att_src"], A["L1_gnn_att_dst"], H, D, None))
        if layer == 0:
            gat_edges("edges1", t_x1, A["L0_gnn_W"][1])
    gat_edges("edges2", t_g, None)
    node_phase("fourth", "layer", [(d_r, D), (t_agg, AGG), (d_xa, D)], [(d_xb, D), (t_c1, D)], D,
               [(0, A["L2_gnn_W1"], None)], gamma=A["L1_gnn_gamma"], beta=A["L1_gnn_beta"])
    gcn_edges("edges3", t_c1)
    node_phase("fifth", "gcn", [(t_c1, D), (t_agg, AGG)], [(t_c2, D)], D, [(0, A["L2_gnn_W2"], None)],
               bias=A["L2_gnn_b1"])
    wmsg = sbw("wmsg", [AGG, D])
    with ExitStack() as ctx:
        gcn_edges("edges4", t_c2, EdgeMlp(ctx, "edge_mlp", wmsg))
    with ExitStack() as ctx:
        gram = gram_bank(ctx, "gram_nf")
        node_phase("sixth", "last", [(t_c2, D), (t_agg, AGG), (d_xb, D)], [(d_xc, D), (t_h3, D), (d_nf, AGG)], D,
                   [(0, A["L3_gnn_W_node"], A["L3_gnn_b_node"])], bias=A["L2_gnn_b2"], gram=gram)
        bn_coefficients("bn_nf", gram, N, A["L3_gnn_g_node"], A["L3_gnn_beta_node"], bn_s, bn_t)
    bm_s = sbw("bm_s", [P, D])
    bm_t = sbw("bm_t", [P, D])
    with ExitStack() as ctx:
        gram = gram_bank(ctx, "gram_msg")
        message_edges("edges5", wmsg, gram)
        bn_coefficients("bn_msg", gram, E, A["L3_gnn_g_msg"], A["L3_gnn_beta_msg"], bm_s, bm_t)
    last_sum("out")
    whole.close()


_INS = ['x', 'src', 'dst', 'edge_attr_4', 'L0_gnn_W', 'L0_gnn_att_src', 'L0_gnn_att_dst', 'L0_gnn_bias',
        'L0_gnn_gamma', 'L0_gnn_beta', 'L1_gnn_W', 'L1_gnn_att_src', 'L1_gnn_att_dst', 'L1_gnn_bias',
        'L1_gnn_gamma', 'L1_gnn_beta', 'L2_gnn_W1', 'L2_gnn_b1', 'L2_gnn_W2', 'L2_gnn_b2', 'L3_gnn_W_node',
        'L3_gnn_b_node', 'L3_gnn_g_node', 'L3_gnn_beta_node', 'L3_gnn_W_edge', 'L3_gnn_b_edge', 'L3_gnn_g_edge',
        'L3_gnn_beta_edge', 'L3_gnn_W_msg', 'L3_gnn_b_msg', 'L3_gnn_g_msg', 'L3_gnn_beta_msg']


def kernel(**inputs):
    import numpy as _np
    import concourse.bacc as _bacc
    from concourse import mybir as _mybir
    from concourse.bass_utils import run_bass_kernel_spmd as _run

    nc = _bacc.Bacc("TRN2", target_bir_lowering=False, num_devices=1)
    arrays, args = {}, {}
    for name in _INS:
        a = _np.ascontiguousarray(inputs[name])
        arrays[f"in_{name}_dram"] = a
        args[name] = nc.dram_tensor(f"in_{name}_dram", a.shape, _mybir.dt.from_np(a.dtype), kind="ExternalInput").ap()
    out = nc.dram_tensor("out_0_dram", (N, D), F32, kind="ExternalOutput").ap()
    build(nc, args, out)
    r = _run(nc, [arrays], core_ids=[0])
    return r.results[0]["out_0_dram"]
```
